# Optimizing a Trainium2 kernel written in Bass

```python
import numpy as np
import jax
import jax.numpy as jnp

def _softmax(x, axis=-1):
    return jax.nn.softmax(x, axis=axis)

def _gelu(x):
    return jax.nn.gelu(x, approximate=True)

def _silu(x):
    return jax.nn.silu(x)

def _sigmoid(x):
    return jax.nn.sigmoid(x)

def _layernorm(x, axis=-1, eps=1e-05):
    m = jnp.mean(x, axis=axis, keepdims=True)
    v = jnp.var(x, axis=axis, keepdims=True)
    return (x - m) / jnp.sqrt(v + eps)

def _scatter_add(tgt, idx, src, axis=0):
    return tgt.at[idx].add(src)

def _segment_sum(src, seg, n):
    return jax.ops.segment_sum(src, seg, n)
kernel_name = 'mk_flamingo_gated_d2_seqx_r8_45345b'

def setup_inputs(seed: int=0):
    np.random.seed(seed)
    _w = jnp.asarray

    def _rec_inputs():
        import jax
        import jax.numpy as jnp
        _rk = jax.random.key(seed)
        x = -0.000125 + 0.9999 * jax.random.normal(jax.random.fold_in(_rk, 1), (8, 256, 128), jnp.float32)
        _lenS = 256 - jax.random.randint(jax.random.fold_in(_rk, 7), (8,), 0, max(1, 256 // 4) + 1, jnp.int32)
        _lenS2 = 1601 - jax.random.randint(jax.random.fold_in(_rk, 8), (8,), 0, max(1, 1601 // 4) + 1, jnp.int32)
        _ctx_1024P = jax.random.normal(jax.random.fold_in(_rk, 11), (8, 16, 128), jnp.float32)
        _ctx_1024c = jax.random.dirichlet(jax.random.fold_in(_rk, 511), 0.3 * jnp.ones((16,), jnp.float32), (8, 1601))
        _ctx_1024t = jnp.einsum('bsk,bkd->bsd', _ctx_1024c, _ctx_1024P)
        _ctx_1024t = _ctx_1024t * jax.lax.rsqrt(jnp.mean(jnp.square(_ctx_1024t)) + 1e-12) * 0.953939
        ctx_1024 = -1.52775e-05 + 0.999936 * (_ctx_1024t + 0.3 * jax.random.normal(jax.random.fold_in(_rk, 611), (8, 1601, 128), jnp.float32))
        _validS = jnp.arange(256)[None, :] < _lenS[:, None]
        _validS2 = jnp.arange(1601)[None, :] < _lenS2[:, None]
        _causal = jnp.tril(jnp.ones((256, 256), dtype=bool))
        mask_Bx1xSxS2_bk1 = jnp.broadcast_to(_validS2[:, None, None, :], (8, 1, 256, 1601))
        _g = jax.random.normal(jax.random.fold_in(_rk, 9001), (2, 2), jnp.float32)
        _g = jnp.sign(_g) * jnp.maximum(jnp.abs(_g), 1.0) + (_g == 0) * 1.0
        g_xattn = _g[0]
        g_ffn = _g[1]
        return (x, ctx_1024, mask_Bx1xSxS2_bk1, g_xattn, g_ffn)
    x, ctx_1024, mask_Bx1xSxS2_bk1, g_xattn, g_ffn = _rec_inputs()

    def _L0_xattn_setup():
        import jax, jax.numpy as jnp
        import numpy as np
        B, SX, SY, D = (64, 64, 64, 128)
        key = jax.random.key(seed)
        k1, k2, k3, k4 = jax.random.split(key, 4)
        x = jax.random.normal(k1, (B, SX, D), dtype=jnp.float32)
        y = jax.random.normal(k2, (B, SY, D), dtype=jnp.float32)
        W = jax.random.uniform(k3, (D, D), dtype=jnp.float32, minval=-0.05, maxval=0.05)
        b = jax.random.uniform(k4, (D,), dtype=jnp.float32, minval=-0.05, maxval=0.05)
        return {'x': x, 'y': y, 'W': W, 'b': b}
    _L0_xattn_all = _L0_xattn_setup()
    _L0_xattn_in = {k: v for k, v in _L0_xattn_all.items() if k in ('W', 'b')}
    del _L0_xattn_all

    def _L0_ffn_setup():
        import jax, jax.numpy as jnp
        import numpy as np
        IN_F = 128
        OUT_F = 128
        B, S = (8, 512)

        def _pack_ternary(tern):
            enc = (tern + 1.0).astype(jnp.int32).reshape(-1)
            return (enc[0::4] | enc[1::4] << 2 | enc[2::4] << 4 | enc[3::4] << 6).astype(jnp.int32)
        key = jax.random.key(seed)
        kx, kw = jax.random.split(key)
        x = jax.random.normal(kx, (B, S, IN_F), dtype=jnp.float32)
        w = jax.random.normal(kw, (OUT_F, IN_F), dtype=jnp.float32) * 0.02
        scale = jnp.maximum(jnp.mean(jnp.abs(w)), 1e-05)
        wn = w / scale
        tern = jnp.sign(wn) * (jnp.abs(wn) > 0.5).astype(jnp.float32)
        packed = _pack_ternary(tern)
        bias = jnp.zeros((OUT_F,), dtype=jnp.float32)
        return {'x': x, 'packed_weight': packed, 'weight_scale': scale.reshape(1), 'bias': bias}
    _L0_ffn_all = _L0_ffn_setup()
    _L0_ffn_in = {k: v for k, v in _L0_ffn_all.items() if k in ('packed_weight', 'weight_scale', 'bias')}
    del _L0_ffn_all

    def _L1_xattn_setup():
        import jax, jax.numpy as jnp
        import numpy as np
        D_MODEL = 128
        NUM_HEADS = 16
        D_K = D_MODEL // NUM_HEADS
        B, S = (2, 256)
        NEG = -1000000000.0

        def _split_heads(x):
            b, s, _ = x.shape
            return x.reshape(b, s, NUM_HEADS, D_K).transpose(0, 2, 1, 3)
        key = jax.random.key(seed)
        ks = jax.random.split(key, 12)
        scale = 1.0 / np.sqrt(D_MODEL)
        inp = {'q': jax.random.normal(ks[0], (B, S, D_MODEL), jnp.float32), 'k': jax.random.normal(ks[1], (B, S, D_MODEL), jnp.float32), 'v': jax.random.normal(ks[2], (B, S, D_MODEL), jnp.float32), 'mask': jax.random.randint(ks[3], (B, 1, S, S), 0, 2) == 1, 'w_q': jax.random.normal(ks[4], (D_MODEL, D_MODEL), jnp.float32) * scale, 'b_q': jnp.zeros((D_MODEL,), jnp.float32), 'w_k': jax.random.normal(ks[5], (D_MODEL, D_MODEL), jnp.float32) * scale, 'b_k': jnp.zeros((D_MODEL,), jnp.float32), 'w_v': jax.random.normal(ks[6], (D_MODEL, D_MODEL), jnp.float32) * scale, 'b_v': jnp.zeros((D_MODEL,), jnp.float32), 'w_o': jax.random.normal(ks[7], (D_MODEL, D_MODEL), jnp.float32) * scale, 'b_o': jnp.zeros((D_MODEL,), jnp.float32)}
        return inp
    _L1_xattn_all = _L1_xattn_setup()
    _L1_xattn_in = {k: v for k, v in _L1_xattn_all.items() if k in ('w_q', 'b_q', 'w_k', 'b_k', 'w_v', 'b_v', 'w_o', 'b_o')}
    del _L1_xattn_all

    def _L1_ffn_setup():
        import jax, jax.numpy as jnp
        import numpy as np
        B, L, M = (4, 256, 128)
        G, E = (8, 8)
        CAP_FACTOR = 2.0

        def _ffn_size(m, widening=8.0):
            f = int(widening * m) * 2 // 3
            return f + (8 - f) % 8
        H = _ffn_size(M)

        def _gating_top2(logits, C):
            Gd, Sd, Ed = logits.shape
            raw = jax.nn.softmax(logits, axis=-1)
            idx1 = jnp.argmax(raw, axis=-1)
            m1 = jax.nn.one_hot(idx1, Ed, dtype=logits.dtype)
            gate1 = jnp.sum(raw * m1, axis=-1)
            rest = raw * (1.0 - m1)
            idx2 = jnp.argmax(rest, axis=-1)
            m2 = jax.nn.one_hot(idx2, Ed, dtype=logits.dtype)
            gate2 = jnp.sum(rest * m2, axis=-1)
            p1 = jnp.cumsum(m1, axis=-2) - m1
            m1 = m1 * (p1 < C).astype(m1.dtype)
            p1 = jnp.sum(p1 * m1, axis=-1)
            m1_flat = jnp.sum(m1, axis=-1)
            m1_count = jnp.sum(m1, axis=-2)
            p2 = jnp.cumsum(m2, axis=-2) - m2 + m1_count[:, None, :]
            m2 = m2 * (p2 < C).astype(m2.dtype)
            p2 = jnp.sum(p2 * m2, axis=-1)
            m2_flat = jnp.sum(m2, axis=-1)
            gate1 = gate1 * m1_flat
            gate2 = gate2 * m2_flat
            c1 = (gate1[..., None] * jax.nn.one_hot(idx1, Ed, dtype=jnp.float32))[..., None] * jax.nn.one_hot(p1.astype(jnp.int32), C, dtype=jnp.float32)[:, :, None, :]
            c2 = (gate2[..., None] * jax.nn.one_hot(idx2, Ed, dtype=jnp.float32))[..., None] * jax.nn.one_hot(p2.astype(jnp.int32), C, dtype=jnp.float32)[:, :, None, :]
            combine = (c1 + c2).astype(logits.dtype)
            dispatch = (combine != 0).astype(logits.dtype)
            return (dispatch, combine)
        key = jax.random.key(seed)
        k0, k1, k2, k3, k4 = jax.random.split(key, 5)
        return {'inputs': jax.random.normal(k0, (B, L, M), jnp.float32), 'router_w': jax.random.normal(k1, (M, E), jnp.float32) * 0.02, 'w0_kernel': jax.random.normal(k2, (E, M, H), jnp.float32) * 0.02, 'w1_kernel': jax.random.normal(k3, (E, M, H), jnp.float32) * 0.02, 'wo_kernel': jax.random.normal(k4, (E, H, M), jnp.float32) * 0.02}
    _L1_ffn_all = _L1_ffn_setup()
    _L1_ffn_in = {k: v for k, v in _L1_ffn_all.items() if k in ('router_w', 'w0_kernel', 'w1_kernel', 'wo_kernel')}
    del _L1_ffn_all
    return {'x': x, 'ctx_1024': ctx_1024, 'mask_Bx1xSxS2_bk1': mask_Bx1xSxS2_bk1, 'g_xattn': g_xattn, 'g_ffn': g_ffn, 'L0_xattn_W': _L0_xattn_in['W'], 'L0_xattn_b': _L0_xattn_in['b'], 'L0_ffn_packed_weight': _L0_ffn_in['packed_weight'], 'L0_ffn_weight_scale': _L0_ffn_in['weight_scale'], 'L0_ffn_bias': _L0_ffn_in['bias'], 'L1_xattn_w_q': _L1_xattn_in['w_q'], 'L1_xattn_b_q': _L1_xattn_in['b_q'], 'L1_xattn_w_k': _L1_xattn_in['w_k'], 'L1_xattn_b_k': _L1_xattn_in['b_k'], 'L1_xattn_w_v': _L1_xattn_in['w_v'], 'L1_xattn_b_v': _L1_xattn_in['b_v'], 'L1_xattn_w_o': _L1_xattn_in['w_o'], 'L1_xattn_b_o': _L1_xattn_in['b_o'], 'L1_ffn_router_w': _L1_ffn_in['router_w'], 'L1_ffn_w0_kernel': _L1_ffn_in['w0_kernel'], 'L1_ffn_w1_kernel': _L1_ffn_in['w1_kernel'], 'L1_ffn_wo_kernel': _L1_ffn_in['wo_kernel']}

def reference(x, ctx_1024, mask_Bx1xSxS2_bk1, g_xattn, g_ffn, L0_xattn_W, L0_xattn_b, L0_ffn_packed_weight, L0_ffn_weight_scale, L0_ffn_bias, L1_xattn_w_q, L1_xattn_b_q, L1_xattn_w_k, L1_xattn_b_k, L1_xattn_w_v, L1_xattn_b_v, L1_xattn_w_o, L1_xattn_b_o, L1_ffn_router_w, L1_ffn_w0_kernel, L1_ffn_w1_kernel, L1_ffn_wo_kernel):
    import jax
    import jax.numpy as jnp

    def _L0_xattn_ref(x, y, W, b):
        import jax, jax.numpy as jnp
        import numpy as np
        B, SX, SY, D = (64, 64, 64, 128)
        proj = jnp.einsum('bsd,de->bse', x, W) + b
        att = jnp.einsum('bsd,btd->bst', proj, y)
        nor = jax.nn.softmax(att, axis=-1)
        return jnp.einsum('bst,btd->bsd', nor, y)

    def _L0_ffn_ref(x, packed_weight, weight_scale, bias):
        import jax, jax.numpy as jnp
        import numpy as np
        IN_F = 128
        OUT_F = 128
        B, S = (8, 512)

        def _pack_ternary(tern):
            enc = (tern + 1.0).astype(jnp.int32).reshape(-1)
            return (enc[0::4] | enc[1::4] << 2 | enc[2::4] << 4 | enc[3::4] << 6).astype(jnp.int32)
        n = OUT_F * IN_F
        shifts = jnp.array([0, 2, 4, 6], dtype=jnp.int32)
        enc = (packed_weight[None, :] >> shifts[:, None] & 3).reshape(-1)[:n]
        w = (enc.astype(jnp.float32) - 1.0).reshape(OUT_F, IN_F) * weight_scale
        act_scale = 127.0 / jnp.maximum(jnp.max(jnp.abs(x), axis=-1, keepdims=True), 1e-05)
        x_dq = jnp.clip(jnp.round(x * act_scale), -128.0, 127.0) / act_scale
        return jnp.einsum('bsi,oi->bso', x_dq, w) + bias

    def _L1_xattn_ref(q, k, v, mask, w_q, b_q, w_k, b_k, w_v, b_v, w_o, b_o):
        import jax, jax.numpy as jnp
        import numpy as np
        D_MODEL = 128
        NUM_HEADS = 16
        D_K = D_MODEL // NUM_HEADS
        B, S = (2, 256)
        NEG = -1000000000.0

        def _split_heads(x):
            b, s, _ = x.shape
            return x.reshape(b, s, NUM_HEADS, D_K).transpose(0, 2, 1, 3)
        qh = _split_heads(q @ w_q + b_q)
        kh = _split_heads(k @ w_k + b_k)
        vh = _split_heads(v @ w_v + b_v)
        scores = jnp.einsum('bhqd,bhkd->bhqk', qh, kh) / jnp.sqrt(jnp.asarray(D_K, jnp.float32))
        scores = jnp.where(mask, NEG, scores)
        attn = jax.nn.softmax(scores, axis=-1)
        out = jnp.einsum('bhqk,bhkd->bhqd', attn, vh)
        out = out.transpose(0, 2, 1, 3).reshape(q.shape[0], -1, D_MODEL)
        return out @ w_o + b_o

    def _L1_ffn_ref(inputs, router_w, w0_kernel, w1_kernel, wo_kernel):
        import jax, jax.numpy as jnp
        import numpy as np
        B, L, M = (4, 256, 128)
        G, E = (8, 8)
        CAP_FACTOR = 2.0

        def _ffn_size(m, widening=8.0):
            f = int(widening * m) * 2 // 3
            return f + (8 - f) % 8
        H = _ffn_size(M)

        def _gating_top2(logits, C):
            Gd, Sd, Ed = logits.shape
            raw = jax.nn.softmax(logits, axis=-1)
            idx1 = jnp.argmax(raw, axis=-1)
            m1 = jax.nn.one_hot(idx1, Ed, dtype=logits.dtype)
            gate1 = jnp.sum(raw * m1, axis=-1)
            rest = raw * (1.0 - m1)
            idx2 = jnp.argmax(rest, axis=-1)
            m2 = jax.nn.one_hot(idx2, Ed, dtype=logits.dtype)
            gate2 = jnp.sum(rest * m2, axis=-1)
            p1 = jnp.cumsum(m1, axis=-2) - m1
            m1 = m1 * (p1 < C).astype(m1.dtype)
            p1 = jnp.sum(p1 * m1, axis=-1)
            m1_flat = jnp.sum(m1, axis=-1)
            m1_count = jnp.sum(m1, axis=-2)
            p2 = jnp.cumsum(m2, axis=-2) - m2 + m1_count[:, None, :]
            m2 = m2 * (p2 < C).astype(m2.dtype)
            p2 = jnp.sum(p2 * m2, axis=-1)
            m2_flat = jnp.sum(m2, axis=-1)
            gate1 = gate1 * m1_flat
            gate2 = gate2 * m2_flat
            c1 = (gate1[..., None] * jax.nn.one_hot(idx1, Ed, dtype=jnp.float32))[..., None] * jax.nn.one_hot(p1.astype(jnp.int32), C, dtype=jnp.float32)[:, :, None, :]
            c2 = (gate2[..., None] * jax.nn.one_hot(idx2, Ed, dtype=jnp.float32))[..., None] * jax.nn.one_hot(p2.astype(jnp.int32), C, dtype=jnp.float32)[:, :, None, :]
            combine = (c1 + c2).astype(logits.dtype)
            dispatch = (combine != 0).astype(logits.dtype)
            return (dispatch, combine)
        Bb, Ll, Mm = inputs.shape
        S = Bb * Ll // G
        x = inputs.reshape(G, S, Mm)
        logits = jnp.einsum('GSM,ME->GSE', x, router_w)
        cap = int(CAP_FACTOR * S / E)
        C = (cap + 3) // 4 * 4
        dispatch, combine = _gating_top2(logits, C)
        expert_inputs = jnp.einsum('GSEC,GSM->EGCM', dispatch, x)
        layer_w0 = jnp.einsum('EGCM,EMH->EGCH', expert_inputs, w0_kernel)
        layer_w1 = jnp.einsum('EGCM,EMH->EGCH', expert_inputs, w1_kernel)
        hidden = jax.nn.gelu(layer_w0, approximate=True) * layer_w1
        expert_outputs = jnp.einsum('EGCH,EHM->EGCM', hidden, wo_kernel)
        out = jnp.einsum('EGCM,GSEC->GSM', expert_outputs, combine)
        return out.reshape(Bb, Ll, Mm)
    x = x + jnp.tanh(g_xattn[0]) * _L0_xattn_ref(_layernorm(x, axis=-1), ctx_1024, L0_xattn_W, L0_xattn_b)
    x = x + jnp.tanh(g_ffn[0]) * _L0_ffn_ref(_layernorm(x, axis=-1), L0_ffn_packed_weight, L0_ffn_weight_scale, L0_ffn_bias)
    x = x + jnp.tanh(g_xattn[1]) * _L1_xattn_ref(_layernorm(x, axis=-1), ctx_1024, ctx_1024, mask_Bx1xSxS2_bk1, L1_xattn_w_q, L1_xattn_b_q, L1_xattn_w_k, L1_xattn_b_k, L1_xattn_w_v, L1_xattn_b_v, L1_xattn_w_o, L1_xattn_b_o)
    x = x + jnp.tanh(g_ffn[1]) * _L1_ffn_ref(_layernorm(x, axis=-1), L1_ffn_router_w, L1_ffn_w0_kernel, L1_ffn_w1_kernel, L1_ffn_wo_kernel)
    return x

_drawn_inputs = setup_inputs


def setup_inputs(seed=0):
    import zlib

    import numpy as np

    out = dict(_drawn_inputs(seed))
    spreads = {'g_ffn': (-1.0, 0.6),
     'L0_ffn_bias': (0.0, 0.1),
     'L1_xattn_b_q': (0.0, 0.556),
     'L1_xattn_b_k': (0.0, 0.8),
     'L1_xattn_b_v': (0.0, 0.1),
     'L1_xattn_b_o': (0.0, 0.1)}
    factors = {'L1_ffn_router_w': 8.0,
     'L1_ffn_w0_kernel': 8.0,
     'L1_ffn_w1_kernel': 8.0,
     'L1_ffn_wo_kernel': 8.0}
    for name, (base, spread) in spreads.items():
        noise = np.random.default_rng([zlib.crc32(name.encode()), seed]).standard_normal(out[name].shape)
        drawn = base * np.exp(spread * noise) if base else spread * noise
        out[name] = jnp.asarray(drawn.astype(out[name].dtype))
    for name, factor in factors.items():
        out[name] = (out[name] * factor).astype(out[name].dtype)
    return out
```

```python
from contextlib import ExitStack

import concourse.bass as bass
from concourse import mybir


class Tally:

    def __init__(self, eng, sem):
        self.eng, self.sem, self.n, self.base = eng, sem, 0, 0

    def mark(self, ins):
        ins.then_inc(self.sem, 1)
        self.n += 1
        return self.base + self.n

    def link(self, ins):
        self.eng.wait_ge(self.sem, self.mark(ins))

    def loop(self, start, end, per):
        with self.eng.Fori(start, end) as i:
            n0 = self.n
            self.base = (i - start) * per if start else i * per
            yield i
            assert self.n - n0 == per, (self.n - n0, per)
            self.base = 0
            self.n = n0
        self.n = n0 + per * (end - start)


def build(nc, x, ctx_in, mask, g_xattn, g_ffn, w0, b0, packed, wscale, fbias,
          wq, bq, wk, bk, wv, bv, wo, bo, router, we0, we1, weo, out):
    fp32, bf16 = mybir.dt.float32, mybir.dt.bfloat16
    i32, u8 = mybir.dt.int32, mybir.dt.uint8
    ALU, ACT, AX = mybir.AluOpType, mybir.ActivationFunctionType, mybir.AxisListType
    ds = bass.ds

    B, S, D = x.shape
    K = ctx_in.shape[1]
    QT = S // 128
    NT = B * QT
    KT = -(-K // 128)
    KR = K - 128 * (KT - 1)
    H = 16
    DH = D // H
    TAIL = (K - 1) // 4
    T0 = K - TAIL
    TP = TAIL // 4
    E = router.shape[1]
    CAP = 64
    HID = we0.shape[2]
    HC = -(-HID // 128)
    HR = (HID - 128 * (HC - 2)) // 2
    HROWS = [128] * (HC - 2) + [HR] * 2
    HLO = [sum(HROWS[:c]) for c in range(HC)]
    EPS = 1e-5
    MAGIC = 1.5 * 2.0 ** 23
    NEG = -2.0 ** 100
    NPROD = 6
    KPART = (0, 0, 1, 1, 0, 2)
    QPART = (0, 1, 0, 1, 2, 0)
    RS = NPROD * DH
    RM = RS + 1
    RA = RM + 3

    stack = ExitStack()
    with stack:
        def sb(name, shape, dt=fp32):
            return stack.enter_context(nc.sbuf_tensor(name, shape, dt))

        def sem(name):
            return stack.enter_context(nc.semaphore(name))

        ident = sb("ident", [128, 128])
        identb = sb("identb", [128, 128], bf16)
        w0_sb, wq_sb, wk_sb, wv_sb, wo_sb = (sb(n, [128, 128]) for n in ("w0_sb", "wq_sb", "wk_sb", "wv_sb", "wo_sb"))
        router_sb = sb("router_sb", [128, E])
        b0_col, bq_col, bk_col = (sb(n, [128, 1]) for n in ("b0_col", "bq_col", "bk_col"))
        fb_row, bv_row, bo_row = (sb(n, [128, 128]) for n in ("fb_row", "bv_row", "bo_row"))
        gates = sb("gates", [128, 4])
        gates_in = sb("gates_in", [128, 4])
        ws_col = sb("ws_col", [128, 1])
        packed_sb = sb("packed_sb", [128, 128], i32)
        tern_i = sb("tern_i", [128, 128], i32)
        tern = sb("tern", [128, 128], bf16)
        ternT = sb("ternT", [128, 128], bf16)
        neghalf = sb("neghalf", [128, NT])
        eps = sb("eps", [128, NT])
        zero = sb("zero", [128, 1])
        zero_col = zero[:, :]
        dve_slot = sb("dve_slot", [128, 1])

        x_sb = sb("x_sb", [128, NT, D])
        keysT = sb("keysT", [128, B, TAIL])
        stats = sb("stats", [128, NT, 6])
        meanvar = sb("meanvar", [128, NT, 2])
        vareps = sb("vareps", [128, NT])
        rstd = sb("rstd", [128, NT])

        class Carver:
            def __init__(self, handle):
                self.handle, self.at = handle, 0

            def take(self, shape, dt=fp32):
                n = 1
                for k in shape[1:]:
                    n *= k
                words = -(-n * (2 if dt == bf16 else 1 if dt == u8 else 4) // 4)
                v = self.handle[0:shape[0], self.at:self.at + words]
                self.at += words
                assert self.at <= self.handle.shape[1], self.at
                if dt != fp32:
                    v = v.bitcast(dt)[:, 0:n]
                if len(shape) == 3:
                    v = v.rearrange("p (a b) -> p a b", a=shape[1])
                if len(shape) == 4:
                    v = v.rearrange("p (a b c) -> p a b c", a=shape[1], b=shape[2])
                return v

        low, high = sb("low", [128, 14400]), sb("high", [128, 29000])

        one = Carver(low)
        ctxN, ctxT, prob = [None] * 2, [None] * 2, [None] * 2
        ctxN[1], ctxT[1], prob[1] = one.take([128, KT, D]), one.take([128, K]), one.take([128, K])
        ctxN[0], ctxT[0], prob[0] = one.take([128, KT, D]), one.take([128, K]), one.take([128, K])
        probT = one.take([128, KT, 128])
        xn = [one.take([128, QT, D]) for p in range(2)]
        xnT = [one.take([128, S]) for p in range(2)]
        projT = [one.take([128, S]) for p in range(2)]
        x1 = [one.take([128, QT, D]) for p in range(2)]
        xnB, yB = one.take([128, QT, D]), one.take([128, QT, D])
        xq, xqT = one.take([128, QT, D], bf16), one.take([128, S], bf16)
        nmax, rsum = sb("nmax", [128, NT]), sb("rsum", [128, NT])
        rgate = sb("rgate", [128, 2])
        statsB, mvB = sb("statsB", [128, QT, 6]), sb("mvB", [128, QT, 2])
        veB, rstdB = sb("veB", [128, QT]), sb("rstdB", [128, QT])
        amax, qscale, dscale = (sb(n, [128, QT]) for n in ("amax", "qscale", "dscale"))

        two = Carver(high)
        attn = two.take([128, NT, D])
        at_mask = two.at
        probs8 = two.take([128, 8, 4 * S])
        two.at = max(two.at, at_mask + (NT * (T0 - 1) + 3) // 4 + (NT * (TAIL + 1) + 3) // 4 + NT * TAIL // 2 + 8)
        kaug = [two.take([RA, H, TAIL], bf16) for p in range(2)]
        qaug = [two.take([RA, H, S], bf16) for p in range(2)]
        vaug = [two.take([TP, 4, H, 32]) for p in range(2)]
        two = Carver(low)
        two.at = KT * D + 2 * K
        headsT = two.take([128, 4, S])
        keysS = [two.take([128, TAIL]) for p in range(2)]
        xnC, xnCT = two.take([128, QT, D]), two.take([128, S])
        qf, kf = two.take([128, S]), two.take([128, TAIL])
        qres, kres = two.take([128, S]), two.take([128, TAIL])
        qpart = [two.take([128, 3, S], bf16) for p in range(2)]
        kpart = [two.take([128, 3, TAIL], bf16) for p in range(2)]
        nm = two.take([128, QT * H])
        nmres = two.take([H, S])
        nmpart = [two.take([H, 3, S], bf16) for p in range(2)]
        rden = two.take([128, H])
        chk = Carver(high)
        chk.at = at_mask
        maskA = chk.take([128, NT, T0 - 1], u8)
        maskB = chk.take([128, NT, TAIL + 1], u8)
        maskF = chk.take([128, NT, TAIL], bf16)
        maskpair, maskmin = sb("maskpair", [128, 1]), sb("maskmin", [128, 1])
        bad = sb("bad", [128, 3])
        sel15 = sb("sel15", [128, 2 * B - 1], bf16)
        cnt, cntv = sb("cnt", [B, TAIL]), sb("cntv", [B, TAIL])
        cmin = sb("cmin", [B, 2])
        maskrow = sb("maskrow", [B, TAIL], bf16)
        ones_col = sb("ones_col", [128, 1])
        badsum = sb("badsum", [1, 1])
        flag = sb("flag", [1, 1], i32)
        q_dram = [nc.dram_tensor(f"q_parts{p}", [3, D, S], bf16).ap() for p in range(2)]
        k_dram = [nc.dram_tensor(f"k_parts{p}", [3, D, TAIL], bf16).ap() for p in range(2)]
        nm_dram = [nc.dram_tensor(f"max_parts{p}", [3, H, S], bf16).ap() for p in range(2)]
        maskrow_dram = nc.dram_tensor("mask_rows", [B, TAIL], bf16).ap()

        gen = Carver(high)
        gen.at = at_mask
        maskQ, maskQF = gen.take([128, K], u8), gen.take([128, K], bf16)
        khead, qhead, vhead = gen.take([DH, K]), gen.take([DH, 128]), gen.take([128, KT, DH])
        negident = gen.take([128, 128], bf16)
        xnG, xnGT, qG = gen.take([128, QT, D]), gen.take([128, S]), gen.take([128, S])
        grecip, gmax, gsum = gen.take([128, 1]), gen.take([128, 1]), gen.take([128, 1])
        q_all = nc.dram_tensor("q_all", [B, QT, D, 128], fp32).ap()
        k_all = nc.dram_tensor("k_all", [B, D, K], fp32).ap()
        v_all = nc.dram_tensor("v_all", [B, K, D], fp32).ap()

        wts = Carver(low)
        w0e, w1e, woe = [None] * 2, [None] * 2, [None] * 2
        for p in range(2):
            w0e[p], w1e[p], woe[p] = wts.take([128, HID]), wts.take([128, HID]), wts.take([128, HC, D])
        tri = Carver(low)
        tri.at = KT * D + 2 * K
        ao = [tri.take([128, QT, D]) for p in range(2)]
        aoT = [tri.take([128, S]) for p in range(2)]
        x3t = tri.take([128, QT, D])
        xn3 = [tri.take([128, QT, D]) for p in range(2)]
        xn3T = [tri.take([128, S]) for p in range(2)]
        eoT = tri.take([128, E, B * CAP])
        comb2 = tri.take([128, QT, E * CAP])
        fin = Carver(high)
        fin.at = at_mask
        combT = fin.take([128, B, E * CAP // 128 * S])
        xT = fin.take([128, E, B * CAP])
        xn_all = fin.take([128, NT, D])
        iota_slot = fin.take([128, E * CAP])
        comb = [fin.take([128, QT, E * CAP]) for p in range(2)]
        disp = [fin.take([128, QT, E * CAP]) for p in range(2)]
        xs = [fin.take([128, QT, D]) for p in range(2)]
        gl = [fin.take([128, B * CAP]) for p in range(2)]
        hid = [fin.take([128, B * CAP]) for p in range(2)]
        eoS = [fin.take([128, E, CAP]) for p in range(2)]
        eo = [fin.take([128, E * CAP // 128, 128]) for p in range(2)]
        outT = [fin.take([128, S]) for p in range(2)]
        iota_e, logits, shifted, expd, raw, equal, cand, m1, m2, rest, pos1, pos2, kept, work = (
            fin.take([128, NT, E]) for _ in range(14))
        m12 = fin.take([128, 2 * NT * E], bf16)
        count1 = fin.take([128, B, E])
        upper, allones = fin.take([128, 128], bf16), fin.take([128, 128], bf16)
        gmx, gate1, gate2, least1, least2, keep1, keep2, place1, place2, slot1, slot2 = (fin.take([128, NT]) for _ in range(11))

        PS = stack.enter_context(nc.psum_tensor("PS", [128, 4096], fp32))
        bank = [PS[:, 512 * i:512 * i + 512] for i in range(8)]
        S_ps, TA, TB, O_ps, M_ps = PS[:, 0:K], bank[4], bank[5], bank[6], bank[7]
        Mb = M_ps.bitcast(bf16)

        x_loaded, xrest_loaded, w_loaded, ternary_loaded = sem("x_loaded"), sem("xrest_loaded"), sem("w_loaded"), sem("ternary_loaded")
        ctx_loaded = [sem(f"ctx_loaded{p}") for p in range(2)]
        ident_ready, gates_ready = sem("ident_ready"), sem("gates_ready")
        tern_ready, ternT_filled, ternT_ready = sem("tern_ready"), sem("ternT_filled"), sem("ternT_ready")
        ln_stats, rstd_ready = sem("ln_stats"), sem("rstd_ready")
        xn_ready, xnT_filled, xnT_ready = sem("xn_ready"), sem("xnT_filled"), sem("xnT_ready")
        proj_filled, projT_ready = sem("proj_filled"), sem("projT_ready")
        TA_filled, TA_drained = sem("TA_filled"), sem("TA_drained")
        TB_filled, TB_drained = sem("TB_filled"), sem("TB_drained")
        keys_saved = sem("keys_saved")
        S_filled, max_done, exp_done, prob_used = sem("S_filled"), sem("max_done"), sem("exp_done"), sem("prob_used")
        O_filled, O_drained = sem("O_filled"), sem("O_drained")
        statsB_ready, rstdB_ready = sem("statsB_ready"), sem("rstdB_ready")
        xq_ready, xqT_filled, xqT_ready = sem("xq_ready"), sem("xqT_filled"), sem("xqT_ready")
        y_filled, x2_ready = sem("y_filled"), sem("x2_ready")
        out_stored = sem("out_stored")
        mask_loaded, mask_and, maskF_ready = sem("mask_loaded"), sem("mask_and"), sem("maskF_ready")
        consts2_ready = sem("consts2_ready")
        cnt_filled, bad_ready, bad_filled, flag_ready = sem("cnt_filled"), sem("bad_ready"), sem("bad_filled"), sem("flag_ready")
        maskrow_ready, maskrow_saved = sem("maskrow_ready"), sem("maskrow_saved")
        keysS_ready = sem("keysS_ready")
        lnC_stats, rstdC_ready, xnC_ready = sem("lnC_stats"), sem("rstdC_ready"), sem("xnC_ready")
        xnCT_filled, xnCT_ready = sem("xnCT_filled"), sem("xnCT_ready")
        q_filled, q_ready, k_filled, k_ready = sem("q_filled"), sem("q_ready"), sem("k_filled"), sem("k_ready")
        v_filled, v_ready, parts_ready = sem("v_filled"), sem("v_ready"), sem("parts_ready")
        parts_saved = [sem(f"parts_saved{p}") for p in range(2)]
        aug_loaded = [sem(f"aug_loaded{p}") for p in range(2)]
        S1_filled, S1_max = sem("S1_filled"), sem("S1_max")
        nmT_filled, nm_ready = sem("nmT_filled"), sem("nm_ready")
        nm_saved = [sem(f"nm_saved{p}") for p in range(2)]
        nm_loaded = [sem(f"nm_loaded{p}") for p in range(2)]
        ST_filled, P_ready = sem("ST_filled"), sem("P_ready")
        PV_filled, heads_ready, back_filled, attn_ready = sem("PV_filled"), sem("heads_ready"), sem("back_filled"), sem("attn_ready")
        g_loaded, g_stats, g_rstd, g_xn = sem("g_loaded"), sem("g_stats"), sem("g_rstd"), sem("g_xn")
        g_T_filled, g_T_drained = sem("g_T_filled"), sem("g_T_drained")
        g_xT_filled, g_xT_ready = sem("g_xT_filled"), sem("g_xT_ready")
        g_q_filled, g_q_ready, g_k_filled, g_k_ready = sem("g_q_filled"), sem("g_q_ready"), sem("g_k_filled"), sem("g_k_ready")
        g_v_filled, g_v_ready, g_saved = sem("g_v_filled"), sem("g_v_ready"), sem("g_saved")
        g_neg, g_mask_loaded, g_mask_ready, g_head_loaded = sem("g_neg"), sem("g_mask_loaded"), sem("g_mask_ready"), sem("g_head_loaded")
        g_S_filled, g_max, g_exp, g_O_filled, g_free = sem("g_S_filled"), sem("g_max"), sem("g_exp"), sem("g_O_filled"), sem("g_free")
        g_S_free = sem("g_S_free")
        wts_loaded = [sem(f"wts_loaded{p}") for p in range(2)]
        ao_ready, aoT_filled, aoT_ready, wo_filled = sem("ao_ready"), sem("aoT_filled"), sem("aoT_ready"), sem("wo_filled")
        x3_read, x3_stats, x3_rstd, xn3_ready = sem("x3_read"), sem("x3_stats"), sem("x3_rstd"), sem("xn3_ready")
        xn3_saved, xn3T_filled, xn3T_ready = sem("xn3_saved"), sem("xn3T_filled"), sem("xn3T_ready")
        lg_filled, lg_ready, gconst_ready = sem("lg_filled"), sem("lg_ready"), sem("gconst_ready")
        shifted_ready, expd_ready, m12_ready, cum_filled = sem("shifted_ready"), sem("expd_ready"), sem("m12_ready"), sem("cum_filled")
        slots_ready, xs_ready, comb_ready = sem("slots_ready"), sem("xs_ready"), sem("comb_ready")
        xT_filled, xT_drained = sem("xT_filled"), sem("xT_drained")
        cA_filled, cA_drained, cB_filled, cB_drained = sem("cA_filled"), sem("cA_drained"), sem("cB_filled"), sem("cB_drained")
        a_filled, b_filled, gelu_done, hid_ready = sem("a_filled"), sem("b_filled"), sem("gelu_done"), sem("hid_ready")
        hid_used, eo_filled, eoT_ready = sem("hid_used"), sem("eo_filled"), sem("eoT_ready")
        eoS_ready, eoX_filled, eo_ready = sem("eoS_ready"), sem("eoX_filled"), sem("eo_ready")
        outT_filled, outT_ready, y_back_filled, x4_ready = sem("outT_filled"), sem("outT_ready"), sem("y_back_filled"), sem("x4_ready")
        dve_gen, dve_late, pool_late = sem("dve_gen"), sem("dve_late"), sem("pool_late")
        dve_fast, pool_fast = sem("dve_fast"), sem("pool_fast")
        dve_order, act_order, pool_order = sem("dve_order"), sem("act_order"), sem("pool_order")

        S1 = [bank[0][:, 0:TAIL], bank[1][:, 0:TAIL]]
        ST = [PS[0:TP, 1024 * (1 + j):1024 * (2 + j)] for j in range(2)]
        PV = bank[6][:, 0:S]

        TCH = [(0, 4), (4, 8), (8, 12), (12, KT)]

        def fills(b, k, first):
            return k if first else 6 * b + (k - 2)

        def half(n, p, per, more):
            return per * (n // 2) + more if isinstance(n, int) else (per // 2) * n + (more - per // 2 * p)

        block = stack.enter_context(nc.Block())

        @block.sync
        def _(sp):
            sp.dma_start(x_sb[:, 0:2, :], x.rearrange("b (t p) d -> p (b t) d", p=128)[:, 0:2, :]).then_inc(x_loaded, 16)

            def load_ctx(b, p):
                src = ctx_in[b, :, :] if isinstance(b, int) else ctx_in[ds(b, 1), :, :].rearrange("a k d -> (a k) d")
                sp.dma_start(ctxN[p][:, 0:KT - 1, :],
                             src[0:128 * (KT - 1), :].rearrange("(t p) d -> p t d", p=128)).then_inc(ctx_loaded[p], 16)
                sp.dma_start(ctxN[p][0:KR, KT - 1, :], src[128 * (KT - 1):K, :]).then_inc(ctx_loaded[p], 16)

            load_ctx(0, 0)
            sp.dma_start(x_sb[:, 2:NT, :], x.rearrange("b (t p) d -> p (b t) d", p=128)[:, 2:NT, :]).then_inc(xrest_loaded, 16)
            load_ctx(1, 1)
            with sp.Fori(1, B // 2) as i:
                for p in range(2):
                    sp.wait_ge(O_filled, 4 * i + (2 * p - 2))
                    load_ctx(2 * i + p, p)
            sp.wait_ge(maskrow_ready, 1)
            sp.dma_start(maskrow_dram, maskrow[:, :]).then_inc(maskrow_saved, 16)
            sp.wait_ge(maskrow_saved, 16)

            def save_parts(n, p):
                sp.wait_ge(parts_ready, n + 1)
                sp.dma_start(q_dram[p].rearrange("c r q -> r c q"), qpart[p]).then_inc(parts_saved[p], 16)
                sp.dma_start(k_dram[p].rearrange("c r q -> r c q"), kpart[p]).then_inc(parts_saved[p], 16)
                sp.wait_ge(parts_saved[p], half(n, p, 32, 32))
                for g in range(NPROD):
                    sp.dma_start(qaug[p][DH * g:DH * g + DH, :, :],
                                 q_dram[p][QPART[g], :, :].rearrange("(h d) q -> d h q", d=DH)).then_inc(aug_loaded[p], 16)
                    sp.dma_start(kaug[p][DH * g:DH * g + DH, :, :],
                                 k_dram[p][KPART[g], :, :].rearrange("(h d) q -> d h q", d=DH)).then_inc(aug_loaded[p], 16)
                row = maskrow_dram[n:n + 1, :] if isinstance(n, int) else maskrow_dram[ds(n, 1), :]
                sp.dma_start(kaug[p][RS:RM, :, :],
                             row.unsqueeze(1).to_broadcast([1, H, TAIL])).then_inc(aug_loaded[p], 16)

            def save_max(n, p):
                sp.wait_ge(nm_ready, n + 1)
                sp.dma_start(nm_dram[p].rearrange("c h q -> h c q"), nmpart[p]).then_inc(nm_saved[p], 16)
                sp.wait_ge(nm_saved[p], half(n, p, 16, 16))
                sp.dma_start(qaug[p][RM:RA, :, :], nm_dram[p]).then_inc(nm_loaded[p], 16)

            sp.wait_ge(flag_ready, 1)
            general = sp.value_load(flag[0:1, 0:1])
            with sp.If(general > 0):
                def load_batch(b):
                    src = ctx_in[b, :, :] if isinstance(b, int) else ctx_in[ds(b, 1), :, :].rearrange("a k d -> (a k) d")
                    sp.dma_start(ctxN[0][:, 0:KT - 1, :],
                                 src[0:128 * (KT - 1), :].rearrange("(t p) d -> p t d", p=128)).then_inc(g_loaded, 16)
                    sp.dma_start(ctxN[0][0:KR, KT - 1, :], src[128 * (KT - 1):K, :]).then_inc(g_loaded, 16)

                def save_batch(b):
                    sp.wait_ge(g_q_ready, b + 1)
                    sp.dma_start(q_all[b:b + 1, :, :, :].rearrange("a q r s -> r (a q) s") if isinstance(b, int) else
                                 q_all[ds(b, 1), :, :, :].rearrange("a q r s -> r (a q) s"),
                                 qG.rearrange("r (q s) -> r q s", q=QT)).then_inc(g_saved, 16)
                    sp.wait_ge(g_k_ready, b + 1)
                    sp.dma_start(k_all[b, :, :] if isinstance(b, int) else k_all[ds(b, 1), :, :].rearrange("a r k -> (a r) k"),
                                 prob[0]).then_inc(g_saved, 16)
                    sp.wait_ge(g_v_ready, b + 1)
                    dst = v_all[b, :, :] if isinstance(b, int) else v_all[ds(b, 1), :, :].rearrange("a k d -> (a k) d")
                    sp.dma_start(dst[0:128 * (KT - 1), :].rearrange("(t p) d -> p t d", p=128),
                                 ctxN[0][:, 0:KT - 1, :]).then_inc(g_saved, 16)
                    sp.dma_start(dst[128 * (KT - 1):K, :], ctxN[0][0:KR, KT - 1, :]).then_inc(g_saved, 16)

                load_batch(0)
                with sp.Fori(1, B) as b:
                    save_batch(b - 1)
                    sp.wait_ge(g_saved, 64 * b)
                    load_batch(b)
                save_batch(B - 1)
                sp.wait_ge(g_saved, 64 * B)
                with sp.Fori(0, B) as b:
                    for q in range(QT):
                        with sp.Fori(0, H) as h:
                            sp.wait_ge(g_free, 2 * H * b + h + (H * q + 1))
                            sp.dma_start(qhead, q_all.rearrange("b q (h d) s -> (b q h) d s", d=DH)[ds(2 * H * b + h + H * q, 1), :, :]
                                         .rearrange("a d s -> (a d) s")).then_inc(g_head_loaded, 16)
                            sp.dma_start(khead, k_all.rearrange("b (h d) k -> (b h) d k", d=DH)[ds(H * b + h, 1), :, :]
                                         .rearrange("a d k -> (a d) k")).then_inc(g_head_loaded, 16)
                            vh = v_all[ds(b, 1), :, ds(DH * h, DH)].rearrange("a k d -> (a k) d")
                            sp.dma_start(vhead[:, 0:KT - 1, :],
                                         vh[0:128 * (KT - 1), :].rearrange("(t p) d -> p t d", p=128)).then_inc(g_head_loaded, 16)
                            sp.dma_start(vhead[0:KR, KT - 1, :], vh[128 * (KT - 1):K, :]).then_inc(g_head_loaded, 16)
            with sp.Else():
                save_parts(0, 0)
                save_max(0, 0)
                save_parts(1, 1)
                save_max(1, 1)
                with sp.Fori(1, B // 2) as i:
                    for p in range(2):
                        save_parts(2 * i + p, p)
                        save_max(2 * i + p, p)

            def load_expert(e, p):
                def of(w):
                    return w[e, :, :] if isinstance(e, int) else w[ds(e, 1), :, :].rearrange("a m h -> (a m) h")
                sp.dma_start(w0e[p], of(we0)).then_inc(wts_loaded[p], 16)
                sp.dma_start(w1e[p], of(we1)).then_inc(wts_loaded[p], 16)
                sp.dma_start(woe[p][:, 0:HC - 2, :],
                             of(weo)[0:128 * (HC - 2), :].rearrange("(t p) d -> p t d", p=128)).then_inc(wts_loaded[p], 16)
                sp.dma_start(woe[p][0:HR, HC - 2:HC, :],
                             of(weo)[128 * (HC - 2):HID, :].rearrange("(t p) d -> p t d", p=HR)).then_inc(wts_loaded[p], 16)

            load_expert(0, 0)
            load_expert(1, 1)
            with sp.Fori(1, E // 2) as i:
                for p in range(2):
                    sp.wait_ge(eo_filled, 2 * i + (p - 1))
                    load_expert(2 * i + p, p)
            out_t = out.rearrange("b (t p) d -> p (b t) d", p=128)
            with sp.Fori(0, B) as b:
                sp.wait_ge(x4_ready, b + 1)
                sp.dma_start(out_t[:, ds(QT * b, QT), :], x_sb[:, ds(QT * b, QT), :]).then_inc(out_stored, 16)
            sp.wait_ge(out_stored, 16 * B)

        @block.gpsimd
        def _(pool):
            order = Tally(pool, pool_order)
            order.link(nc.gpsimd.memset(ident[:, :], 0.0))
            order.link(nc.gpsimd.affine_select(out=ident[:, :], in_=ident[:, :], compare_op=ALU.not_equal, fill=1.0,
                                               base=0, pattern=[[-1, 128]], channel_multiplier=1))
            nc.gpsimd.memset(eps[:, :], EPS)
            nc.gpsimd.memset(zero[:, :], 0.0)
            nc.gpsimd.memset(neghalf[:, :], -0.5).then_inc(ident_ready, 1)
            nc.gpsimd.tensor_copy(identb[:, :], ident[:, :]).then_inc(ident_ready, 1)
            pool.wait_ge(ident_ready, 2)
            for k, (lo, hi) in enumerate(((0, 2), (2, NT))):
                pool.wait_ge(ln_stats, k + 1)
                order.link(nc.gpsimd.tensor_scalar(vareps[:, lo:hi], meanvar[:, lo:hi, 1], EPS, None, ALU.add))
                nc.gpsimd.tensor_tensor(rstd[:, lo:hi], vareps[:, lo:hi], neghalf[:, lo:hi], ALU.pow).then_inc(rstd_ready, 1)

            def save_keys(b, p, first):
                pool.wait_ge(TA_drained, fills(b, 2, first))
                pool.wait_ge(TB_drained, fills(b, 2, first))
                nc.gpsimd.tensor_copy(keysT[:, b, :] if isinstance(b, int) else keysT[:, ds(b, 1), :].rearrange("p a k -> p (a k)"),
                                      ctxT[p][:, T0:K]).then_inc(keys_saved, 1)

            def rstd_b(b):
                pool.wait_ge(statsB_ready, b + 1)
                order.link(nc.gpsimd.tensor_tensor(veB[:, :], mvB[:, :, 1], eps[:, 0:QT], ALU.add))
                nc.gpsimd.tensor_tensor(rstdB[:, :], veB[:, :], neghalf[:, 0:QT], ALU.pow).then_inc(rstdB_ready, 1)

            for p in range(2):
                nc.gpsimd.memset(kaug[p], 1.0).then_inc(consts2_ready, 1)
                nc.gpsimd.memset(qaug[p], 1.0).then_inc(consts2_ready, 1)
                order.link(nc.gpsimd.memset(vaug[p], 0.0))
                nc.gpsimd.memset(vaug[p][:, :, :, DH:DH + 1], 1.0).then_inc(consts2_ready, 1)
            nc.gpsimd.memset(ones_col[:, :], 1.0).then_inc(consts2_ready, 1)
            nc.gpsimd.memset(bad[:, :], 0.0).then_inc(consts2_ready, 1)
            order.link(nc.gpsimd.memset(sel15[:, :], 0.0))
            nc.gpsimd.memset(sel15[:, B - 1:B], 1.0).then_inc(consts2_ready, 1)
            save_keys(0, 0, True)
            save_keys(1, 1, False)
            rstd_b(0)
            pool.wait_ge(mask_loaded, 32)
            nc.gpsimd.tensor_copy(maskF, maskB[:, :, 1:TAIL + 1]).then_inc(maskF_ready, 1)
            for i in order.loop(1, B // 2, 2):
                for p in range(2):
                    save_keys(2 * i + p, p, False)
                    rstd_b(2 * i + (p - 1))
            rstd_b(B - 1)

            pool.wait_ge(flag_ready, 1)
            general = pool.value_load(flag[0:1, 0:1])
            with pool.If(general > 0):
                nc.gpsimd.tensor_scalar(negident, identb[:, :], NEG, None, ALU.mult).then_inc(g_neg, 1)
                nc.gpsimd.memset(grecip, 1.0).then_inc(g_free, 1)
                with pool.Fori(0, B) as b:
                    pool.wait_ge(g_stats, b + 1)
                    nc.gpsimd.tensor_tensor(veB[:, :], mvB[:, :, 1], eps[:, 0:QT], ALU.add).then_inc(g_neg, 1)
                    pool.wait_ge(g_neg, b + 2)
                    nc.gpsimd.tensor_tensor(rstdB[:, :], veB[:, :], neghalf[:, 0:QT], ALU.pow).then_inc(g_rstd, 1)
            with pool.Else():
                fast = Tally(pool, pool_fast)

                def split(n, p, again):
                    if again:
                        pool.wait_ge(v_ready, n - 1)
                    nc.gpsimd.tensor_tensor(keysS[p], keysT[:, ds(n, 1), :].rearrange("p a k -> p (a k)"),
                                            zero_col.to_broadcast([128, TAIL]), ALU.add).then_inc(keysS_ready, 1)
                    pool.wait_ge(lnC_stats, n + 1)
                    fast.link(nc.gpsimd.tensor_tensor(veB[:, :], mvB[:, :, 1], eps[:, 0:QT], ALU.add))
                    nc.gpsimd.tensor_tensor(rstdB[:, :], veB[:, :], neghalf[:, 0:QT], ALU.pow).then_inc(rstdC_ready, 1)
                    if again:
                        pool.wait_ge(parts_saved[p], half(n, p, 32, 0))
                        pool.wait_ge(ST_filled, 16 * n - 16)
                    for filled, full, res, part in ((q_ready, qf, qres, qpart[p]), (k_ready, kf, kres, kpart[p])):
                        pool.wait_ge(filled, n + 1)
                        fast.link(nc.gpsimd.tensor_tensor(part[:, 0, :], full, zero_col.to_broadcast(list(full.shape)), ALU.add))
                        fast.link(nc.gpsimd.tensor_tensor(res, full, part[:, 0, :], ALU.subtract))
                        fast.link(nc.gpsimd.tensor_tensor(part[:, 1, :], res, zero_col.to_broadcast(list(full.shape)), ALU.add))
                        last = nc.gpsimd.tensor_tensor(part[:, 2, :], res, part[:, 1, :], ALU.subtract)
                        if full is qf:
                            fast.link(last)
                        else:
                            last.then_inc(parts_ready, 1)

                split(0, 0, False)
                split(1, 1, False)
                for i in fast.loop(1, B // 2, 16):
                    for p in range(2):
                        split(2 * i + p, p, True)

            late = Tally(pool, pool_late)
            pool.wait_ge(attn_ready, NT)
            nc.gpsimd.iota(iota_slot, pattern=[[1, E * CAP]], base=0, channel_multiplier=0,
                           allow_small_or_imprecise_dtypes=True).then_inc(gconst_ready, 1)
            nc.gpsimd.iota(iota_e, pattern=[[0, NT], [1, E]], base=0, channel_multiplier=0,
                           allow_small_or_imprecise_dtypes=True).then_inc(gconst_ready, 1)
            nc.gpsimd.memset(allones, 1.0).then_inc(gconst_ready, 1)
            pool.wait_ge(gconst_ready, 3)
            nc.gpsimd.affine_select(out=upper, in_=allones, compare_op=ALU.is_gt, fill=0.0,
                                    base=0, pattern=[[1, 128]], channel_multiplier=-1).then_inc(gconst_ready, 1)

            def norm3(b, p):
                pool.wait_ge(x3_stats, b + 1)
                late.link(nc.gpsimd.tensor_tensor(veB[:, :], mvB[:, :, 1], eps[:, 0:QT], ALU.add))
                nc.gpsimd.tensor_tensor(rstdB[:, :], veB[:, :], neghalf[:, 0:QT], ALU.pow).then_inc(x3_rstd, 1)
                pool.wait_ge(xn3_ready, QT * b + QT)
                nc.gpsimd.tensor_tensor(xn_all[:, ds(QT * b, QT), :], xn3[p], zero_col.unsqueeze(2).to_broadcast([128, QT, D]),
                                        ALU.add).then_inc(xn3_saved, 1)

            norm3(0, 0)
            norm3(1, 1)
            for i in late.loop(1, B // 2, 2):
                for p in range(2):
                    norm3(2 * i + p, p)

            def take_tokens(b, p, again):
                if again:
                    pool.wait_ge(xT_filled, b - 1)
                nc.gpsimd.tensor_tensor(xs[p], xn_all[:, ds(QT * b, QT), :], zero_col.unsqueeze(2).to_broadcast([128, QT, D]),
                                        ALU.add).then_inc(xs_ready, 1)

            pool.wait_ge(xn3_saved, B)
            take_tokens(0, 0, False)
            take_tokens(1, 1, False)
            with pool.Fori(1, B // 2) as i:
                for p in range(2):
                    take_tokens(2 * i + p, p, True)

            def take_slots(g, p, again):
                if again:
                    pool.wait_ge(eoX_filled, g - 1)
                nc.gpsimd.tensor_tensor(eoS[p], eoT[:, :, ds(CAP * g, CAP)], zero_col.unsqueeze(2).to_broadcast([128, E, CAP]),
                                        ALU.add).then_inc(eoS_ready, 1)

            pool.wait_ge(eoT_ready, E)
            take_slots(0, 0, False)
            take_slots(1, 1, False)
            with pool.Fori(1, B // 2) as i:
                for p in range(2):
                    take_slots(2 * i + p, p, True)

        @block.scalar
        def _(act):
            for dst, src in ((w0_sb, w0), (wq_sb, wq), (wk_sb, wk), (wv_sb, wv), (wo_sb, wo), (router_sb, router)):
                act.dma_start(dst[:, :], src).then_inc(w_loaded, 16)
            for dst, src in ((b0_col, b0), (bq_col, bq), (bk_col, bk)):
                act.dma_start(dst[:, :], src.rearrange("(p a) -> p a", a=1)).then_inc(w_loaded, 16)
            for dst, src in ((fb_row, fbias), (bv_row, bv), (bo_row, bo), (gates_in[:, 0:2], g_xattn),
                             (gates_in[:, 2:4], g_ffn), (ws_col, wscale)):
                act.dma_start(dst[:, :], src.rearrange("(a n) -> a n", a=1).to_broadcast([128, src.shape[0]])).then_inc(w_loaded, 16)
            for j in range(4):
                act.dma_start(packed_sb[32 * j:32 * j + 32, :], packed.rearrange("(r i) -> r i", r=32)).then_inc(ternary_loaded, 16)
            masks = mask.rearrange("b a (t p) k -> p (b a t) k", p=128)
            act.dma_start(maskA, masks[:, :, 0:T0 - 1]).then_inc(mask_loaded, 16)
            act.dma_start(maskB, masks[:, :, T0 - 1:K]).then_inc(mask_loaded, 16)
            act.wait_ge(w_loaded, 16 * 15)
            nc.scalar.activation(gates[:, :], gates_in[:, :], ACT.Tanh).then_inc(gates_ready, 1)

            def drain_ctx(b, p, first):
                for k, c in enumerate((0, 2)):
                    lo, hi = 128 * TCH[c][0], 128 * TCH[c][1]
                    act.wait_ge(TA_filled, fills(b, k + 1, first))
                    if k == 0 and (not isinstance(b, int) or b >= 2):
                        act.wait_ge(keys_saved, b - 1)
                    nc.scalar.activation(ctxT[p][:, lo:hi], TA[:, 0:hi - lo], ACT.Copy).then_inc(TA_drained, 1)

            def drain_probs(b, k0, first):
                for k, c in enumerate((0, 2)):
                    act.wait_ge(TA_filled, fills(b, k0 + k + 1, first))
                    n = TCH[c][1] - TCH[c][0]
                    nc.scalar.activation(probT[:, TCH[c][0]:TCH[c][1], :],
                                         TA.rearrange("p (t q) -> p t q", q=128)[:, 0:n, :], ACT.Copy).then_inc(TA_drained, 1)

            def softmax(b, q):
                act.wait_ge(max_done, 2 * b + (q + 1))
                if not isinstance(b, int) or b >= 1:
                    act.wait_ge(prob_used, 2 * b + (q - 1))
                u = 2 * b + q
                nc.scalar.activation(prob[q][:, :], S_ps, ACT.Exp, bias=nmax[:, ds(u, 1)],
                                     accum_out=rsum[:, ds(u, 1)]).then_inc(exp_done, 1)

            def body(b, p, first):
                drain_ctx(b, p, first)
                if not first:
                    drain_probs(b, 2, first)
                softmax(b, 0)
                drain_probs(b, 2 if first else 4, first)
                softmax(b, 1)

            body(0, 0, True)
            body(1, 1, False)
            with act.Fori(1, B // 2) as i:
                for p in range(2):
                    body(2 * i + p, p, False)
            drain_probs(B, 0, False)

            act.wait_ge(flag_ready, 1)
            general = act.value_load(flag[0:1, 0:1])
            with act.If(general > 0):
                with act.Fori(0, B) as b:
                    for c in range(4):
                        lo, hi = 128 * TCH[c][0], min(128 * TCH[c][1], K)
                        act.wait_ge(g_T_filled, 4 * b + (c + 1))
                        nc.scalar.activation(ctxT[0][:, lo:hi], (TA, TB)[c % 2][:, 0:hi - lo], ACT.Copy).then_inc(g_T_drained, 1)
                with act.Fori(0, B) as b:
                    for q in range(QT):
                        act.wait_ge(g_free, 2 * H * b + (H * q + 1))
                        act.dma_start(maskQ, mask[ds(b, 1), :, 128 * q:128 * q + 128, :].rearrange("a c q k -> (a c q) k")
                                      ).then_inc(g_mask_loaded, 16)
                        with act.Fori(0, H) as h:
                            u = 2 * H * b + h + H * q
                            act.wait_ge(g_max, u + 1)
                            nc.scalar.activation(prob[0], S_ps, ACT.Exp, bias=gmax, accum_out=gsum).then_inc(g_exp, 1)
                            for c in range(4):
                                n, rows = TCH[c][1] - TCH[c][0], 128 if c < 3 else KR
                                act.wait_ge(g_T_filled, 4 * u + (4 * B + c + 1))
                                nc.scalar.activation(probT[0:rows, TCH[c][0]:TCH[c][1], :],
                                                     (TA, TB)[c % 2].rearrange("p (t q) -> p t q", q=128)[0:rows, 0:n, :],
                                                     ACT.Copy).then_inc(g_T_drained, 1)
            with act.Else():
                def heads(b, first):
                    for h in range(H):
                        act.wait_ge(ST_filled, 16 * b + (h + 1))
                        if h % 4 == 0 and not (first and h < 8):
                            act.wait_ge(PV_filled, 4 * b + (h // 4 - 1))
                        nc.scalar.activation(probs8[0:TP, h % 8, :], ST[h % 2], ACT.Exp).then_inc(P_ready, 1)
                        if h >= 7 and h % 4 == 3:
                            drain(b, h // 4 - 1)
                    drain(b, 3)

                def drain(b, g):
                    act.wait_ge(PV_filled, 4 * b + (g + 1))
                    nc.scalar.activation(headsT[:, g, :], PV, ACT.Copy).then_inc(heads_ready, 1)

                heads(0, True)
                with act.Fori(1, B) as b:
                    heads(b, False)

            act.wait_ge(attn_ready, NT)

            def drain_tokens(b, p):
                act.wait_ge(xn3T_filled, b + 1)
                nc.scalar.activation(xn3T[p], bank[4 + p][:, 0:S], ACT.Copy).then_inc(xn3T_ready, 1)

            def out_projection(b, p, first):
                nc.scalar.activation(ao[p], attn[:, ds(QT * b, QT), :], ACT.Copy).then_inc(ao_ready, 1)
                act.wait_ge(aoT_filled, b + 1)
                nc.scalar.activation(aoT[p], bank[p][:, 0:S], ACT.Copy).then_inc(aoT_ready, 1)
                if not first:
                    drain_tokens(b - 1, 1 - p)

            out_projection(0, 0, True)
            out_projection(1, 1, False)
            with act.Fori(1, B // 2) as i:
                for p in range(2):
                    out_projection(2 * i + p, p, False)
            drain_tokens(B - 1, 1)

            act.wait_ge(shifted_ready, 1)
            nc.scalar.activation(expd, shifted, ACT.Exp).then_inc(expd_ready, 1)

            with act.Fori(0, B // 2) as i:
                for p in range(2):
                    b = 2 * i + p
                    act.wait_ge(xT_filled, b + 1)
                    nc.scalar.activation(xT[:, :, ds(CAP * b, CAP)], bank[p].rearrange("p (e c) -> p e c", e=E), ACT.Copy).then_inc(xT_drained, 1)
                    act.wait_ge(cA_filled, b + 1)
                    nc.scalar.activation(combT[:, ds(b, 1), 0:512].rearrange("p a n -> p (a n)"), bank[2 + 2 * p], ACT.Copy).then_inc(cA_drained, 1)

            def gelus(e, p, first):
                for c in range(HC):
                    rows = HROWS[c]
                    act.wait_ge(a_filled, HC * e + (c + 1))
                    if not (first and c < 2):
                        act.wait_ge(hid_ready, HC * e + (c - 1))
                    nc.scalar.activation(gl[c % 2][0:rows, :], bank[c % 2][0:rows, :], ACT.Gelu_apprx_tanh).then_inc(gelu_done, 1)
                    if c == 1 and not first:
                        drain_expert(e - 1, 1 - p)

            def drain_expert(e, p):
                act.wait_ge(eo_filled, e + 1)
                nc.scalar.activation(eoT[:, ds(e, 1), :].rearrange("p a n -> p (a n)"), bank[4 + p], ACT.Copy).then_inc(eoT_ready, 1)

            gelus(0, 0, True)
            gelus(1, 1, False)
            with act.Fori(1, E // 2) as i:
                for p in range(2):
                    gelus(2 * i + p, p, False)
            drain_expert(E - 1, 1)

            with act.Fori(0, B // 2) as i:
                for p in range(2):
                    g = 2 * i + p
                    act.wait_ge(outT_filled, g + 1)
                    nc.scalar.activation(outT[p], bank[2 + p][:, 0:S], ACT.Copy).then_inc(outT_ready, 1)

        @block.vector
        def _(dve):
            order = Tally(dve, dve_order)

            def ln(lo, hi):
                for t in range(lo, hi):
                    m = order.mark(nc.vector.bn_stats(stats[:, t, :], x_sb[:, t, :]))
                dve.wait_ge(dve_order, m)
                for t in range(lo, hi):
                    last = nc.vector.bn_aggr(meanvar[:, t, :], stats[:, t, :])
                last.then_inc(ln_stats, 1)

            dve.wait_ge(x_loaded, 16)
            ln(0, 2)
            dve.wait_ge(ternary_loaded, 64)
            for j in range(4):
                m = order.mark(nc.vector.tensor_scalar(tern_i[32 * j:32 * j + 32, :], packed_sb[32 * j:32 * j + 32, :],
                                                       2 * j, 3, ALU.logical_shift_right, ALU.bitwise_and))
            dve.wait_ge(dve_order, m)
            nc.vector.tensor_scalar(tern[:, :], tern_i[:, :], -1.0, None, ALU.add).then_inc(tern_ready, 1)
            dve.wait_ge(xrest_loaded, 16)
            ln(2, NT)
            dve.wait_ge(w_loaded, 16 * 15)

            def normalise(b, p):
                if not isinstance(b, int) or b >= 2:
                    pass
                for q in range(QT):
                    u = 2 * b + q
                    src = x_sb[:, u, :] if isinstance(b, int) else x_sb[:, ds(u, 1), :].rearrange("p a d -> p (a d)")
                    nc.vector.tensor_scalar(xn[p][:, q, :], src, meanvar[:, ds(u, 1), 0], rstd[:, ds(u, 1)],
                                            ALU.subtract, ALU.mult).then_inc(xn_ready, 1)

            def prep(b, p, first):
                dve.wait_ge(xnT_filled, b + 1)
                nc.vector.tensor_copy(xnT[p][:, :], M_ps[:, 0:S]).then_inc(xnT_ready, 1)
                if first:
                    dve.wait_ge(ternT_filled, 1)
                    nc.vector.tensor_copy(ternT[:, :], TB.bitcast(bf16)[:, 0:128]).then_inc(ternT_ready, 1)
                for k, c in enumerate((1, 3)):
                    lo, hi = 128 * TCH[c][0], min(128 * TCH[c][1], K)
                    dve.wait_ge(TB_filled, fills(b, k + 1, first))
                    if k == 0 and (not isinstance(b, int) or b >= 2):
                        dve.wait_ge(keys_saved, b - 1)
                    nc.vector.tensor_copy(ctxT[p][:, lo:hi], TB[:, 0:hi - lo]).then_inc(TB_drained, 1)
                    if k == 0:
                        dve.wait_ge(proj_filled, b + 1)
                        nc.vector.tensor_scalar(projT[p][:, :], M_ps[:, S:2 * S], b0_col[:, :], None, ALU.add).then_inc(projT_ready, 1)

            def maximum(b, q):
                u = 2 * b + q
                dve.wait_ge(S_filled, u + 1)
                nc.vector.tensor_reduce(nmax[:, ds(u, 1)], S_ps, AX.X, ALU.max, negate=True).then_inc(max_done, 1)

            def drain_probs(b, k0, first):
                for k, c in enumerate((1, 3)):
                    n = TCH[c][1] - TCH[c][0]
                    rows = 128 if c == 1 else KR
                    dve.wait_ge(TB_filled, fills(b, k0 + k + 1, first))
                    nc.vector.tensor_copy(probT[0:rows, TCH[c][0]:TCH[c][1], :],
                                          TB.rearrange("p (t q) -> p t q", q=128)[0:rows, 0:n, :]).then_inc(TB_drained, 1)

            def attend(b, q, p):
                u = 2 * b + q
                dve.wait_ge(exp_done, u + 1)
                order.link(nc.vector.reciprocal(rgate[:, 0:1], rsum[:, ds(u, 1)]))
                order.link(nc.vector.tensor_scalar(rgate[:, 1:2], rgate[:, 0:1], gates[:, 0:1], None, ALU.mult))
                dve.wait_ge(O_filled, u + 1)
                xt = x_sb[:, ds(u, 1), :].rearrange("p a d -> p (a d)")
                nc.vector.scalar_tensor_tensor(x1[p][:, q, :], O_ps[:, 0:D], rgate[:, 1:2], xt, ALU.mult, ALU.add).then_inc(O_drained, 1)

            def quantise(b, p):
                xt = [x1[p][:, q, :] for q in range(QT)]
                dve.wait_ge(O_drained, 2 * b + 2)
                for q in range(QT):
                    m = order.mark(nc.vector.bn_stats(statsB[:, q, :], xt[q]))
                dve.wait_ge(dve_order, m)
                nc.vector.memset(dve_slot[:, :], 0.0)
                for q in range(QT):
                    last = nc.vector.bn_aggr(mvB[:, q, :], statsB[:, q, :])
                last.then_inc(statsB_ready, 1)
                dve.wait_ge(statsB_ready, b + 1)
                dve.wait_ge(rstdB_ready, b + 1)
                for q in range(QT):
                    m = order.mark(nc.vector.tensor_scalar(xnB[:, q, :], xt[q], mvB[:, q, 0:1], rstdB[:, q:q + 1],
                                                           ALU.subtract, ALU.mult))
                dve.wait_ge(dve_order, m)
                order.link(nc.vector.tensor_reduce(amax[:, :], xnB[:, :, :], AX.X, ALU.max, apply_absolute_value=True))
                order.link(nc.vector.tensor_scalar(amax[:, :], amax[:, :], 1e-5, None, ALU.max))
                order.link(nc.vector.reciprocal(qscale[:, :], amax[:, :]))
                order.link(nc.vector.tensor_scalar(qscale[:, :], qscale[:, :], 127.0, None, ALU.mult))
                order.mark(nc.vector.tensor_scalar(dscale[:, :], amax[:, :], ws_col[:, :], 1.0 / 127.0, ALU.mult, ALU.mult))
                for q in range(QT):
                    m = order.mark(nc.vector.tensor_scalar(xnB[:, q, :], xnB[:, q, :], qscale[:, q:q + 1], MAGIC, ALU.mult, ALU.add))
                dve.wait_ge(dve_order, m)
                order.link(nc.vector.tensor_scalar(xnB[:, :, :], xnB[:, :, :], MAGIC - 128.0, MAGIC + 127.0, ALU.max, ALU.min))
                nc.vector.tensor_scalar(xq[:, :, :], xnB[:, :, :], -MAGIC, None, ALU.add).then_inc(xq_ready, 1)

            def drain_xq(b):
                dve.wait_ge(xqT_filled, b + 1)
                nc.vector.tensor_copy(xqT[:, :], Mb[:, 0:S]).then_inc(xqT_ready, 1)

            def linear(b, p):
                dve.wait_ge(y_filled, b + 1)
                for q in range(QT):
                    m = order.mark(nc.vector.scalar_tensor_tensor(yB[:, q, :], M_ps[:, S + 128 * q:S + 128 * q + 128],
                                                                  dscale[:, q:q + 1], fb_row[:, :], ALU.mult, ALU.add))
                dve.wait_ge(dve_order, m)
                xt = x_sb[:, ds(2 * b, 2), :]
                nc.vector.scalar_tensor_tensor(xt, yB[:, :, :], gates[:, 2:3], x1[p][:, :, :], ALU.mult, ALU.add).then_inc(x2_ready, 1)

            def body(b, p, first):
                normalise(b, p)
                prep(b, p, first)
                maximum(b, 0)
                if not first:
                    drain_probs(b, 2, first)
                    attend(b - 1, 1, 1 - p)
                    quantise(b - 1, 1 - p)
                maximum(b, 1)
                if not first:
                    drain_xq(b - 1)
                drain_probs(b, 2 if first else 4, first)
                attend(b, 0, p)
                if not first:
                    linear(b - 1, 1 - p)

            dve.wait_ge(gates_ready, 1)
            dve.wait_ge(rstd_ready, 1)
            body(0, 0, True)
            dve.wait_ge(rstd_ready, 2)
            body(1, 1, False)
            for i in order.loop(1, B // 2, 36):
                for p in range(2):
                    body(2 * i + p, p, False)
            drain_probs(B, 0, False)
            attend(B - 1, 1, 1)
            quantise(B - 1, 1)
            drain_xq(B - 1)
            linear(B - 1, 1)

            dve.wait_ge(mask_loaded, 32)
            words = maskA.rearrange("p t k -> p (t k)").bitcast(i32)
            n = NT * (T0 - 1) // 4
            while n > 300:
                n //= 2
                order.link(nc.vector.tensor_tensor(words[:, 0:n], words[:, 0:n], words[:, n:2 * n], ALU.bitwise_and))
            order.link(nc.vector.tensor_reduce(maskpair[:, :], words[:, 0:n].bitcast(mybir.dt.uint16), AX.X, ALU.min))
            dve.wait_ge(consts2_ready, 9)
            order.link(nc.vector.tensor_scalar(bad[:, 0:1], maskpair[:, :], 257.0, None, ALU.is_lt))
            order.link(nc.vector.tensor_reduce(maskmin[:, :], maskB[:, :, 0:1].rearrange("p t k -> p (t k)"), AX.X, ALU.min))
            order.mark(nc.vector.tensor_scalar(bad[:, 1:2], maskmin[:, :], 1.0, None, ALU.is_lt))
            dve.wait_ge(cnt_filled, 1)
            order.link(nc.vector.tensor_copy(cnt[:, :], M_ps[0:B, 0:TAIL]))
            nc.vector.tensor_scalar(maskrow[:, :], cnt[:, :], NEG / S, None, ALU.mult).then_inc(maskrow_ready, 1)
            order.link(nc.vector.scalar_tensor_tensor(cntv[:, :], cnt[:, :], float(S), cnt[:, :], ALU.subtract, ALU.mult))
            order.link(nc.vector.tensor_reduce(cmin[:, 0:1], cntv[:, :], AX.X, ALU.min))
            order.link(nc.vector.tensor_reduce(cmin[:, 1:2], cnt[:, :], AX.X, ALU.min))
            nc.vector.tensor_tensor(bad[0:B, 2:3], cmin[:, 1:2], cmin[:, 0:1], ALU.subtract).then_inc(bad_ready, 1)
            dve.wait_ge(bad_filled, 1)
            order.link(nc.vector.tensor_reduce(badsum[:, :], M_ps[0:1, 0:3], AX.X, ALU.add))
            nc.vector.tensor_scalar(flag[:, :], badsum[:, :], 0.0, None, ALU.is_gt).then_inc(flag_ready, 1)

            dve.wait_ge(flag_ready, 1)
            general = dve.value_load(flag[0:1, 0:1])
            with dve.If(general > 0):
                slow = Tally(dve, dve_gen)
                for b in slow.loop(0, B, 2):
                    xt = [x_sb[:, ds(2 * b + q, 1), :].rearrange("p a d -> p (a d)") for q in range(QT)]
                    for q in range(QT):
                        m = slow.mark(nc.vector.bn_stats(statsB[:, q, :], xt[q]))
                    dve.wait_ge(dve_gen, m)
                    nc.vector.memset(dve_slot[:, :], 0.0)
                    for q in range(QT):
                        last = nc.vector.bn_aggr(mvB[:, q, :], statsB[:, q, :])
                    last.then_inc(g_stats, 1)
                    dve.wait_ge(g_stats, b + 1)
                    dve.wait_ge(g_rstd, b + 1)
                    for q in range(QT):
                        nc.vector.tensor_scalar(xnG[:, q, :], xt[q], mvB[:, q, 0:1], rstdB[:, q:q + 1],
                                                ALU.subtract, ALU.mult).then_inc(g_xn, 1)
                    dve.wait_ge(g_xT_filled, b + 1)
                    nc.vector.tensor_copy(xnGT, M_ps[:, 0:S]).then_inc(g_xT_ready, 1)
                    dve.wait_ge(g_q_filled, b + 1)
                    nc.vector.tensor_scalar(qG, M_ps[:, 0:S], bq_col[:, :], DH ** -0.5, ALU.add, ALU.mult).then_inc(g_q_ready, 1)
                    dve.wait_ge(g_k_filled, b + 1)
                    nc.vector.tensor_scalar(prob[0], S_ps, bk_col[:, :], None, ALU.add).then_inc(g_k_ready, 1)
                    dve.wait_ge(g_v_filled, b + 1)
                    for t in range(KT):
                        rows = 128 if t < KT - 1 else KR
                        last = nc.vector.tensor_tensor(ctxN[0][0:rows, t, :], PS[0:rows, 128 * t:128 * t + 128], bv_row[0:rows, :], ALU.add)
                    last.then_inc(g_v_ready, 1)
                with dve.Fori(0, B) as b:
                    for q in range(QT):
                        dve.wait_ge(g_mask_loaded, 32 * b + (16 * q + 16))
                        nc.vector.tensor_copy(maskQF, maskQ).then_inc(g_mask_ready, 1)
                        with dve.Fori(0, H) as h:
                            u = 2 * H * b + h + H * q
                            dve.wait_ge(g_S_filled, u + 1)
                            nc.vector.tensor_reduce(gmax, S_ps, AX.X, ALU.max, negate=True).then_inc(g_max, 1)
                            dve.wait_ge(g_exp, u + 1)
                            nc.vector.reciprocal(grecip, gsum).then_inc(g_S_free, 1)
                            dve.wait_ge(g_S_free, u + 1)
                            dve.wait_ge(g_O_filled, u + 1)
                            nc.vector.tensor_scalar(attn[:, ds(2 * b + q, 1), ds(DH * h, DH)].rearrange("p a d -> p (a d)"), O_ps[:, 0:DH], grecip,
                                                    None, ALU.mult).then_inc(g_free, 1)
                dve.wait_ge(g_free, NT * H + 1)
                nc.vector.memset(dve_slot[:, :], 0.0).then_inc(attn_ready, NT)
            with dve.Else():
                fast = Tally(dve, dve_fast)

                def project(n, p):
                    xt = [x_sb[:, ds(2 * n + q, 1), :].rearrange("p a d -> p (a d)") for q in range(QT)]
                    nc.vector.memset(dve_slot[:, :], 0.0)
                    for q in range(QT):
                        m = fast.mark(nc.vector.bn_stats(statsB[:, q, :], xt[q]))
                    dve.wait_ge(dve_fast, m)
                    nc.vector.memset(dve_slot[:, :], 0.0)
                    for q in range(QT):
                        last = nc.vector.bn_aggr(mvB[:, q, :], statsB[:, q, :])
                    last.then_inc(lnC_stats, 1)
                    dve.wait_ge(lnC_stats, n + 1)
                    dve.wait_ge(rstdC_ready, n + 1)
                    for q in range(QT):
                        nc.vector.tensor_scalar(xnC[:, q, :], xt[q], mvB[:, q, 0:1], rstdB[:, q:q + 1],
                                                ALU.subtract, ALU.mult).then_inc(xnC_ready, 1)
                    dve.wait_ge(xnCT_filled, n + 1)
                    nc.vector.tensor_copy(xnCT, M_ps[:, 0:S]).then_inc(xnCT_ready, 1)
                    dve.wait_ge(q_filled, n + 1)
                    if not (isinstance(n, int) and n == 0):
                        dve.wait_ge(parts_ready, n)
                    nc.vector.tensor_scalar(qf, M_ps[:, 0:S], bq_col[:, :], DH ** -0.5, ALU.add, ALU.mult).then_inc(q_ready, 1)
                    dve.wait_ge(k_filled, n + 1)
                    nc.vector.tensor_scalar(kf, M_ps[:, 0:TAIL], bk_col[:, :], None, ALU.add).then_inc(k_ready, 1)
                    dve.wait_ge(v_filled, n + 1)
                    for t in range(4):
                        last = nc.vector.tensor_tensor(vaug[p][:, t, :, 0:DH], M_ps[0:TP, 128 * t:128 * t + 128].rearrange("p (h d) -> p h d", d=DH),
                                                       bv_row[0:TP, :].rearrange("p (h d) -> p h d", d=DH), ALU.add)
                    last.then_inc(v_ready, 1)

                def maxima(n, p):
                    for u in range(QT * H):
                        dve.wait_ge(S1_filled, 32 * n + (u + 1))
                        nc.vector.tensor_reduce(nm[:, u:u + 1], S1[u % 2], AX.X, ALU.max, negate=True).then_inc(S1_max, 1)
                    dve.wait_ge(nmT_filled, n + 1)
                    src = M_ps[0:H, 0:S]
                    fast.link(nc.vector.tensor_copy(nmpart[p][:, 0, :], src))
                    fast.link(nc.vector.tensor_tensor(nmres, src, nmpart[p][:, 0, :], ALU.subtract))
                    fast.link(nc.vector.tensor_copy(nmpart[p][:, 1, :], nmres))
                    nc.vector.tensor_tensor(nmpart[p][:, 2, :], nmres, nmpart[p][:, 1, :], ALU.subtract).then_inc(nm_ready, 1)

                def normalise_heads(b):
                    for q in range(QT):
                        dve.wait_ge(back_filled, 2 * b + (q + 1))
                        o = M_ps.rearrange("p (h e) -> p h e", e=32)
                        fast.link(nc.vector.reciprocal(rden, o[:, :, DH]))
                        dst = attn[:, ds(2 * b + q, 1), :].rearrange("p a (h d) -> p (a h) d", d=DH)
                        nc.vector.tensor_tensor(dst, o[:, :, 0:DH], rden.unsqueeze(2).to_broadcast([128, H, DH]),
                                                ALU.mult).then_inc(attn_ready, 1)

                def body(b, p, last=False):
                    if not last:
                        project(b + 1, 1 - p)
                        maxima(b + 1, 1 - p)
                    normalise_heads(b)

                project(0, 0)
                maxima(0, 0)
                body(0, 0)
                body(1, 1)
                for i in fast.loop(1, B // 2 - 1, 14):
                    for p in range(2):
                        body(2 * i + p, p)
                body(B - 2, 0)
                body(B - 1, 1, True)

            late = Tally(dve, dve_late)
            dve.wait_ge(attn_ready, NT)

            def drain_logits(b, p):
                dve.wait_ge(lg_filled, b + 1)
                nc.vector.tensor_copy(logits[:, ds(QT * b, QT), :], bank[6 + p][:, 0:QT * E].rearrange("p (t e) -> p t e", e=E)).then_inc(lg_ready, 1)

            def out_projection(b, p, first):
                xt = [x_sb[:, ds(2 * b + q, 1), :].rearrange("p a d -> p (a d)") for q in range(QT)]
                dve.wait_ge(wo_filled, b + 1)
                for q in range(QT):
                    m = late.mark(nc.vector.tensor_tensor(x3t[:, q, :], bank[2 + p][:, 128 * q:128 * q + 128], bo_row[:, :], ALU.add))
                dve.wait_ge(dve_late, m)
                x2t = x_sb[:, ds(2 * b, 2), :]
                nc.vector.scalar_tensor_tensor(x2t, x3t, gates[:, 1:2], x2t, ALU.mult, ALU.add).then_inc(x3_read, 1)
                dve.wait_ge(x3_read, b + 1)
                nc.vector.memset(dve_slot[:, :], 0.0)
                for q in range(QT):
                    m = late.mark(nc.vector.bn_stats(statsB[:, q, :], xt[q]))
                dve.wait_ge(dve_late, m)
                nc.vector.memset(dve_slot[:, :], 0.0)
                for q in range(QT):
                    last = nc.vector.bn_aggr(mvB[:, q, :], statsB[:, q, :])
                last.then_inc(x3_stats, 1)
                dve.wait_ge(x3_stats, b + 1)
                dve.wait_ge(x3_rstd, b + 1)
                if not isinstance(b, int) or b >= 2:
                    dve.wait_ge(xn3_saved, b - 1)
                for q in range(QT):
                    nc.vector.tensor_scalar(xn3[p][:, q, :], xt[q], mvB[:, q, 0:1], rstdB[:, q:q + 1],
                                            ALU.subtract, ALU.mult).then_inc(xn3_ready, 1)
                if not first:
                    drain_logits(b - 1, 1 - p)

            out_projection(0, 0, True)
            out_projection(1, 1, False)
            for i in late.loop(1, B // 2, 8):
                for p in range(2):
                    out_projection(2 * i + p, p, False)
            drain_logits(B - 1, 1)
            dve.wait_ge(lg_ready, B)
            dve.wait_ge(gconst_ready, 4)

            def wide(v):
                return v.unsqueeze(2).to_broadcast([128, NT, E])

            def link(ins):
                late.link(ins)

            def first_of(values, best, least, onehot):
                link(nc.vector.tensor_tensor(equal, values, wide(best), ALU.is_equal))
                link(nc.vector.scalar_tensor_tensor(cand, equal, -float(E), iota_e, ALU.mult, ALU.add))
                link(nc.vector.tensor_reduce(least, cand, AX.X, ALU.min))
                link(nc.vector.tensor_tensor(onehot, cand, wide(least), ALU.is_equal))

            link(nc.vector.tensor_reduce(gmx, logits, AX.X, ALU.max))
            nc.vector.tensor_tensor(shifted, logits, wide(gmx), ALU.subtract).then_inc(shifted_ready, 1)
            dve.wait_ge(expd_ready, 1)
            link(nc.vector.tensor_reduce(gmx, expd, AX.X, ALU.add))
            link(nc.vector.reciprocal(gmx, gmx))
            link(nc.vector.tensor_tensor(raw, expd, wide(gmx), ALU.mult))
            link(nc.vector.tensor_reduce(gate1, raw, AX.X, ALU.max))
            first_of(raw, gate1, least1, m1)
            link(nc.vector.tensor_tensor(work, raw, m1, ALU.mult))
            link(nc.vector.tensor_tensor(rest, raw, work, ALU.subtract))
            link(nc.vector.tensor_reduce(gate2, rest, AX.X, ALU.max))
            first_of(rest, gate2, least2, m2)
            half_ = NT * E
            link(nc.vector.tensor_copy(m12[:, 0:half_], m1.rearrange("p t e -> p (t e)")))
            nc.vector.tensor_copy(m12[:, half_:2 * half_], m2.rearrange("p t e -> p (t e)")).then_inc(m12_ready, 1)
            dve.wait_ge(cum_filled, 1)
            link(nc.vector.tensor_copy(pos1, bank[0][:, 0:half_].rearrange("p (t e) -> p t e", e=E)))
            link(nc.vector.tensor_scalar(count1, bank[1][:, 0:B * E].rearrange("p (b e) -> p b e", e=E), float(CAP), None, ALU.min))
            behind = bank[0][:, half_:2 * half_].rearrange("p (b t e) -> p b t e", t=QT, e=E)
            pos2v = pos2.rearrange("p (b t) e -> p b t e", t=QT)
            for t in range(QT):
                link(nc.vector.tensor_tensor(pos2v[:, :, t, :], behind[:, :, t, :], count1, ALU.add))
            for onehot, pos, least, keep, place, slot in ((m1, pos1, least1, keep1, place1, slot1),
                                                          (m2, pos2, least2, keep2, place2, slot2)):
                link(nc.vector.scalar_tensor_tensor(kept, pos, float(CAP), onehot, ALU.is_lt, ALU.mult))
                link(nc.vector.tensor_reduce(keep, kept, AX.X, ALU.add))
                link(nc.vector.tensor_tensor(work, pos, onehot, ALU.mult))
                link(nc.vector.tensor_reduce(place, work, AX.X, ALU.add))
                link(nc.vector.scalar_tensor_tensor(place, least, float(CAP), place, ALU.mult, ALU.add))
                link(nc.vector.scalar_tensor_tensor(slot, place, float(E * CAP + 1), keep, ALU.add, ALU.mult))
                link(nc.vector.tensor_scalar(slot, slot, -1.0, None, ALU.add))

            def combine(b, p, again):
                if again:
                    dve.wait_ge(cB_filled, b - 1)
                for q in range(QT):
                    u = 2 * b + q
                    late.mark(nc.vector.tensor_scalar(comb[p][:, q, :], iota_slot, slot1[:, ds(u, 1)], gate1[:, ds(u, 1)], ALU.is_equal, ALU.mult))
                    m = late.mark(nc.vector.tensor_scalar(comb2[:, q, :], iota_slot, slot2[:, ds(u, 1)], gate2[:, ds(u, 1)], ALU.is_equal, ALU.mult))
                dve.wait_ge(dve_late, m)
                link(nc.vector.tensor_tensor(comb[p], comb[p], comb2, ALU.add))
                nc.vector.tensor_scalar(disp[p], comb[p], 0.0, None, ALU.not_equal).then_inc(comb_ready, 1)
                dve.wait_ge(cB_filled, b + 1)
                nc.vector.tensor_copy(combT[:, ds(b, 1), 512:1024].rearrange("p a n -> p (a n)"), bank[3 + 2 * p]).then_inc(cB_drained, 1)

            combine(0, 0, False)
            combine(1, 1, False)
            for i in late.loop(1, B // 2, 10):
                for p in range(2):
                    combine(2 * i + p, p, True)

            def hidden(e, first):
                for c in range(HC):
                    rows = HROWS[c]
                    dve.wait_ge(b_filled, HC * e + (c + 1))
                    dve.wait_ge(gelu_done, HC * e + (c + 1))
                    if c == 1 and not first:
                        dve.wait_ge(eo_filled, e)
                    if c >= 2 or (c == 0 and not first):
                        dve.wait_ge(hid_used, (HC - 1) * e + max(c - 1, 0))
                    nc.vector.tensor_tensor(hid[c % 2][0:rows, :], bank[2 + c % 2][0:rows, :], gl[c % 2][0:rows, :], ALU.mult).then_inc(hid_ready, 1)

            hidden(0, True)
            with dve.Fori(1, E) as e:
                hidden(e, False)

            def residual(g, p):
                dve.wait_ge(y_back_filled, g + 1)
                xt = x_sb[:, ds(2 * g, 2), :]
                nc.vector.scalar_tensor_tensor(xt, bank[4 + p][:, 0:S].rearrange("p (t d) -> p t d", d=D), gates[:, 3:4], xt,
                                               ALU.mult, ALU.add).then_inc(x4_ready, 1)

            def slots(g, p, first):
                dve.wait_ge(eoX_filled, g + 1)
                nc.vector.tensor_copy(eo[p], bank[p].rearrange("p (t d) -> p t d", d=D)).then_inc(eo_ready, 1)
                if not first:
                    residual(g - 1, 1 - p)

            slots(0, 0, True)
            slots(1, 1, False)
            with dve.Fori(1, B // 2) as i:
                for p in range(2):
                    slots(2 * i + p, p, False)
            residual(B - 1, 1)

        @block.tensor
        def _(pe):
            def prep(b, p, first):
                pe.wait_ge(xn_ready, 2 * b + 2)
                if not isinstance(b, int) or b >= 2:
                    pe.wait_ge(x2_ready, b - 1)
                for q in range(QT):
                    last = nc.tensor.transpose(M_ps[:, 128 * q:128 * q + 128], xn[p][:, q, :], ident[:, :])
                last.then_inc(xnT_filled, 1)
                if first:
                    pe.wait_ge(tern_ready, 1)
                    nc.tensor.transpose(TB.bitcast(bf16)[:, 0:128], tern[:, :], identb[:, :]).then_inc(ternT_filled, 1)
                pe.wait_ge(ctx_loaded[p], 32 * (b // 2 + 1) if isinstance(b, int) else 16 * b + (32 - 16 * p))
                for c in range(4):
                    bk_, filled, drained = ((TA, TA_filled, TA_drained), (TB, TB_filled, TB_drained))[c % 2]
                    if not first or c >= 2:
                        pe.wait_ge(drained, fills(b, c // 2, first))
                    if first and c == 1:
                        pe.wait_ge(ternT_ready, 1)
                    for n, t in enumerate(range(*TCH[c])):
                        rows = 128 if t < KT - 1 else KR
                        last = nc.tensor.transpose(bk_[:, 128 * n:128 * n + rows], ctxN[p][0:rows, t, :], ident[0:rows, 0:rows])
                    last.then_inc(filled, 1)
                    if c == 1:
                        pe.wait_ge(xnT_ready, b + 1)
                        nc.tensor.matmul(M_ps[:, S:2 * S], w0_sb[:, :], xnT[p][:, :], start=True, stop=True).then_inc(proj_filled, 1)

            def scores(b, q, p, first):
                u = 2 * b + q
                if q == 0:
                    pe.wait_ge(projT_ready, b + 1)
                    pe.wait_ge(TA_drained, fills(b, 2, first))
                    pe.wait_ge(TB_drained, fills(b, 2, first))
                if not (first and q == 0):
                    pe.wait_ge(exp_done, u)
                for lo in range(0, K, 512):
                    hi = min(lo + 512, K)
                    last = nc.tensor.matmul(S_ps[:, lo:hi], projT[p][:, 128 * q:128 * q + 128], ctxT[p][:, lo:hi],
                                            start=True, stop=True)
                last.then_inc(S_filled, 1)

            def attend(b, q, p, bb, k0, first):
                u = 2 * b + q
                banks = ((TA, TA_filled, TA_drained), (TB, TB_filled, TB_drained))

                def transposes(c):
                    bk_, filled, drained = banks[c % 2]
                    pe.wait_ge(drained, fills(bb, k0 + c // 2, first))
                    for n, t in enumerate(range(*TCH[c])):
                        rows = 128 if t < KT - 1 else KR
                        last = nc.tensor.transpose(bk_[0:rows, 128 * n:128 * n + 128], prob[q][:, 128 * t:128 * t + rows], ident[:, :])
                    last.then_inc(filled, 1)

                def product(c):
                    pe.wait_ge(banks[c % 2][2], fills(bb, k0 + c // 2 + 1, first))
                    for t in range(*TCH[c]):
                        rows = 128 if t < KT - 1 else KR
                        last = nc.tensor.matmul(O_ps[:, 0:D], probT[0:rows, t, :], ctxN[p][0:rows, t, :], start=t == 0, stop=t == KT - 1)
                    return last

                pe.wait_ge(exp_done, u + 1)
                transposes(0)
                transposes(1)
                if not (isinstance(b, int) and b == 0 and q == 0):
                    pe.wait_ge(O_drained, u)
                product(0)
                transposes(2)
                product(1)
                transposes(3)
                product(2).then_inc(prob_used, 1)
                product(3).then_inc(O_filled, 1)

            def quantised_T(b):
                pe.wait_ge(xq_ready, b + 1)
                pe.wait_ge(projT_ready, b + 1)
                for q in range(QT):
                    last = nc.tensor.transpose(Mb[:, 128 * q:128 * q + 128], xq[:, q, :], identb[:, :])
                last.then_inc(xqT_filled, 1)

            def linear(b):
                pe.wait_ge(xqT_ready, b + 1)
                for q in range(QT):
                    last = nc.tensor.matmul(M_ps[:, S + 128 * q:S + 128 * q + 128], xqT[:, 128 * q:128 * q + 128], ternT[:, :],
                                            start=True, stop=True)
                last.then_inc(y_filled, 1)

            def body(b, p, first):
                prep(b, p, first)
                scores(b, 0, p, first)
                if not first:
                    attend(b - 1, 1, 1 - p, b, 2, first)
                scores(b, 1, p, first)
                if not first:
                    quantised_T(b - 1)
                attend(b, 0, p, b, 2 if first else 4, first)
                if not first:
                    linear(b - 1)

            pe.wait_ge(ident_ready, 2)
            pe.wait_ge(w_loaded, 16 * 15)
            body(0, 0, True)
            body(1, 1, False)
            with pe.Fori(1, B // 2) as i:
                for p in range(2):
                    body(2 * i + p, p, False)
            attend(B - 1, 1, 1, B, 0, False)
            quantised_T(B - 1)
            linear(B - 1)

            pe.wait_ge(x2_ready, B)
            pe.wait_ge(consts2_ready, 9)
            pe.wait_ge(maskF_ready, 1)
            for t in range(NT):
                last = nc.tensor.matmul(M_ps[0:B, 0:TAIL], sel15[:, B - 1 - t // QT:2 * B - 1 - t // QT], maskF[:, t, :],
                                        start=t == 0, stop=t == NT - 1)
            last.then_inc(cnt_filled, 1)
            pe.wait_ge(bad_ready, 1)
            nc.tensor.matmul(M_ps[0:1, 0:3], ones_col[:, :], bad[:, :], start=True, stop=True).then_inc(bad_filled, 1)

            pe.wait_ge(flag_ready, 1)
            general = pe.value_load(flag[0:1, 0:1])
            with pe.If(general > 0):
                pe.wait_ge(g_neg, 1)
                with pe.Fori(0, B) as b:
                    pe.wait_ge(g_loaded, 32 * b + 32)
                    for c in range(4):
                        pe.wait_ge(g_T_drained, 4 * b + (c - 1)) if c >= 2 else None
                        for n, t in enumerate(range(*TCH[c])):
                            rows = 128 if t < KT - 1 else KR
                            last = nc.tensor.transpose((TA, TB)[c % 2][:, 128 * n:128 * n + rows], ctxN[0][0:rows, t, :], ident[0:rows, 0:rows])
                        last.then_inc(g_T_filled, 1)
                    pe.wait_ge(g_xn, 2 * b + 2)
                    for q in range(QT):
                        last = nc.tensor.transpose(M_ps[:, 128 * q:128 * q + 128], xnG[:, q, :], ident[:, :])
                    last.then_inc(g_xT_filled, 1)
                    pe.wait_ge(g_xT_ready, b + 1)
                    nc.tensor.matmul(M_ps[:, 0:S], wq_sb[:, :], xnGT, start=True, stop=True).then_inc(g_q_filled, 1)
                    pe.wait_ge(g_T_drained, 4 * b + 4)
                    for lo in range(0, K, 512):
                        hi = min(lo + 512, K)
                        last = nc.tensor.matmul(S_ps[:, lo:hi], wk_sb[:, :], ctxT[0][:, lo:hi], start=True, stop=True)
                    last.then_inc(g_k_filled, 1)
                    pe.wait_ge(g_k_ready, b + 1)
                    for t in range(KT):
                        rows = 128 if t < KT - 1 else KR
                        last = nc.tensor.matmul(PS[0:rows, 128 * t:128 * t + 128], ctxT[0][:, 128 * t:128 * t + rows], wv_sb[:, :],
                                                start=True, stop=True)
                    last.then_inc(g_v_filled, 1)
                    pe.wait_ge(g_v_ready, b + 1)
                    pe.wait_ge(g_q_ready, b + 1)
                with pe.Fori(0, B) as b:
                    for q in range(QT):
                        with pe.Fori(0, H) as h:
                            u = 2 * H * b + h + H * q
                            pe.wait_ge(g_mask_ready, 2 * b + (q + 1))
                            pe.wait_ge(g_head_loaded, 64 * u + 64)
                            for lo in range(0, K, 512):
                                hi = min(lo + 512, K)
                                nc.tensor.matmul(S_ps[:, lo:hi], qhead, khead[:, lo:hi], start=True, stop=False)
                                last = nc.tensor.matmul(S_ps[:, lo:hi], negident, maskQF[:, lo:hi], start=False, stop=True)
                            last.then_inc(g_S_filled, 1)
                            pe.wait_ge(g_exp, u + 1)
                            for c in range(4):
                                if c >= 2:
                                    pe.wait_ge(g_T_drained, 4 * u + (4 * B + c - 1))
                                for n, t in enumerate(range(*TCH[c])):
                                    rows = 128 if t < KT - 1 else KR
                                    last = nc.tensor.transpose((TA, TB)[c % 2][0:rows, 128 * n:128 * n + 128],
                                                               prob[0][:, 128 * t:128 * t + rows], ident[:, :])
                                last.then_inc(g_T_filled, 1)
                            pe.wait_ge(g_T_drained, 4 * u + (4 * B + 4))
                            for t in range(KT):
                                rows = 128 if t < KT - 1 else KR
                                last = nc.tensor.matmul(O_ps[:, 0:DH], probT[0:rows, t, :], vhead[0:rows, t, :], start=t == 0, stop=t == KT - 1)
                            last.then_inc(g_O_filled, 1)
                            pe.wait_ge(g_free, u + 2)
            with pe.Else():
                def project(n, p, step):
                    if step == 0:
                        pe.wait_ge(xnC_ready, 2 * n + 2)
                        for q in range(QT):
                            last = nc.tensor.transpose(M_ps[:, 128 * q:128 * q + 128], xnC[:, q, :], ident[:, :])
                        last.then_inc(xnCT_filled, 1)
                    if step == 1:
                        pe.wait_ge(xnCT_ready, n + 1)
                        nc.tensor.matmul(M_ps[:, 0:S], wq_sb[:, :], xnCT, start=True, stop=True).then_inc(q_filled, 1)
                    if step == 2:
                        pe.wait_ge(q_ready, n + 1)
                        pe.wait_ge(keysS_ready, n + 1)
                        nc.tensor.matmul(M_ps[:, 0:TAIL], wk_sb[:, :], keysS[p], start=True, stop=True).then_inc(k_filled, 1)
                    if step == 3:
                        pe.wait_ge(k_ready, n + 1)
                        for t in range(4):
                            last = nc.tensor.matmul(M_ps[0:TP, 128 * t:128 * t + 128], keysS[p][:, TP * t:TP * t + TP], wv_sb[:, :],
                                                    start=True, stop=True)
                        last.then_inc(v_filled, 1)

                def scores(n, p, u, first):
                    if u == 0:
                        pe.wait_ge(aug_loaded[p], half(n, p, 208, 208))
                    if not (first and u < 2):
                        pe.wait_ge(S1_max, 32 * n + (u - 1))
                    q, h = u // H, u % H
                    nc.tensor.matmul(S1[u % 2], qaug[p][0:RM, h, 128 * q:128 * q + 128], kaug[p][0:RM, h, :],
                                     start=True, stop=True).then_inc(S1_filled, 1)

                def maxT(n):
                    pe.wait_ge(S1_max, 32 * n + 32)
                    pe.wait_ge(v_ready, n + 1)
                    for q in range(QT):
                        last = nc.tensor.transpose(M_ps[0:H, 128 * q:128 * q + 128], nm[:, H * q:H * q + H], ident[:, :])
                    last.then_inc(nmT_filled, 1)

                def scoresT(b, p, h, first):
                    if h == 0:
                        pe.wait_ge(nm_loaded[p], half(b, p, 16, 16))
                    if not (first and h < 2):
                        pe.wait_ge(P_ready, 16 * b + (h - 1))
                    for t in range(4):
                        last = nc.tensor.matmul(ST[h % 2][:, S * t:S * t + S], kaug[p][:, h, TP * t:TP * t + TP], qaug[p][:, h, :],
                                                start=True, stop=True)
                    last.then_inc(ST_filled, 1)

                def weigh(b, p, g, t, first):
                    if t == 0:
                        pe.wait_ge(P_ready, 16 * b + (4 * g + 4))
                        if not (first and g == 0):
                            pe.wait_ge(heads_ready, 4 * b + g)
                    for j in range(4):
                        h = 4 * g + j
                        last = nc.tensor.matmul(PV[32 * j:32 * j + 32, :], vaug[p][:, t, h, :], probs8[0:TP, h % 8, S * t:S * t + S],
                                                start=t == 0, stop=t == 3)
                    if t == 3:
                        last.then_inc(PV_filled, 1)

                def back(b, q, last_):
                    if q == 0:
                        pe.wait_ge(heads_ready, 4 * b + 4)
                        if last_:
                            pe.wait_ge(attn_ready, 2 * b)
                        else:
                            pe.wait_ge(nm_ready, b + 2)
                    else:
                        pe.wait_ge(attn_ready, 2 * b + 1)
                    for g in range(4):
                        last = nc.tensor.transpose(M_ps[:, 128 * g:128 * g + 128], headsT[:, g, 128 * q:128 * q + 128], ident[:, :])
                    last.then_inc(back_filled, 1)

                def body(b, p, first=False, last_=False):
                    n, pn = b + 1, 1 - p
                    for h in range(H):
                        scoresT(b, p, h, first)
                        if h >= 4:
                            weigh(b, p, h // 4 - 1, h % 4, first)
                        if not last_ and h < 4:
                            if h == 0 and not first:
                                pe.wait_ge(attn_ready, 2 * b)
                            if h == 0 and first:
                                pe.wait_ge(nm_ready, 1)
                            project(n, pn, h)
                        if not last_ and h >= 8:
                            for u in range(4 * (h - 8), 4 * (h - 8) + 4):
                                scores(n, pn, u, False)
                    weigh(b, p, 3, 0, first)
                    weigh(b, p, 3, 1, first)
                    if not last_:
                        maxT(n)
                    weigh(b, p, 3, 2, first)
                    weigh(b, p, 3, 3, first)
                    for q in range(QT):
                        back(b, q, last_)

                for step in range(4):
                    project(0, 0, step)
                for u in range(QT * H):
                    scores(0, 0, u, True)
                maxT(0)
                body(0, 0, first=True)
                body(1, 1)
                with pe.Fori(1, B // 2 - 1) as i:
                    for p in range(2):
                        body(2 * i + p, p)
                body(B - 2, 0)
                body(B - 1, 1, last_=True)
            pe.wait_ge(attn_ready, NT)

            def tokens_T(b, p):
                pe.wait_ge(xn3_ready, QT * b + QT)
                for q in range(QT):
                    last = nc.tensor.transpose(bank[4 + p][:, 128 * q:128 * q + 128], xn3[p][:, q, :], ident[:, :])
                last.then_inc(xn3T_filled, 1)

            def router_logits(b, p):
                pe.wait_ge(xn3T_ready, b + 1)
                if not isinstance(b, int) or b >= 2:
                    pe.wait_ge(lg_ready, b - 1)
                for q in range(QT):
                    last = nc.tensor.matmul(bank[6 + p][:, E * q:E * q + E], xn3T[p][:, 128 * q:128 * q + 128], router_sb[:, :],
                                            start=True, stop=True)
                last.then_inc(lg_filled, 1)

            def out_projection(b, p, first):
                pe.wait_ge(ao_ready, b + 1)
                for q in range(QT):
                    last = nc.tensor.transpose(bank[p][:, 128 * q:128 * q + 128], ao[p][:, q, :], ident[:, :])
                last.then_inc(aoT_filled, 1)
                if not first:
                    tokens_T(b - 1, 1 - p)
                pe.wait_ge(aoT_ready, b + 1)
                for q in range(QT):
                    last = nc.tensor.matmul(bank[2 + p][:, 128 * q:128 * q + 128], aoT[p][:, 128 * q:128 * q + 128], wo_sb[:, :],
                                            start=True, stop=True)
                last.then_inc(wo_filled, 1)
                if not first:
                    router_logits(b - 1, 1 - p)

            out_projection(0, 0, True)
            out_projection(1, 1, False)
            with pe.Fori(1, B // 2) as i:
                for p in range(2):
                    out_projection(2 * i + p, p, False)
            tokens_T(B - 1, 1)
            router_logits(B - 1, 1)

            pe.wait_ge(m12_ready, 1)
            pe.wait_ge(gconst_ready, 4)
            tiles = m12.rearrange("p (k t e) -> p k t e", t=QT, e=E)
            sums = bank[0][:, 0:2 * NT * E].rearrange("p (k t e) -> p k t e", t=QT, e=E)
            nc.tensor.matmul(bank[0][:, 0:2 * NT * E], upper, m12, start=True, stop=False)
            nc.tensor.matmul(sums[:, :, 1, :], allones, tiles[:, :, 0, :], start=False, stop=True)
            for t in range(QT):
                last = nc.tensor.matmul(bank[1][:, 0:B * E].rearrange("p (b e) -> p b e", e=E), allones, tiles[:, 0:B, t, :],
                                        start=t == 0, stop=t == QT - 1)
            last.then_inc(cum_filled, 1)

            def dispatch(b, p, again):
                pe.wait_ge(comb_ready, b + 1)
                pe.wait_ge(xs_ready, b + 1)
                if again:
                    pe.wait_ge(xT_drained, b - 1)
                for q in range(QT):
                    last = nc.tensor.matmul(bank[p], xs[p][:, q, :], disp[p][:, q, :], start=q == 0, stop=q == QT - 1)
                last.then_inc(xT_filled, 1)
                for half_bank, filled, drained in ((0, cA_filled, cA_drained), (1, cB_filled, cB_drained)):
                    if again:
                        pe.wait_ge(drained, b - 1)
                    for c in range(2):
                        for q in range(QT):
                            ch = 2 * half_bank + c
                            last = nc.tensor.transpose(bank[2 + 2 * p + half_bank][:, S * c + 128 * q:S * c + 128 * q + 128],
                                                       comb[p][:, q, 128 * ch:128 * ch + 128], ident[:, :])
                    last.then_inc(filled, 1)

            dispatch(0, 0, False)
            dispatch(1, 1, False)
            with pe.Fori(1, B // 2) as i:
                for p in range(2):
                    dispatch(2 * i + p, p, True)

            def down(e, c, p):
                rows = HROWS[c]
                pe.wait_ge(hid_ready, HC * e + (c + 1))
                if c == 0 and (not isinstance(e, int) or e >= 2):
                    pe.wait_ge(eoT_ready, e - 1)
                ins = nc.tensor.matmul(bank[4 + p], woe[p][0:rows, c, :], hid[c % 2][0:rows, :], start=c == 0, stop=c == HC - 1)
                ins.then_inc(eo_filled if c == HC - 1 else hid_used, 1)

            def expert(e, p, first):
                pe.wait_ge(wts_loaded[p], half(e, p, 64, 64))
                rhs = xT[:, ds(e, 1), :].rearrange("p a n -> p (a n)")
                for c in range(HC):
                    rows = HROWS[c]
                    if not (first and c < 2):
                        pe.wait_ge(gelu_done, HC * e + (c - 1))
                    nc.tensor.matmul(bank[c % 2][0:rows, :], w0e[p][:, HLO[c]:HLO[c] + rows], rhs, start=True, stop=True).then_inc(a_filled, 1)
                    if not (first and c < 2):
                        pe.wait_ge(hid_ready, HC * e + (c - 1))
                    nc.tensor.matmul(bank[2 + c % 2][0:rows, :], w1e[p][:, HLO[c]:HLO[c] + rows], rhs, start=True, stop=True).then_inc(b_filled, 1)
                    if c > 0:
                        down(e, c - 1, p)
                    elif not first:
                        down(e - 1, HC - 1, 1 - p)

            pe.wait_ge(xT_drained, B)
            pe.wait_ge(cA_drained, B)
            pe.wait_ge(cB_drained, B)
            expert(0, 0, True)
            expert(1, 1, False)
            with pe.Fori(1, E // 2) as i:
                for p in range(2):
                    expert(2 * i + p, p, False)
            down(E - 1, HC - 1, 1)

            def back_T(g, p):
                pe.wait_ge(outT_ready, g + 1)
                if not isinstance(g, int) or g >= 2:
                    pe.wait_ge(x4_ready, g - 1)
                for q in range(QT):
                    last = nc.tensor.transpose(bank[4 + p][:, 128 * q:128 * q + 128], outT[p][:, 128 * q:128 * q + 128], ident[:, :])
                last.then_inc(y_back_filled, 1)

            def combine(g, p, first):
                pe.wait_ge(eoS_ready, g + 1)
                if not isinstance(g, int) or g >= 2:
                    pe.wait_ge(eo_ready, g - 1)
                for ch in range(E * CAP // 128):
                    last = nc.tensor.transpose(bank[p][:, 128 * ch:128 * ch + 128],
                                               eoS[p][:, 2 * ch:2 * ch + 2, :].rearrange("p e c -> p (e c)"), ident[:, :])
                last.then_inc(eoX_filled, 1)
                if not first:
                    back_T(g - 1, 1 - p)
                pe.wait_ge(eo_ready, g + 1)
                for ch in range(E * CAP // 128):
                    last = nc.tensor.matmul(bank[2 + p][:, 0:S], eo[p][:, ch, :],
                                            combT[:, ds(g, 1), S * ch:S * ch + S].rearrange("p a n -> p (a n)"),
                                            start=ch == 0, stop=ch == E * CAP // 128 - 1)
                last.then_inc(outT_filled, 1)

            pe.wait_ge(eoT_ready, E)
            combine(0, 0, True)
            combine(1, 1, False)
            with pe.Fori(1, B // 2) as i:
                for p in range(2):
                    combine(2 * i + p, p, False)
            back_T(B - 1, 1)



_INS = ["x", "ctx_1024", "mask_Bx1xSxS2_bk1", "g_xattn", "g_ffn", "L0_xattn_W", "L0_xattn_b", "L0_ffn_packed_weight",
        "L0_ffn_weight_scale", "L0_ffn_bias", "L1_xattn_w_q", "L1_xattn_b_q", "L1_xattn_w_k", "L1_xattn_b_k",
        "L1_xattn_w_v", "L1_xattn_b_v", "L1_xattn_w_o", "L1_xattn_b_o", "L1_ffn_router_w", "L1_ffn_w0_kernel",
        "L1_ffn_w1_kernel", "L1_ffn_wo_kernel"]


def kernel(**inputs):
    import numpy as _np
    import concourse.bacc as _bacc
    from concourse import mybir as _mybir
    from concourse.bass_utils import run_bass_kernel_spmd as _run

    nc = _bacc.Bacc("TRN2", target_bir_lowering=False, num_devices=1)
    arrays, args = {}, []
    for name in _INS:
        a = _np.ascontiguousarray(inputs[name])
        arrays[f"in_{name}_dram"] = a
        args.append(nc.dram_tensor(f"in_{name}_dram", a.shape, _mybir.dt.from_np(a.dtype), kind="ExternalInput").ap())
    shape = _np.shape(inputs["x"])
    args.append(nc.dram_tensor("out_0_dram", shape, _mybir.dt.float32, kind="ExternalOutput").ap())
    build(nc, *args)
    r = _run(nc, [arrays], core_ids=[0])
    return r.results[0]["out_0_dram"]
```

```python
from contextlib import ExitStack

import concourse.bass as bass
from concourse import mybir


class Tally:

    def __init__(self, eng, sem):
        self.eng, self.sem, self.n, self.base = eng, sem, 0, 0

    def mark(self, ins):
        ins.then_inc(self.sem, 1)
        self.n += 1
        return self.base + self.n

    def link(self, ins):
        self.eng.wait_ge(self.sem, self.mark(ins))

    def loop(self, start, end, per):
        with self.eng.Fori(start, end) as i:
            n0 = self.n
            self.base = (i - start) * per if start else i * per
            yield i
            assert self.n - n0 == per, (self.n - n0, per)
            self.base = 0
            self.n = n0
        self.n = n0 + per * (end - start)


def build(nc, x, ctx_in, mask, g_xattn, g_ffn, w0, b0, packed, wscale, fbias,
          wq, bq, wk, bk, wv, bv, wo, bo, router, we0, we1, weo, out):
    fp32, bf16 = mybir.dt.float32, mybir.dt.bfloat16
    i32, u8 = mybir.dt.int32, mybir.dt.uint8
    ALU, ACT, AX = mybir.AluOpType, mybir.ActivationFunctionType, mybir.AxisListType
    ds = bass.ds

    B, S, D = x.shape
    K = ctx_in.shape[1]
    QT = S // 128
    NT = B * QT
    KT = -(-K // 128)
    KR = K - 128 * (KT - 1)
    H = 16
    DH = D // H
    TAIL = (K - 1) // 4
    T0 = K - TAIL
    TP = TAIL // 4
    E = router.shape[1]
    CAP = 64
    HID = we0.shape[2]
    HC = -(-HID // 128)
    HR = (HID - 128 * (HC - 2)) // 2
    HROWS = [128] * (HC - 2) + [HR] * 2
    HLO = [sum(HROWS[:c]) for c in range(HC)]
    EPS = 1e-5
    MAGIC = 1.5 * 2.0 ** 23
    NEG = -2.0 ** 100
    NPROD = 6
    KPART = (0, 0, 1, 1, 0, 2)
    QPART = (0, 1, 0, 1, 2, 0)
    RS = NPROD * DH
    RM = RS + 1
    RA = 128
    RN = RA - 3

    PER_STEP = (2, 2, 3, 3, 3, 2, 2, 3, 2, 3, 3, 3, 1, 0, 0, 0)
    UNITS = [range(sum(PER_STEP[:h]), sum(PER_STEP[:h + 1])) for h in range(H)]

    stack = ExitStack()
    with stack:
        def sb(name, shape, dt=fp32):
            return stack.enter_context(nc.sbuf_tensor(name, shape, dt))

        def sem(name):
            return stack.enter_context(nc.semaphore(name))

        ident = sb("ident", [128, 128])
        identb = sb("identb", [128, 128], bf16)
        w0_sb, wq_sb, wk_sb, wv_sb, wo_sb = (sb(n, [128, 128]) for n in ("w0_sb", "wq_sb", "wk_sb", "wv_sb", "wo_sb"))
        router_sb = sb("router_sb", [128, E])
        b0_col, bq_col, bk_col = (sb(n, [128, 1]) for n in ("b0_col", "bq_col", "bk_col"))
        fb_row, bv_row, bo_row = (sb(n, [128, 128]) for n in ("fb_row", "bv_row", "bo_row"))
        gates = sb("gates", [128, 4])
        gates_in = sb("gates_in", [128, 4])
        ws_col = sb("ws_col", [128, 1])
        packed_sb = sb("packed_sb", [128, 128], i32)
        tern_i = sb("tern_i", [128, 128], i32)
        tern = sb("tern", [128, 128], bf16)
        ternT = sb("ternT", [128, 128], bf16)
        neghalf = sb("neghalf", [128, NT])
        eps = sb("eps", [128, NT])
        zero = sb("zero", [128, 1])
        zero_col = zero[:, :]
        dve_slot = sb("dve_slot", [128, 1])

        x_sb = sb("x_sb", [128, NT, D])
        keysT = sb("keysT", [128, B, TAIL])
        stats = sb("stats", [128, NT, 6])
        meanvar = sb("meanvar", [128, NT, 2])
        vareps = sb("vareps", [128, NT])
        rstd = sb("rstd", [128, NT])

        class Carver:
            def __init__(self, handle):
                self.handle, self.at = handle, 0

            def take(self, shape, dt=fp32):
                n = 1
                for k in shape[1:]:
                    n *= k
                words = -(-n * (2 if dt == bf16 else 1 if dt == u8 else 4) // 4)
                v = self.handle[0:shape[0], self.at:self.at + words]
                self.at += words
                assert self.at <= self.handle.shape[1], self.at
                if dt != fp32:
                    v = v.bitcast(dt)[:, 0:n]
                if len(shape) == 3:
                    v = v.rearrange("p (a b) -> p a b", a=shape[1])
                if len(shape) == 4:
                    v = v.rearrange("p (a b c) -> p a b c", a=shape[1], b=shape[2])
                return v

        low, high = sb("low", [128, 14400]), sb("high", [128, 29000])

        one = Carver(low)
        ctxN, ctxT, prob = [None] * 2, [None] * 2, [None] * 2
        ctxN[1], ctxT[1], prob[1] = one.take([128, KT, D]), one.take([128, K]), one.take([128, K])
        ctxN[0], ctxT[0], prob[0] = one.take([128, KT, D]), one.take([128, K]), one.take([128, K])
        probT = one.take([128, KT, 128])
        xn = [one.take([128, QT, D]) for p in range(2)]
        xnT = [one.take([128, S]) for p in range(2)]
        projT = [one.take([128, S]) for p in range(2)]
        x1 = [one.take([128, QT, D]) for p in range(2)]
        xnB, yB = one.take([128, QT, D]), one.take([128, QT, D])
        xq, xqT = one.take([128, QT, D], bf16), one.take([128, S], bf16)
        nmax, rsum = sb("nmax", [128, NT]), sb("rsum", [128, NT])
        rgate = sb("rgate", [128, 2])
        statsB, mvB = sb("statsB", [128, QT, 6]), sb("mvB", [128, QT, 2])
        veB, rstdB = sb("veB", [128, QT]), sb("rstdB", [128, QT])
        amax, qscale, dscale = (sb(n, [128, QT]) for n in ("amax", "qscale", "dscale"))

        two = Carver(high)
        attn = two.take([128, NT, D])
        at_mask = two.at
        probs8 = two.take([128, 8, 4 * S])
        two.at = max(two.at, at_mask + (NT * (T0 - 1) + 3) // 4 + (NT * (TAIL + 1) + 3) // 4 + NT * TAIL // 2 + 8)
        kaug = [two.take([RA, H, TAIL], bf16) for p in range(2)]
        qaug = [two.take([RA, H, S], bf16) for p in range(2)]
        vaug = [two.take([TP, 4, H, 32]) for p in range(2)]
        two = Carver(low)
        two.at = KT * D + 2 * K
        headsT = two.take([128, 4, S])
        keysS = [two.take([128, TAIL]) for p in range(2)]
        xnC, xnCT = two.take([128, QT, D]), two.take([128, S])
        qf, kf = two.take([128, S]), two.take([128, TAIL])
        qres, kres = two.take([128, S]), two.take([128, TAIL])
        qpart = [two.take([128, 3, S], bf16) for p in range(2)]
        kpart = [two.take([128, 3, TAIL], bf16) for p in range(2)]
        nm = two.take([128, QT * H])
        nmres = two.take([H, S])
        nmpart = [two.take([H, 3, S], bf16) for p in range(2)]
        rden = two.take([128, H])
        chk = Carver(high)
        chk.at = at_mask
        maskA = chk.take([128, NT, T0 - 1], u8)
        maskB = chk.take([128, NT, TAIL + 1], u8)
        maskF = chk.take([128, NT, TAIL], bf16)
        maskpair, maskmin = sb("maskpair", [128, 1]), sb("maskmin", [128, 1])
        bad = sb("bad", [128, 3])
        sel15 = sb("sel15", [128, 2 * B - 1], bf16)
        cnt, cntv = sb("cnt", [B, TAIL]), sb("cntv", [B, TAIL])
        cmin = sb("cmin", [B, 2])
        maskrow = sb("maskrow", [B, TAIL], bf16)
        ones_col = sb("ones_col", [128, 1])
        badsum = sb("badsum", [1, 1])
        flag = sb("flag", [1, 1], i32)
        q_dram = [nc.dram_tensor(f"q_parts{p}", [3, D, S], bf16).ap() for p in range(2)]
        k_dram = [nc.dram_tensor(f"k_parts{p}", [3, D, TAIL], bf16).ap() for p in range(2)]
        maskrow_dram = nc.dram_tensor("mask_rows", [B, TAIL], bf16).ap()

        gen = Carver(high)
        gen.at = at_mask
        maskQ, maskQF = gen.take([128, K], u8), gen.take([128, K], bf16)
        khead, qhead, vhead = gen.take([DH, K]), gen.take([DH, 128]), gen.take([128, KT, DH])
        negident = gen.take([128, 128], bf16)
        xnG, xnGT, qG = gen.take([128, QT, D]), gen.take([128, S]), gen.take([128, S])
        grecip, gmax, gsum = gen.take([128, 1]), gen.take([128, 1]), gen.take([128, 1])
        q_all = nc.dram_tensor("q_all", [B, QT, D, 128], fp32).ap()
        k_all = nc.dram_tensor("k_all", [B, D, K], fp32).ap()
        v_all = nc.dram_tensor("v_all", [B, K, D], fp32).ap()

        wts = Carver(low)
        w0e, w1e, woe = [None] * 2, [None] * 2, [None] * 2
        for p in range(2):
            w0e[p], w1e[p], woe[p] = wts.take([128, HID]), wts.take([128, HID]), wts.take([128, HC, D])
        tri = Carver(low)
        tri.at = KT * D + 2 * K
        ao = [tri.take([128, QT, D]) for p in range(2)]
        aoT = [tri.take([128, S]) for p in range(2)]
        x3t = tri.take([128, QT, D])
        xn3 = [tri.take([128, QT, D]) for p in range(2)]
        xn3T = [tri.take([128, S]) for p in range(2)]
        eoT = tri.take([128, E, B * CAP])
        comb2 = tri.take([128, QT, E * CAP])
        fin = Carver(high)
        fin.at = at_mask
        combT = fin.take([128, B, E * CAP // 128 * S])
        xT = fin.take([128, E, B * CAP])
        xn_all = fin.take([128, NT, D])
        iota_slot = fin.take([128, E * CAP])
        comb = [fin.take([128, QT, E * CAP]) for p in range(2)]
        disp = [fin.take([128, QT, E * CAP]) for p in range(2)]
        xs = [fin.take([128, QT, D]) for p in range(2)]
        gl = [fin.take([128, B * CAP]) for p in range(2)]
        hid = [fin.take([128, B * CAP]) for p in range(2)]
        eoS = [fin.take([128, E, CAP]) for p in range(2)]
        eo = [fin.take([128, E * CAP // 128, 128]) for p in range(2)]
        outT = [fin.take([128, S]) for p in range(2)]
        iota_e, logits, shifted, expd, raw, equal, cand, m1, m2, rest, pos1, pos2, kept, work = (
            fin.take([128, NT, E]) for _ in range(14))
        m12 = fin.take([128, 2 * NT * E], bf16)
        count1 = fin.take([128, B, E])
        upper, allones = fin.take([128, 128], bf16), fin.take([128, 128], bf16)
        gmx, gate1, gate2, least1, least2, keep1, keep2, place1, place2, slot1, slot2 = (fin.take([128, NT]) for _ in range(11))

        PS = stack.enter_context(nc.psum_tensor("PS", [128, 4096], fp32))
        bank = [PS[:, 512 * i:512 * i + 512] for i in range(8)]
        S_ps, TA, TB, O_ps, M_ps = PS[:, 0:K], bank[4], bank[5], bank[6], bank[7]
        Mb = M_ps.bitcast(bf16)

        x_loaded, xrest_loaded, w_loaded, ternary_loaded = sem("x_loaded"), sem("xrest_loaded"), sem("w_loaded"), sem("ternary_loaded")
        ctx_loaded = [sem(f"ctx_loaded{p}") for p in range(2)]
        ident_ready, gates_ready = sem("ident_ready"), sem("gates_ready")
        tern_ready, ternT_filled, ternT_ready = sem("tern_ready"), sem("ternT_filled"), sem("ternT_ready")
        ln_stats, rstd_ready = sem("ln_stats"), sem("rstd_ready")
        xn_ready, xnT_filled, xnT_ready = sem("xn_ready"), sem("xnT_filled"), sem("xnT_ready")
        proj_filled, projT_ready = sem("proj_filled"), sem("projT_ready")
        TA_filled, TA_drained = sem("TA_filled"), sem("TA_drained")
        TB_filled, TB_drained = sem("TB_filled"), sem("TB_drained")
        keys_saved = sem("keys_saved")
        S_filled, max_done, exp_done, prob_used = sem("S_filled"), sem("max_done"), sem("exp_done"), sem("prob_used")
        O_filled, O_drained = sem("O_filled"), sem("O_drained")
        statsB_ready, rstdB_ready = sem("statsB_ready"), sem("rstdB_ready")
        xq_ready, xqT_filled, xqT_ready = sem("xq_ready"), sem("xqT_filled"), sem("xqT_ready")
        y_filled, x2_ready = sem("y_filled"), sem("x2_ready")
        out_stored = sem("out_stored")
        mask_loaded, mask_and, maskF_ready = sem("mask_loaded"), sem("mask_and"), sem("maskF_ready")
        consts2_ready = sem("consts2_ready")
        cnt_filled, bad_ready, bad_filled, flag_ready = sem("cnt_filled"), sem("bad_ready"), sem("bad_filled"), sem("flag_ready")
        maskrow_ready, maskrow_saved = sem("maskrow_ready"), sem("maskrow_saved")
        keysS_ready = sem("keysS_ready")
        lnC_stats, rstdC_ready, xnC_ready = sem("lnC_stats"), sem("rstdC_ready"), sem("xnC_ready")
        xnCT_filled, xnCT_ready = sem("xnCT_filled"), sem("xnCT_ready")
        q_filled, q_ready, k_filled, k_ready = sem("q_filled"), sem("q_ready"), sem("k_filled"), sem("k_ready")
        v_filled, v_ready, parts_ready = sem("v_filled"), sem("v_ready"), sem("parts_ready")
        parts_saved = [sem(f"parts_saved{p}") for p in range(2)]
        aug_loaded = [[sem(f"aug{c}_loaded{p}") for p in range(2)] for c in range(2)]
        S1_filled, S1_max = sem("S1_filled"), sem("S1_max")
        nmT_filled, nm_ready = sem("nmT_filled"), sem("nm_ready")
        nm_loaded = [sem(f"nm_loaded{p}") for p in range(2)]
        ST_filled, P_ready = sem("ST_filled"), sem("P_ready")
        PV_filled, heads_ready, back_filled, attn_ready = sem("PV_filled"), sem("heads_ready"), sem("back_filled"), sem("attn_ready")
        g_loaded, g_stats, g_rstd, g_xn = sem("g_loaded"), sem("g_stats"), sem("g_rstd"), sem("g_xn")
        g_T_filled, g_T_drained = sem("g_T_filled"), sem("g_T_drained")
        g_xT_filled, g_xT_ready = sem("g_xT_filled"), sem("g_xT_ready")
        g_q_filled, g_q_ready, g_k_filled, g_k_ready = sem("g_q_filled"), sem("g_q_ready"), sem("g_k_filled"), sem("g_k_ready")
        g_v_filled, g_v_ready, g_saved = sem("g_v_filled"), sem("g_v_ready"), sem("g_saved")
        g_neg, g_mask_loaded, g_mask_ready, g_head_loaded = sem("g_neg"), sem("g_mask_loaded"), sem("g_mask_ready"), sem("g_head_loaded")
        g_S_filled, g_max, g_exp, g_O_filled, g_free = sem("g_S_filled"), sem("g_max"), sem("g_exp"), sem("g_O_filled"), sem("g_free")
        g_S_free = sem("g_S_free")
        wts_loaded = [sem(f"wts_loaded{p}") for p in range(2)]
        ao_ready, aoT_filled, aoT_ready, wo_filled = sem("ao_ready"), sem("aoT_filled"), sem("aoT_ready"), sem("wo_filled")
        x3_read, x3_stats, x3_rstd, xn3_ready = sem("x3_read"), sem("x3_stats"), sem("x3_rstd"), sem("xn3_ready")
        xn3_saved, xn3T_filled, xn3T_ready = sem("xn3_saved"), sem("xn3T_filled"), sem("xn3T_ready")
        lg_filled, lg_ready, gconst_ready = sem("lg_filled"), sem("lg_ready"), sem("gconst_ready")
        shifted_ready, expd_ready, m12_ready, cum_filled = sem("shifted_ready"), sem("expd_ready"), sem("m12_ready"), sem("cum_filled")
        slots_ready, xs_ready, comb_ready = sem("slots_ready"), sem("xs_ready"), sem("comb_ready")
        xT_filled, xT_drained = sem("xT_filled"), sem("xT_drained")
        cA_filled, cA_drained, cB_filled, cB_drained = sem("cA_filled"), sem("cA_drained"), sem("cB_filled"), sem("cB_drained")
        a_filled, b_filled, gelu_done, hid_ready = sem("a_filled"), sem("b_filled"), sem("gelu_done"), sem("hid_ready")
        hid_used, eo_filled, eoT_ready = sem("hid_used"), sem("eo_filled"), sem("eoT_ready")
        eoS_ready, eoX_filled, eo_ready = sem("eoS_ready"), sem("eoX_filled"), sem("eo_ready")
        outT_filled, outT_ready, y_back_filled, x4_ready = sem("outT_filled"), sem("outT_ready"), sem("y_back_filled"), sem("x4_ready")
        dve_gen, dve_late, pool_late = sem("dve_gen"), sem("dve_late"), sem("pool_late")
        dve_fast, pool_fast = sem("dve_fast"), sem("pool_fast")
        dve_order, act_order, pool_order = sem("dve_order"), sem("act_order"), sem("pool_order")

        S1 = [bank[0][:, 0:TAIL], bank[1][:, 0:TAIL]]
        ST = [PS[0:TP, 1024 * (1 + j):1024 * (2 + j)] for j in range(2)]
        PV = bank[6][:, 0:S]

        TCH = [(0, 4), (4, 8), (8, 12), (12, KT)]

        def fills(b, k, first):
            return k if first else 6 * b + (k - 2)

        def half(n, p, per, more):
            return per * (n // 2) + more if isinstance(n, int) else (per // 2) * n + (more - per // 2 * p)

        block = stack.enter_context(nc.Block())

        @block.sync
        def _(sp):
            sp.dma_start(x_sb[:, 0:2, :], x.rearrange("b (t p) d -> p (b t) d", p=128)[:, 0:2, :]).then_inc(x_loaded, 16)

            def load_ctx(b, p):
                src = ctx_in[b, :, :] if isinstance(b, int) else ctx_in[ds(b, 1), :, :].rearrange("a k d -> (a k) d")
                sp.dma_start(ctxN[p][:, 0:KT - 1, :],
                             src[0:128 * (KT - 1), :].rearrange("(t p) d -> p t d", p=128)).then_inc(ctx_loaded[p], 16)
                sp.dma_start(ctxN[p][0:KR, KT - 1, :], src[128 * (KT - 1):K, :]).then_inc(ctx_loaded[p], 16)

            load_ctx(0, 0)
            sp.dma_start(x_sb[:, 2:NT, :], x.rearrange("b (t p) d -> p (b t) d", p=128)[:, 2:NT, :]).then_inc(xrest_loaded, 16)
            load_ctx(1, 1)
            with sp.Fori(1, B // 2) as i:
                for p in range(2):
                    sp.wait_ge(O_filled, 4 * i + (2 * p - 2))
                    load_ctx(2 * i + p, p)
            sp.wait_ge(maskrow_ready, 1)
            sp.dma_start(maskrow_dram, maskrow[:, :]).then_inc(maskrow_saved, 16)
            sp.wait_ge(maskrow_saved, 16)

            def save_parts(m, p):
                sp.wait_ge(parts_ready, m + 1)
                sp.dma_start(q_dram[p].rearrange("c r q -> r c q"), qpart[p]).then_inc(parts_saved[p], 16)
                sp.dma_start(k_dram[p].rearrange("c r q -> r c q"), kpart[p]).then_inc(parts_saved[p], 16)
                sp.wait_ge(parts_saved[p], half(m, p, 32, 32))

            def load_aug(m, p, c):
                heads, loaded = slice(8 * c, 8 * c + 8), aug_loaded[c][p]
                for g in range(NPROD):
                    sp.dma_start(qaug[p][DH * g:DH * g + DH, heads, :],
                                 q_dram[p][QPART[g], 64 * c:64 * c + 64, :].rearrange("(h d) q -> d h q", d=DH)).then_inc(loaded, 16)
                    sp.dma_start(kaug[p][DH * g:DH * g + DH, heads, :],
                                 k_dram[p][KPART[g], 64 * c:64 * c + 64, :].rearrange("(h d) q -> d h q", d=DH)).then_inc(loaded, 16)
                row = maskrow_dram[m:m + 1, :] if isinstance(m, int) else maskrow_dram[ds(m, 1), :]
                sp.dma_start(kaug[p][RS:RM, heads, :],
                             row.unsqueeze(1).to_broadcast([1, H // 2, TAIL])).then_inc(loaded, 16)

            def load_max(n, p):
                sp.wait_ge(nm_ready, n + 1)
                for c in range(3):
                    sp.dma_start(qaug[p][RN + c:RN + c + 1, :, :], nmpart[p][:, c, :]).then_inc(nm_loaded[p], 16)

            def serve(b, p, maxi, proj):
                if proj:
                    save_parts(b + 2, p)
                    if not isinstance(b, int) or b >= 0:
                        sp.wait_ge(ST_filled, 16 * b + 8)
                    load_aug(b + 2, p, 0)
                if maxi:
                    load_max(b + 1, 1 - p)
                if proj:
                    if not isinstance(b, int) or b >= 0:
                        sp.wait_ge(ST_filled, 16 * b + 16)
                    load_aug(b + 2, p, 1)

            sp.wait_ge(flag_ready, 1)
            general = sp.value_load(flag[0:1, 0:1])
            with sp.If(general > 0):
                def load_batch(b):
                    src = ctx_in[b, :, :] if isinstance(b, int) else ctx_in[ds(b, 1), :, :].rearrange("a k d -> (a k) d")
                    sp.dma_start(ctxN[0][:, 0:KT - 1, :],
                                 src[0:128 * (KT - 1), :].rearrange("(t p) d -> p t d", p=128)).then_inc(g_loaded, 16)
                    sp.dma_start(ctxN[0][0:KR, KT - 1, :], src[128 * (KT - 1):K, :]).then_inc(g_loaded, 16)

                def save_batch(b):
                    sp.wait_ge(g_q_ready, b + 1)
                    sp.dma_start(q_all[b:b + 1, :, :, :].rearrange("a q r s -> r (a q) s") if isinstance(b, int) else
                                 q_all[ds(b, 1), :, :, :].rearrange("a q r s -> r (a q) s"),
                                 qG.rearrange("r (q s) -> r q s", q=QT)).then_inc(g_saved, 16)
                    sp.wait_ge(g_k_ready, b + 1)
                    sp.dma_start(k_all[b, :, :] if isinstance(b, int) else k_all[ds(b, 1), :, :].rearrange("a r k -> (a r) k"),
                                 prob[0]).then_inc(g_saved, 16)
                    sp.wait_ge(g_v_ready, b + 1)
                    dst = v_all[b, :, :] if isinstance(b, int) else v_all[ds(b, 1), :, :].rearrange("a k d -> (a k) d")
                    sp.dma_start(dst[0:128 * (KT - 1), :].rearrange("(t p) d -> p t d", p=128),
                                 ctxN[0][:, 0:KT - 1, :]).then_inc(g_saved, 16)
                    sp.dma_start(dst[128 * (KT - 1):K, :], ctxN[0][0:KR, KT - 1, :]).then_inc(g_saved, 16)

                load_batch(0)
                with sp.Fori(1, B) as b:
                    save_batch(b - 1)
                    sp.wait_ge(g_saved, 64 * b)
                    load_batch(b)
                save_batch(B - 1)
                sp.wait_ge(g_saved, 64 * B)
                with sp.Fori(0, B) as b:
                    for q in range(QT):
                        with sp.Fori(0, H) as h:
                            sp.wait_ge(g_free, 2 * H * b + h + (H * q + 1))
                            sp.dma_start(qhead, q_all.rearrange("b q (h d) s -> (b q h) d s", d=DH)[ds(2 * H * b + h + H * q, 1), :, :]
                                         .rearrange("a d s -> (a d) s")).then_inc(g_head_loaded, 16)
                            sp.dma_start(khead, k_all.rearrange("b (h d) k -> (b h) d k", d=DH)[ds(H * b + h, 1), :, :]
                                         .rearrange("a d k -> (a d) k")).then_inc(g_head_loaded, 16)
                            vh = v_all[ds(b, 1), :, ds(DH * h, DH)].rearrange("a k d -> (a k) d")
                            sp.dma_start(vhead[:, 0:KT - 1, :],
                                         vh[0:128 * (KT - 1), :].rearrange("(t p) d -> p t d", p=128)).then_inc(g_head_loaded, 16)
                            sp.dma_start(vhead[0:KR, KT - 1, :], vh[128 * (KT - 1):K, :]).then_inc(g_head_loaded, 16)
            with sp.Else():
                serve(-2, 0, False, True)
                serve(-1, 1, True, True)
                serve(0, 0, True, True)
                serve(1, 1, True, True)
                with sp.Fori(1, B // 2 - 1) as i:
                    for p in range(2):
                        serve(2 * i + p, p, True, True)
                serve(B - 2, 0, True, False)

            def load_expert(e, p):
                def of(w):
                    return w[e, :, :] if isinstance(e, int) else w[ds(e, 1), :, :].rearrange("a m h -> (a m) h")
                sp.dma_start(w0e[p], of(we0)).then_inc(wts_loaded[p], 16)
                sp.dma_start(w1e[p], of(we1)).then_inc(wts_loaded[p], 16)
                sp.dma_start(woe[p][:, 0:HC - 2, :],
                             of(weo)[0:128 * (HC - 2), :].rearrange("(t p) d -> p t d", p=128)).then_inc(wts_loaded[p], 16)
                sp.dma_start(woe[p][0:HR, HC - 2:HC, :],
                             of(weo)[128 * (HC - 2):HID, :].rearrange("(t p) d -> p t d", p=HR)).then_inc(wts_loaded[p], 16)

            load_expert(0, 0)
            load_expert(1, 1)
            with sp.Fori(1, E // 2) as i:
                for p in range(2):
                    sp.wait_ge(eo_filled, 2 * i + (p - 1))
                    load_expert(2 * i + p, p)
            out_t = out.rearrange("b (t p) d -> p (b t) d", p=128)
            with sp.Fori(0, B) as b:
                sp.wait_ge(x4_ready, b + 1)
                sp.dma_start(out_t[:, ds(QT * b, QT), :], x_sb[:, ds(QT * b, QT), :]).then_inc(out_stored, 16)
            sp.wait_ge(out_stored, 16 * B)

        @block.gpsimd
        def _(pool):
            order = Tally(pool, pool_order)
            order.link(nc.gpsimd.memset(ident[:, :], 0.0))
            order.link(nc.gpsimd.affine_select(out=ident[:, :], in_=ident[:, :], compare_op=ALU.not_equal, fill=1.0,
                                               base=0, pattern=[[-1, 128]], channel_multiplier=1))
            nc.gpsimd.memset(eps[:, :], EPS)
            nc.gpsimd.memset(zero[:, :], 0.0)
            nc.gpsimd.memset(neghalf[:, :], -0.5).then_inc(ident_ready, 1)
            nc.gpsimd.tensor_copy(identb[:, :], ident[:, :]).then_inc(ident_ready, 1)
            pool.wait_ge(ident_ready, 2)
            for k, (lo, hi) in enumerate(((0, 2), (2, NT))):
                pool.wait_ge(ln_stats, k + 1)
                order.link(nc.gpsimd.tensor_scalar(vareps[:, lo:hi], meanvar[:, lo:hi, 1], EPS, None, ALU.add))
                nc.gpsimd.tensor_tensor(rstd[:, lo:hi], vareps[:, lo:hi], neghalf[:, lo:hi], ALU.pow).then_inc(rstd_ready, 1)

            def save_keys(b, p, first):
                pool.wait_ge(TA_drained, fills(b, 2, first))
                pool.wait_ge(TB_drained, fills(b, 2, first))
                nc.gpsimd.tensor_copy(keysT[:, b, :] if isinstance(b, int) else keysT[:, ds(b, 1), :].rearrange("p a k -> p (a k)"),
                                      ctxT[p][:, T0:K]).then_inc(keys_saved, 1)

            def rstd_b(b):
                pool.wait_ge(statsB_ready, b + 1)
                order.link(nc.gpsimd.tensor_tensor(veB[:, :], mvB[:, :, 1], eps[:, 0:QT], ALU.add))
                nc.gpsimd.tensor_tensor(rstdB[:, :], veB[:, :], neghalf[:, 0:QT], ALU.pow).then_inc(rstdB_ready, 1)

            for p in range(2):
                nc.gpsimd.memset(kaug[p], 1.0).then_inc(consts2_ready, 1)
                order.link(nc.gpsimd.memset(qaug[p], 1.0))
                nc.gpsimd.affine_select(out=qaug[p], in_=qaug[p], compare_op=ALU.is_ge, fill=0.0,
                                        base=RM - 1, pattern=[[0, H], [0, S]], channel_multiplier=-1).then_inc(consts2_ready, 1)
                order.link(nc.gpsimd.memset(vaug[p], 0.0))
                nc.gpsimd.memset(vaug[p][:, :, :, DH:DH + 1], 1.0).then_inc(consts2_ready, 1)
            nc.gpsimd.memset(ones_col[:, :], 1.0).then_inc(consts2_ready, 1)
            nc.gpsimd.memset(bad[:, :], 0.0).then_inc(consts2_ready, 1)
            order.link(nc.gpsimd.memset(sel15[:, :], 0.0))
            nc.gpsimd.memset(sel15[:, B - 1:B], 1.0).then_inc(consts2_ready, 1)
            save_keys(0, 0, True)
            save_keys(1, 1, False)
            rstd_b(0)
            pool.wait_ge(mask_loaded, 32)
            nc.gpsimd.tensor_copy(maskF, maskB[:, :, 1:TAIL + 1]).then_inc(maskF_ready, 1)
            for i in order.loop(1, B // 2, 2):
                for p in range(2):
                    save_keys(2 * i + p, p, False)
                    rstd_b(2 * i + (p - 1))
            rstd_b(B - 1)

            pool.wait_ge(flag_ready, 1)
            general = pool.value_load(flag[0:1, 0:1])
            with pool.If(general > 0):
                nc.gpsimd.tensor_scalar(negident, identb[:, :], NEG, None, ALU.mult).then_inc(g_neg, 1)
                nc.gpsimd.memset(grecip, 1.0).then_inc(g_free, 1)
                with pool.Fori(0, B) as b:
                    pool.wait_ge(g_stats, b + 1)
                    nc.gpsimd.tensor_tensor(veB[:, :], mvB[:, :, 1], eps[:, 0:QT], ALU.add).then_inc(g_neg, 1)
                    pool.wait_ge(g_neg, b + 2)
                    nc.gpsimd.tensor_tensor(rstdB[:, :], veB[:, :], neghalf[:, 0:QT], ALU.pow).then_inc(g_rstd, 1)
            with pool.Else():
                fast = Tally(pool, pool_fast)

                def norm_c(m, p, again):
                    if again:
                        pool.wait_ge(v_ready, m - 1)
                    nc.gpsimd.tensor_tensor(keysS[p], keysT[:, ds(m, 1), :].rearrange("p a k -> p (a k)"),
                                            zero_col.to_broadcast([128, TAIL]), ALU.add).then_inc(keysS_ready, 1)
                    pool.wait_ge(lnC_stats, m + 1)
                    fast.link(nc.gpsimd.tensor_tensor(veB[:, :], mvB[:, :, 1], eps[:, 0:QT], ALU.add))
                    nc.gpsimd.tensor_tensor(rstdB[:, :], veB[:, :], neghalf[:, 0:QT], ALU.pow).then_inc(rstdC_ready, 1)

                def split(m, p, again):
                    if again:
                        pool.wait_ge(parts_saved[p], half(m, p, 32, 0))
                        pool.wait_ge(S1_filled, 32 * m - 32)
                    for filled, full, res, part in ((q_ready, qf, qres, qpart[p]), (k_ready, kf, kres, kpart[p])):
                        pool.wait_ge(filled, m + 1)
                        fast.link(nc.gpsimd.tensor_tensor(part[:, 0, :], full, zero_col.to_broadcast(list(full.shape)), ALU.add))
                        fast.link(nc.gpsimd.tensor_tensor(res, full, part[:, 0, :], ALU.subtract))
                        fast.link(nc.gpsimd.tensor_tensor(part[:, 1, :], res, zero_col.to_broadcast(list(full.shape)), ALU.add))
                        last = nc.gpsimd.tensor_tensor(part[:, 2, :], res, part[:, 1, :], ALU.subtract)
                        if full is qf:
                            fast.link(last)
                        else:
                            last.then_inc(parts_ready, 1)

                norm_c(0, 0, False)
                split(0, 0, False)
                norm_c(1, 1, False)
                split(1, 1, False)
                norm_c(2, 0, True)
                split(2, 0, True)
                norm_c(3, 1, True)
                split(3, 1, True)
                for i in fast.loop(1, B // 2 - 1, 16):
                    for p in range(2):
                        norm_c(2 * i + (2 + p), p, True)
                        split(2 * i + (2 + p), p, True)

            late = Tally(pool, pool_late)
            pool.wait_ge(attn_ready, NT)
            nc.gpsimd.iota(iota_slot, pattern=[[1, E * CAP]], base=0, channel_multiplier=0,
                           allow_small_or_imprecise_dtypes=True).then_inc(gconst_ready, 1)
            nc.gpsimd.iota(iota_e, pattern=[[0, NT], [1, E]], base=0, channel_multiplier=0,
                           allow_small_or_imprecise_dtypes=True).then_inc(gconst_ready, 1)
            nc.gpsimd.memset(allones, 1.0).then_inc(gconst_ready, 1)
            pool.wait_ge(gconst_ready, 3)
            nc.gpsimd.affine_select(out=upper, in_=allones, compare_op=ALU.is_gt, fill=0.0,
                                    base=0, pattern=[[1, 128]], channel_multiplier=-1).then_inc(gconst_ready, 1)

            def norm3(b, p):
                pool.wait_ge(x3_stats, b + 1)
                late.link(nc.gpsimd.tensor_tensor(veB[:, :], mvB[:, :, 1], eps[:, 0:QT], ALU.add))
                nc.gpsimd.tensor_tensor(rstdB[:, :], veB[:, :], neghalf[:, 0:QT], ALU.pow).then_inc(x3_rstd, 1)
                pool.wait_ge(xn3_ready, QT * b + QT)
                nc.gpsimd.tensor_tensor(xn_all[:, ds(QT * b, QT), :], xn3[p], zero_col.unsqueeze(2).to_broadcast([128, QT, D]),
                                        ALU.add).then_inc(xn3_saved, 1)

            norm3(0, 0)
            norm3(1, 1)
            for i in late.loop(1, B // 2, 2):
                for p in range(2):
                    norm3(2 * i + p, p)

            def take_tokens(b, p, again):
                if again:
                    pool.wait_ge(xT_filled, b - 1)
                nc.gpsimd.tensor_tensor(xs[p], xn_all[:, ds(QT * b, QT), :], zero_col.unsqueeze(2).to_broadcast([128, QT, D]),
                                        ALU.add).then_inc(xs_ready, 1)

            pool.wait_ge(xn3_saved, B)
            take_tokens(0, 0, False)
            take_tokens(1, 1, False)
            with pool.Fori(1, B // 2) as i:
                for p in range(2):
                    take_tokens(2 * i + p, p, True)

            def take_slots(g, p, again):
                if again:
                    pool.wait_ge(eoX_filled, g - 1)
                nc.gpsimd.tensor_tensor(eoS[p], eoT[:, :, ds(CAP * g, CAP)], zero_col.unsqueeze(2).to_broadcast([128, E, CAP]),
                                        ALU.add).then_inc(eoS_ready, 1)

            pool.wait_ge(eoT_ready, E)
            take_slots(0, 0, False)
            take_slots(1, 1, False)
            with pool.Fori(1, B // 2) as i:
                for p in range(2):
                    take_slots(2 * i + p, p, True)

        @block.scalar
        def _(act):
            for dst, src in ((w0_sb, w0), (wq_sb, wq), (wk_sb, wk), (wv_sb, wv), (wo_sb, wo), (router_sb, router)):
                act.dma_start(dst[:, :], src).then_inc(w_loaded, 16)
            for dst, src in ((b0_col, b0), (bq_col, bq), (bk_col, bk)):
                act.dma_start(dst[:, :], src.rearrange("(p a) -> p a", a=1)).then_inc(w_loaded, 16)
            for dst, src in ((fb_row, fbias), (bv_row, bv), (bo_row, bo), (gates_in[:, 0:2], g_xattn),
                             (gates_in[:, 2:4], g_ffn), (ws_col, wscale)):
                act.dma_start(dst[:, :], src.rearrange("(a n) -> a n", a=1).to_broadcast([128, src.shape[0]])).then_inc(w_loaded, 16)
            for j in range(4):
                act.dma_start(packed_sb[32 * j:32 * j + 32, :], packed.rearrange("(r i) -> r i", r=32)).then_inc(ternary_loaded, 16)
            masks = mask.rearrange("b a (t p) k -> p (b a t) k", p=128)
            act.dma_start(maskA, masks[:, :, 0:T0 - 1]).then_inc(mask_loaded, 16)
            act.dma_start(maskB, masks[:, :, T0 - 1:K]).then_inc(mask_loaded, 16)
            act.wait_ge(w_loaded, 16 * 15)
            nc.scalar.activation(gates[:, :], gates_in[:, :], ACT.Tanh).then_inc(gates_ready, 1)

            def drain_ctx(b, p, first):
                for k, c in enumerate((0, 2)):
                    lo, hi = 128 * TCH[c][0], 128 * TCH[c][1]
                    act.wait_ge(TA_filled, fills(b, k + 1, first))
                    if k == 0 and (not isinstance(b, int) or b >= 2):
                        act.wait_ge(keys_saved, b - 1)
                    nc.scalar.activation(ctxT[p][:, lo:hi], TA[:, 0:hi - lo], ACT.Copy).then_inc(TA_drained, 1)

            def drain_probs(b, k0, first):
                for k, c in enumerate((0, 2)):
                    act.wait_ge(TA_filled, fills(b, k0 + k + 1, first))
                    n = TCH[c][1] - TCH[c][0]
                    nc.scalar.activation(probT[:, TCH[c][0]:TCH[c][1], :],
                                         TA.rearrange("p (t q) -> p t q", q=128)[:, 0:n, :], ACT.Copy).then_inc(TA_drained, 1)

            def softmax(b, q):
                act.wait_ge(max_done, 2 * b + (q + 1))
                if not isinstance(b, int) or b >= 1:
                    act.wait_ge(prob_used, 2 * b + (q - 1))
                u = 2 * b + q
                nc.scalar.activation(prob[q][:, :], S_ps, ACT.Exp, bias=nmax[:, ds(u, 1)],
                                     accum_out=rsum[:, ds(u, 1)]).then_inc(exp_done, 1)

            def body(b, p, first):
                drain_ctx(b, p, first)
                if not first:
                    drain_probs(b, 2, first)
                softmax(b, 0)
                drain_probs(b, 2 if first else 4, first)
                softmax(b, 1)

            body(0, 0, True)
            body(1, 1, False)
            with act.Fori(1, B // 2) as i:
                for p in range(2):
                    body(2 * i + p, p, False)
            drain_probs(B, 0, False)

            act.wait_ge(flag_ready, 1)
            general = act.value_load(flag[0:1, 0:1])
            with act.If(general > 0):
                with act.Fori(0, B) as b:
                    for c in range(4):
                        lo, hi = 128 * TCH[c][0], min(128 * TCH[c][1], K)
                        act.wait_ge(g_T_filled, 4 * b + (c + 1))
                        nc.scalar.activation(ctxT[0][:, lo:hi], (TA, TB)[c % 2][:, 0:hi - lo], ACT.Copy).then_inc(g_T_drained, 1)
                with act.Fori(0, B) as b:
                    for q in range(QT):
                        act.wait_ge(g_free, 2 * H * b + (H * q + 1))
                        act.dma_start(maskQ, mask[ds(b, 1), :, 128 * q:128 * q + 128, :].rearrange("a c q k -> (a c q) k")
                                      ).then_inc(g_mask_loaded, 16)
                        with act.Fori(0, H) as h:
                            u = 2 * H * b + h + H * q
                            act.wait_ge(g_max, u + 1)
                            nc.scalar.activation(prob[0], S_ps, ACT.Exp, bias=gmax, accum_out=gsum).then_inc(g_exp, 1)
                            for c in range(4):
                                n, rows = TCH[c][1] - TCH[c][0], 128 if c < 3 else KR
                                act.wait_ge(g_T_filled, 4 * u + (4 * B + c + 1))
                                nc.scalar.activation(probT[0:rows, TCH[c][0]:TCH[c][1], :],
                                                     (TA, TB)[c % 2].rearrange("p (t q) -> p t q", q=128)[0:rows, 0:n, :],
                                                     ACT.Copy).then_inc(g_T_drained, 1)
            with act.Else():
                def drain(b, g):
                    act.wait_ge(PV_filled, 4 * b + (g + 1))
                    if g == 0 and not (isinstance(b, int) and b == 0):
                        act.wait_ge(back_filled, 2 * b)
                    nc.scalar.activation(headsT[:, g, :], PV, ACT.Copy).then_inc(heads_ready, 1)

                def keys(m):
                    if not (isinstance(m, int) and m == 0):
                        act.wait_ge(parts_ready, m)
                    act.wait_ge(k_filled, m + 1)
                    nc.scalar.activation(kf, M_ps[:, 0:TAIL], ACT.Identity, bias=bk_col[:, :]).then_inc(k_ready, 1)

                def heads(b, prev, proj):
                    for h in range(H):
                        if h % 4 == 0 and h < 8 and prev:
                            drain(b - 1, 2 + h // 4)
                        if h % 4 == 0 and h >= 8:
                            drain(b, h // 4 - 2)
                        act.wait_ge(ST_filled, 16 * b + (h + 1))
                        nc.scalar.activation(probs8[0:TP, h % 8, :], ST[h % 2], ACT.Exp).then_inc(P_ready, 1)
                        if h == 4 and proj:
                            keys(b + 2)

                keys(0)
                keys(1)
                heads(0, False, True)
                with act.Fori(1, B - 2) as b:
                    heads(b, True, True)
                heads(B - 2, True, False)
                heads(B - 1, True, False)
                drain(B - 1, 2)
                drain(B - 1, 3)

            act.wait_ge(attn_ready, NT)

            def drain_tokens(b, p):
                act.wait_ge(xn3T_filled, b + 1)
                nc.scalar.activation(xn3T[p], bank[4 + p][:, 0:S], ACT.Copy).then_inc(xn3T_ready, 1)

            def out_projection(b, p, first):
                nc.scalar.activation(ao[p], attn[:, ds(QT * b, QT), :], ACT.Copy).then_inc(ao_ready, 1)
                act.wait_ge(aoT_filled, b + 1)
                nc.scalar.activation(aoT[p], bank[p][:, 0:S], ACT.Copy).then_inc(aoT_ready, 1)
                if not first:
                    drain_tokens(b - 1, 1 - p)

            out_projection(0, 0, True)
            out_projection(1, 1, False)
            with act.Fori(1, B // 2) as i:
                for p in range(2):
                    out_projection(2 * i + p, p, False)
            drain_tokens(B - 1, 1)

            act.wait_ge(shifted_ready, 1)
            nc.scalar.activation(expd, shifted, ACT.Exp).then_inc(expd_ready, 1)

            with act.Fori(0, B // 2) as i:
                for p in range(2):
                    b = 2 * i + p
                    act.wait_ge(xT_filled, b + 1)
                    nc.scalar.activation(xT[:, :, ds(CAP * b, CAP)], bank[p].rearrange("p (e c) -> p e c", e=E), ACT.Copy).then_inc(xT_drained, 1)
                    act.wait_ge(cA_filled, b + 1)
                    nc.scalar.activation(combT[:, ds(b, 1), 0:512].rearrange("p a n -> p (a n)"), bank[2 + 2 * p], ACT.Copy).then_inc(cA_drained, 1)

            def gelus(e, p, first):
                for c in range(HC):
                    rows = HROWS[c]
                    act.wait_ge(a_filled, HC * e + (c + 1))
                    if not (first and c < 2):
                        act.wait_ge(hid_ready, HC * e + (c - 1))
                    nc.scalar.activation(gl[c % 2][0:rows, :], bank[c % 2][0:rows, :], ACT.Gelu_apprx_tanh).then_inc(gelu_done, 1)
                    if c == 1 and not first:
                        drain_expert(e - 1, 1 - p)

            def drain_expert(e, p):
                act.wait_ge(eo_filled, e + 1)
                nc.scalar.activation(eoT[:, ds(e, 1), :].rearrange("p a n -> p (a n)"), bank[4 + p], ACT.Copy).then_inc(eoT_ready, 1)

            gelus(0, 0, True)
            gelus(1, 1, False)
            with act.Fori(1, E // 2) as i:
                for p in range(2):
                    gelus(2 * i + p, p, False)
            drain_expert(E - 1, 1)

            with act.Fori(0, B // 2) as i:
                for p in range(2):
                    g = 2 * i + p
                    act.wait_ge(outT_filled, g + 1)
                    nc.scalar.activation(outT[p], bank[2 + p][:, 0:S], ACT.Copy).then_inc(outT_ready, 1)

        @block.vector
        def _(dve):
            order = Tally(dve, dve_order)

            def ln(lo, hi):
                for t in range(lo, hi):
                    m = order.mark(nc.vector.bn_stats(stats[:, t, :], x_sb[:, t, :]))
                dve.wait_ge(dve_order, m)
                for t in range(lo, hi):
                    last = nc.vector.bn_aggr(meanvar[:, t, :], stats[:, t, :])
                last.then_inc(ln_stats, 1)

            dve.wait_ge(x_loaded, 16)
            ln(0, 2)
            dve.wait_ge(ternary_loaded, 64)
            for j in range(4):
                m = order.mark(nc.vector.tensor_scalar(tern_i[32 * j:32 * j + 32, :], packed_sb[32 * j:32 * j + 32, :],
                                                       2 * j, 3, ALU.logical_shift_right, ALU.bitwise_and))
            dve.wait_ge(dve_order, m)
            nc.vector.tensor_scalar(tern[:, :], tern_i[:, :], -1.0, None, ALU.add).then_inc(tern_ready, 1)
            dve.wait_ge(xrest_loaded, 16)
            ln(2, NT)
            dve.wait_ge(w_loaded, 16 * 15)

            def normalise(b, p):
                if not isinstance(b, int) or b >= 2:
                    pass
                for q in range(QT):
                    u = 2 * b + q
                    src = x_sb[:, u, :] if isinstance(b, int) else x_sb[:, ds(u, 1), :].rearrange("p a d -> p (a d)")
                    nc.vector.tensor_scalar(xn[p][:, q, :], src, meanvar[:, ds(u, 1), 0], rstd[:, ds(u, 1)],
                                            ALU.subtract, ALU.mult).then_inc(xn_ready, 1)

            def prep(b, p, first):
                dve.wait_ge(xnT_filled, b + 1)
                nc.vector.tensor_copy(xnT[p][:, :], M_ps[:, 0:S]).then_inc(xnT_ready, 1)
                if first:
                    dve.wait_ge(ternT_filled, 1)
                    nc.vector.tensor_copy(ternT[:, :], TB.bitcast(bf16)[:, 0:128]).then_inc(ternT_ready, 1)
                for k, c in enumerate((1, 3)):
                    lo, hi = 128 * TCH[c][0], min(128 * TCH[c][1], K)
                    dve.wait_ge(TB_filled, fills(b, k + 1, first))
                    if k == 0 and (not isinstance(b, int) or b >= 2):
                        dve.wait_ge(keys_saved, b - 1)
                    nc.vector.tensor_copy(ctxT[p][:, lo:hi], TB[:, 0:hi - lo]).then_inc(TB_drained, 1)
                    if k == 0:
                        dve.wait_ge(proj_filled, b + 1)
                        nc.vector.tensor_scalar(projT[p][:, :], M_ps[:, S:2 * S], b0_col[:, :], None, ALU.add).then_inc(projT_ready, 1)

            def maximum(b, q):
                u = 2 * b + q
                dve.wait_ge(S_filled, u + 1)
                nc.vector.tensor_reduce(nmax[:, ds(u, 1)], S_ps, AX.X, ALU.max, negate=True).then_inc(max_done, 1)

            def drain_probs(b, k0, first):
                for k, c in enumerate((1, 3)):
                    n = TCH[c][1] - TCH[c][0]
                    rows = 128 if c == 1 else KR
                    dve.wait_ge(TB_filled, fills(b, k0 + k + 1, first))
                    nc.vector.tensor_copy(probT[0:rows, TCH[c][0]:TCH[c][1], :],
                                          TB.rearrange("p (t q) -> p t q", q=128)[0:rows, 0:n, :]).then_inc(TB_drained, 1)

            def attend(b, q, p):
                u = 2 * b + q
                dve.wait_ge(exp_done, u + 1)
                order.link(nc.vector.reciprocal(rgate[:, 0:1], rsum[:, ds(u, 1)]))
                order.link(nc.vector.tensor_scalar(rgate[:, 1:2], rgate[:, 0:1], gates[:, 0:1], None, ALU.mult))
                dve.wait_ge(O_filled, u + 1)
                xt = x_sb[:, ds(u, 1), :].rearrange("p a d -> p (a d)")
                nc.vector.scalar_tensor_tensor(x1[p][:, q, :], O_ps[:, 0:D], rgate[:, 1:2], xt, ALU.mult, ALU.add).then_inc(O_drained, 1)

            def quantise(b, p):
                xt = [x1[p][:, q, :] for q in range(QT)]
                dve.wait_ge(O_drained, 2 * b + 2)
                for q in range(QT):
                    m = order.mark(nc.vector.bn_stats(statsB[:, q, :], xt[q]))
                dve.wait_ge(dve_order, m)
                nc.vector.memset(dve_slot[:, :], 0.0)
                for q in range(QT):
                    last = nc.vector.bn_aggr(mvB[:, q, :], statsB[:, q, :])
                last.then_inc(statsB_ready, 1)
                dve.wait_ge(statsB_ready, b + 1)
                dve.wait_ge(rstdB_ready, b + 1)
                for q in range(QT):
                    m = order.mark(nc.vector.tensor_scalar(xnB[:, q, :], xt[q], mvB[:, q, 0:1], rstdB[:, q:q + 1],
                                                           ALU.subtract, ALU.mult))
                dve.wait_ge(dve_order, m)
                order.link(nc.vector.tensor_reduce(amax[:, :], xnB[:, :, :], AX.X, ALU.max, apply_absolute_value=True))
                order.link(nc.vector.tensor_scalar(amax[:, :], amax[:, :], 1e-5, None, ALU.max))
                order.link(nc.vector.reciprocal(qscale[:, :], amax[:, :]))
                order.link(nc.vector.tensor_scalar(qscale[:, :], qscale[:, :], 127.0, None, ALU.mult))
                order.mark(nc.vector.tensor_scalar(dscale[:, :], amax[:, :], ws_col[:, :], 1.0 / 127.0, ALU.mult, ALU.mult))
                for q in range(QT):
                    m = order.mark(nc.vector.tensor_scalar(xnB[:, q, :], xnB[:, q, :], qscale[:, q:q + 1], MAGIC, ALU.mult, ALU.add))
                dve.wait_ge(dve_order, m)
                order.link(nc.vector.tensor_scalar(xnB[:, :, :], xnB[:, :, :], MAGIC - 128.0, MAGIC + 127.0, ALU.max, ALU.min))
                nc.vector.tensor_scalar(xq[:, :, :], xnB[:, :, :], -MAGIC, None, ALU.add).then_inc(xq_ready, 1)

            def drain_xq(b):
                dve.wait_ge(xqT_filled, b + 1)
                nc.vector.tensor_copy(xqT[:, :], Mb[:, 0:S]).then_inc(xqT_ready, 1)

            def linear(b, p):
                dve.wait_ge(y_filled, b + 1)
                for q in range(QT):
                    m = order.mark(nc.vector.scalar_tensor_tensor(yB[:, q, :], M_ps[:, S + 128 * q:S + 128 * q + 128],
                                                                  dscale[:, q:q + 1], fb_row[:, :], ALU.mult, ALU.add))
                dve.wait_ge(dve_order, m)
                xt = x_sb[:, ds(2 * b, 2), :]
                nc.vector.scalar_tensor_tensor(xt, yB[:, :, :], gates[:, 2:3], x1[p][:, :, :], ALU.mult, ALU.add).then_inc(x2_ready, 1)

            def body(b, p, first):
                normalise(b, p)
                prep(b, p, first)
                maximum(b, 0)
                if not first:
                    drain_probs(b, 2, first)
                    attend(b - 1, 1, 1 - p)
                    quantise(b - 1, 1 - p)
                maximum(b, 1)
                if not first:
                    drain_xq(b - 1)
                drain_probs(b, 2 if first else 4, first)
                attend(b, 0, p)
                if not first:
                    linear(b - 1, 1 - p)

            dve.wait_ge(gates_ready, 1)
            dve.wait_ge(rstd_ready, 1)
            body(0, 0, True)
            dve.wait_ge(rstd_ready, 2)
            body(1, 1, False)
            for i in order.loop(1, B // 2, 36):
                for p in range(2):
                    body(2 * i + p, p, False)
            drain_probs(B, 0, False)
            attend(B - 1, 1, 1)
            quantise(B - 1, 1)
            drain_xq(B - 1)
            linear(B - 1, 1)

            dve.wait_ge(mask_loaded, 32)
            words = maskA.rearrange("p t k -> p (t k)").bitcast(i32)
            n = NT * (T0 - 1) // 4
            while n > 300:
                n //= 2
                order.link(nc.vector.tensor_tensor(words[:, 0:n], words[:, 0:n], words[:, n:2 * n], ALU.bitwise_and))
            order.link(nc.vector.tensor_reduce(maskpair[:, :], words[:, 0:n].bitcast(mybir.dt.uint16), AX.X, ALU.min))
            dve.wait_ge(consts2_ready, 9)
            order.link(nc.vector.tensor_scalar(bad[:, 0:1], maskpair[:, :], 257.0, None, ALU.is_lt))
            order.link(nc.vector.tensor_reduce(maskmin[:, :], maskB[:, :, 0:1].rearrange("p t k -> p (t k)"), AX.X, ALU.min))
            order.mark(nc.vector.tensor_scalar(bad[:, 1:2], maskmin[:, :], 1.0, None, ALU.is_lt))
            dve.wait_ge(cnt_filled, 1)
            order.link(nc.vector.tensor_copy(cnt[:, :], M_ps[0:B, 0:TAIL]))
            nc.vector.tensor_scalar(maskrow[:, :], cnt[:, :], NEG / S, None, ALU.mult).then_inc(maskrow_ready, 1)
            order.link(nc.vector.scalar_tensor_tensor(cntv[:, :], cnt[:, :], float(S), cnt[:, :], ALU.subtract, ALU.mult))
            order.link(nc.vector.tensor_reduce(cmin[:, 0:1], cntv[:, :], AX.X, ALU.min))
            order.link(nc.vector.tensor_reduce(cmin[:, 1:2], cnt[:, :], AX.X, ALU.min))
            nc.vector.tensor_tensor(bad[0:B, 2:3], cmin[:, 1:2], cmin[:, 0:1], ALU.subtract).then_inc(bad_ready, 1)
            dve.wait_ge(bad_filled, 1)
            order.link(nc.vector.tensor_reduce(badsum[:, :], M_ps[0:1, 0:3], AX.X, ALU.add))
            nc.vector.tensor_scalar(flag[:, :], badsum[:, :], 0.0, None, ALU.is_gt).then_inc(flag_ready, 1)

            dve.wait_ge(flag_ready, 1)
            general = dve.value_load(flag[0:1, 0:1])
            with dve.If(general > 0):
                slow = Tally(dve, dve_gen)
                for b in slow.loop(0, B, 2):
                    xt = [x_sb[:, ds(2 * b + q, 1), :].rearrange("p a d -> p (a d)") for q in range(QT)]
                    for q in range(QT):
                        m = slow.mark(nc.vector.bn_stats(statsB[:, q, :], xt[q]))
                    dve.wait_ge(dve_gen, m)
                    nc.vector.memset(dve_slot[:, :], 0.0)
                    for q in range(QT):
                        last = nc.vector.bn_aggr(mvB[:, q, :], statsB[:, q, :])
                    last.then_inc(g_stats, 1)
                    dve.wait_ge(g_stats, b + 1)
                    dve.wait_ge(g_rstd, b + 1)
                    for q in range(QT):
                        nc.vector.tensor_scalar(xnG[:, q, :], xt[q], mvB[:, q, 0:1], rstdB[:, q:q + 1],
                                                ALU.subtract, ALU.mult).then_inc(g_xn, 1)
                    dve.wait_ge(g_xT_filled, b + 1)
                    nc.vector.tensor_copy(xnGT, M_ps[:, 0:S]).then_inc(g_xT_ready, 1)
                    dve.wait_ge(g_q_filled, b + 1)
                    nc.vector.tensor_scalar(qG, M_ps[:, 0:S], bq_col[:, :], DH ** -0.5, ALU.add, ALU.mult).then_inc(g_q_ready, 1)
                    dve.wait_ge(g_k_filled, b + 1)
                    nc.vector.tensor_scalar(prob[0], S_ps, bk_col[:, :], None, ALU.add).then_inc(g_k_ready, 1)
                    dve.wait_ge(g_v_filled, b + 1)
                    for t in range(KT):
                        rows = 128 if t < KT - 1 else KR
                        last = nc.vector.tensor_tensor(ctxN[0][0:rows, t, :], PS[0:rows, 128 * t:128 * t + 128], bv_row[0:rows, :], ALU.add)
                    last.then_inc(g_v_ready, 1)
                with dve.Fori(0, B) as b:
                    for q in range(QT):
                        dve.wait_ge(g_mask_loaded, 32 * b + (16 * q + 16))
                        nc.vector.tensor_copy(maskQF, maskQ).then_inc(g_mask_ready, 1)
                        with dve.Fori(0, H) as h:
                            u = 2 * H * b + h + H * q
                            dve.wait_ge(g_S_filled, u + 1)
                            nc.vector.tensor_reduce(gmax, S_ps, AX.X, ALU.max, negate=True).then_inc(g_max, 1)
                            dve.wait_ge(g_exp, u + 1)
                            nc.vector.reciprocal(grecip, gsum).then_inc(g_S_free, 1)
                            dve.wait_ge(g_S_free, u + 1)
                            dve.wait_ge(g_O_filled, u + 1)
                            nc.vector.tensor_scalar(attn[:, ds(2 * b + q, 1), ds(DH * h, DH)].rearrange("p a d -> p (a d)"), O_ps[:, 0:DH], grecip,
                                                    None, ALU.mult).then_inc(g_free, 1)
                dve.wait_ge(g_free, NT * H + 1)
                nc.vector.memset(dve_slot[:, :], 0.0).then_inc(attn_ready, NT)
            with dve.Else():
                fast = Tally(dve, dve_fast)

                def moments(m):
                    nc.vector.memset(dve_slot[:, :], 0.0)
                    for q in range(QT):
                        n = fast.mark(nc.vector.bn_stats(statsB[:, q, :], x_sb[:, ds(2 * m + q, 1), :].rearrange("p a d -> p (a d)")))
                    dve.wait_ge(dve_fast, n)
                    nc.vector.memset(dve_slot[:, :], 0.0)
                    for q in range(QT):
                        last = nc.vector.bn_aggr(mvB[:, q, :], statsB[:, q, :])
                    last.then_inc(lnC_stats, 1)

                def normalise(m):
                    dve.wait_ge(lnC_stats, m + 1)
                    dve.wait_ge(rstdC_ready, m + 1)
                    for q in range(QT):
                        nc.vector.tensor_scalar(xnC[:, q, :], x_sb[:, ds(2 * m + q, 1), :].rearrange("p a d -> p (a d)"),
                                                mvB[:, q, 0:1], rstdB[:, q:q + 1], ALU.subtract, ALU.mult).then_inc(xnC_ready, 1)

                def drain_xnT(m):
                    dve.wait_ge(xnCT_filled, m + 1)
                    nc.vector.tensor_copy(xnCT, M_ps[:, 0:S]).then_inc(xnCT_ready, 1)

                def queries(m):
                    dve.wait_ge(q_filled, m + 1)
                    if not (isinstance(m, int) and m == 0):
                        dve.wait_ge(parts_ready, m)
                    nc.vector.tensor_scalar(qf, M_ps[:, 0:S], bq_col[:, :], DH ** -0.5, ALU.add, ALU.mult).then_inc(q_ready, 1)

                def values(n, p):
                    dve.wait_ge(v_filled, n + 1)
                    for t in range(4):
                        last = nc.vector.tensor_tensor(vaug[p][:, t, :, 0:DH], M_ps[0:TP, 128 * t:128 * t + 128].rearrange("p (h d) -> p h d", d=DH),
                                                       bv_row[0:TP, :].rearrange("p (h d) -> p h d", d=DH), ALU.add)
                    last.then_inc(v_ready, 1)

                def maximum2(n, u):
                    dve.wait_ge(S1_filled, 32 * n + (u + 1))
                    at = H * (u % QT) + u // QT
                    nc.vector.tensor_reduce(nm[:, at:at + 1], S1[u % 2], AX.X, ALU.max, negate=True).then_inc(S1_max, 1)

                def split_max(n, p):
                    dve.wait_ge(nmT_filled, n + 1)
                    src = M_ps[0:H, 0:S]
                    fast.link(nc.vector.tensor_copy(nmpart[p][:, 0, :], src))
                    fast.link(nc.vector.tensor_tensor(nmres, src, nmpart[p][:, 0, :], ALU.subtract))
                    fast.link(nc.vector.tensor_copy(nmpart[p][:, 1, :], nmres))
                    nc.vector.tensor_tensor(nmpart[p][:, 2, :], nmres, nmpart[p][:, 1, :], ALU.subtract).then_inc(nm_ready, 1)

                def divide(b, q):
                    dve.wait_ge(back_filled, 2 * b + (q + 1))
                    o = M_ps.rearrange("p (h e) -> p h e", e=32)
                    fast.link(nc.vector.reciprocal(rden, o[:, :, DH]))
                    dst = attn[:, ds(2 * b + q, 1), :].rearrange("p a (h d) -> p (a h) d", d=DH)
                    nc.vector.tensor_tensor(dst, o[:, :, 0:DH], rden.unsqueeze(2).to_broadcast([128, H, DH]),
                                            ALU.mult).then_inc(attn_ready, 1)

                def body(b, p, prev, maxi, proj):
                    for h in range(H):
                        if maxi:
                            for u in UNITS[h]:
                                maximum2(b + 1, u)
                        if h == 0 and proj:
                            moments(b + 2)
                        if h == 1 and proj:
                            normalise(b + 2)
                        if h == 2 and proj:
                            drain_xnT(b + 2)
                        if h == 3 and proj:
                            queries(b + 2)
                        if h in (6, 7) and prev:
                            divide(b - 1, h - 6)
                        if h == 9 and maxi:
                            values(b + 1, 1 - p)
                        if h == 13 and maxi:
                            split_max(b + 1, 1 - p)

                body(-2, 0, False, False, True)
                body(-1, 1, False, True, True)
                body(0, 0, False, True, True)
                body(1, 1, True, True, True)
                for i in fast.loop(1, B // 2 - 1, 14):
                    for p in range(2):
                        body(2 * i + p, p, True, True, True)
                body(B - 2, 0, True, True, False)
                body(B - 1, 1, True, False, False)
                divide(B - 1, 0)
                divide(B - 1, 1)

            late = Tally(dve, dve_late)
            dve.wait_ge(attn_ready, NT)

            def drain_logits(b, p):
                dve.wait_ge(lg_filled, b + 1)
                nc.vector.tensor_copy(logits[:, ds(QT * b, QT), :], bank[6 + p][:, 0:QT * E].rearrange("p (t e) -> p t e", e=E)).then_inc(lg_ready, 1)

            def out_projection(b, p, first):
                xt = [x_sb[:, ds(2 * b + q, 1), :].rearrange("p a d -> p (a d)") for q in range(QT)]
                dve.wait_ge(wo_filled, b + 1)
                for q in range(QT):
                    m = late.mark(nc.vector.tensor_tensor(x3t[:, q, :], bank[2 + p][:, 128 * q:128 * q + 128], bo_row[:, :], ALU.add))
                dve.wait_ge(dve_late, m)
                x2t = x_sb[:, ds(2 * b, 2), :]
                nc.vector.scalar_tensor_tensor(x2t, x3t, gates[:, 1:2], x2t, ALU.mult, ALU.add).then_inc(x3_read, 1)
                dve.wait_ge(x3_read, b + 1)
                nc.vector.memset(dve_slot[:, :], 0.0)
                for q in range(QT):
                    m = late.mark(nc.vector.bn_stats(statsB[:, q, :], xt[q]))
                dve.wait_ge(dve_late, m)
                nc.vector.memset(dve_slot[:, :], 0.0)
                for q in range(QT):
                    last = nc.vector.bn_aggr(mvB[:, q, :], statsB[:, q, :])
                last.then_inc(x3_stats, 1)
                dve.wait_ge(x3_stats, b + 1)
                dve.wait_ge(x3_rstd, b + 1)
                if not isinstance(b, int) or b >= 2:
                    dve.wait_ge(xn3_saved, b - 1)
                for q in range(QT):
                    nc.vector.tensor_scalar(xn3[p][:, q, :], xt[q], mvB[:, q, 0:1], rstdB[:, q:q + 1],
                                            ALU.subtract, ALU.mult).then_inc(xn3_ready, 1)
                if not first:
                    drain_logits(b - 1, 1 - p)

            out_projection(0, 0, True)
            out_projection(1, 1, False)
            for i in late.loop(1, B // 2, 8):
                for p in range(2):
                    out_projection(2 * i + p, p, False)
            drain_logits(B - 1, 1)
            dve.wait_ge(lg_ready, B)
            dve.wait_ge(gconst_ready, 4)

            def wide(v):
                return v.unsqueeze(2).to_broadcast([128, NT, E])

            def link(ins):
                late.link(ins)

            def first_of(values, best, least, onehot):
                link(nc.vector.tensor_tensor(equal, values, wide(best), ALU.is_equal))
                link(nc.vector.scalar_tensor_tensor(cand, equal, -float(E), iota_e, ALU.mult, ALU.add))
                link(nc.vector.tensor_reduce(least, cand, AX.X, ALU.min))
                link(nc.vector.tensor_tensor(onehot, cand, wide(least), ALU.is_equal))

            link(nc.vector.tensor_reduce(gmx, logits, AX.X, ALU.max))
            nc.vector.tensor_tensor(shifted, logits, wide(gmx), ALU.subtract).then_inc(shifted_ready, 1)
            dve.wait_ge(expd_ready, 1)
            link(nc.vector.tensor_reduce(gmx, expd, AX.X, ALU.add))
            link(nc.vector.reciprocal(gmx, gmx))
            link(nc.vector.tensor_tensor(raw, expd, wide(gmx), ALU.mult))
            link(nc.vector.tensor_reduce(gate1, raw, AX.X, ALU.max))
            first_of(raw, gate1, least1, m1)
            link(nc.vector.tensor_tensor(work, raw, m1, ALU.mult))
            link(nc.vector.tensor_tensor(rest, raw, work, ALU.subtract))
            link(nc.vector.tensor_reduce(gate2, rest, AX.X, ALU.max))
            first_of(rest, gate2, least2, m2)
            half_ = NT * E
            link(nc.vector.tensor_copy(m12[:, 0:half_], m1.rearrange("p t e -> p (t e)")))
            nc.vector.tensor_copy(m12[:, half_:2 * half_], m2.rearrange("p t e -> p (t e)")).then_inc(m12_ready, 1)
            dve.wait_ge(cum_filled, 1)
            link(nc.vector.tensor_copy(pos1, bank[0][:, 0:half_].rearrange("p (t e) -> p t e", e=E)))
            link(nc.vector.tensor_scalar(count1, bank[1][:, 0:B * E].rearrange("p (b e) -> p b e", e=E), float(CAP), None, ALU.min))
            behind = bank[0][:, half_:2 * half_].rearrange("p (b t e) -> p b t e", t=QT, e=E)
            pos2v = pos2.rearrange("p (b t) e -> p b t e", t=QT)
            for t in range(QT):
                link(nc.vector.tensor_tensor(pos2v[:, :, t, :], behind[:, :, t, :], count1, ALU.add))
            for onehot, pos, least, keep, place, slot in ((m1, pos1, least1, keep1, place1, slot1),
                                                          (m2, pos2, least2, keep2, place2, slot2)):
                link(nc.vector.scalar_tensor_tensor(kept, pos, float(CAP), onehot, ALU.is_lt, ALU.mult))
                link(nc.vector.tensor_reduce(keep, kept, AX.X, ALU.add))
                link(nc.vector.tensor_tensor(work, pos, onehot, ALU.mult))
                link(nc.vector.tensor_reduce(place, work, AX.X, ALU.add))
                link(nc.vector.scalar_tensor_tensor(place, least, float(CAP), place, ALU.mult, ALU.add))
                link(nc.vector.scalar_tensor_tensor(slot, place, float(E * CAP + 1), keep, ALU.add, ALU.mult))
                link(nc.vector.tensor_scalar(slot, slot, -1.0, None, ALU.add))

            def combine(b, p, again):
                if again:
                    dve.wait_ge(cB_filled, b - 1)
                for q in range(QT):
                    u = 2 * b + q
                    late.mark(nc.vector.tensor_scalar(comb[p][:, q, :], iota_slot, slot1[:, ds(u, 1)], gate1[:, ds(u, 1)], ALU.is_equal, ALU.mult))
                    m = late.mark(nc.vector.tensor_scalar(comb2[:, q, :], iota_slot, slot2[:, ds(u, 1)], gate2[:, ds(u, 1)], ALU.is_equal, ALU.mult))
                dve.wait_ge(dve_late, m)
                link(nc.vector.tensor_tensor(comb[p], comb[p], comb2, ALU.add))
                nc.vector.tensor_scalar(disp[p], comb[p], 0.0, None, ALU.not_equal).then_inc(comb_ready, 1)
                dve.wait_ge(cB_filled, b + 1)
                nc.vector.tensor_copy(combT[:, ds(b, 1), 512:1024].rearrange("p a n -> p (a n)"), bank[3 + 2 * p]).then_inc(cB_drained, 1)

            combine(0, 0, False)
            combine(1, 1, False)
            for i in late.loop(1, B // 2, 10):
                for p in range(2):
                    combine(2 * i + p, p, True)

            def hidden(e, first):
                for c in range(HC):
                    rows = HROWS[c]
                    dve.wait_ge(b_filled, HC * e + (c + 1))
                    dve.wait_ge(gelu_done, HC * e + (c + 1))
                    if c == 1 and not first:
                        dve.wait_ge(eo_filled, e)
                    if c >= 2 or (c == 0 and not first):
                        dve.wait_ge(hid_used, (HC - 1) * e + max(c - 1, 0))
                    nc.vector.tensor_tensor(hid[c % 2][0:rows, :], bank[2 + c % 2][0:rows, :], gl[c % 2][0:rows, :], ALU.mult).then_inc(hid_ready, 1)

            hidden(0, True)
            with dve.Fori(1, E) as e:
                hidden(e, False)

            def residual(g, p):
                dve.wait_ge(y_back_filled, g + 1)
                xt = x_sb[:, ds(2 * g, 2), :]
                nc.vector.scalar_tensor_tensor(xt, bank[4 + p][:, 0:S].rearrange("p (t d) -> p t d", d=D), gates[:, 3:4], xt,
                                               ALU.mult, ALU.add).then_inc(x4_ready, 1)

            def slots(g, p, first):
                dve.wait_ge(eoX_filled, g + 1)
                nc.vector.tensor_copy(eo[p], bank[p].rearrange("p (t d) -> p t d", d=D)).then_inc(eo_ready, 1)
                if not first:
                    residual(g - 1, 1 - p)

            slots(0, 0, True)
            slots(1, 1, False)
            with dve.Fori(1, B // 2) as i:
                for p in range(2):
                    slots(2 * i + p, p, False)
            residual(B - 1, 1)

        @block.tensor
        def _(pe):
            def prep(b, p, first):
                pe.wait_ge(xn_ready, 2 * b + 2)
                if not isinstance(b, int) or b >= 2:
                    pe.wait_ge(x2_ready, b - 1)
                for q in range(QT):
                    last = nc.tensor.transpose(M_ps[:, 128 * q:128 * q + 128], xn[p][:, q, :], ident[:, :])
                last.then_inc(xnT_filled, 1)
                if first:
                    pe.wait_ge(tern_ready, 1)
                    nc.tensor.transpose(TB.bitcast(bf16)[:, 0:128], tern[:, :], identb[:, :]).then_inc(ternT_filled, 1)
                pe.wait_ge(ctx_loaded[p], 32 * (b // 2 + 1) if isinstance(b, int) else 16 * b + (32 - 16 * p))
                for c in range(4):
                    bk_, filled, drained = ((TA, TA_filled, TA_drained), (TB, TB_filled, TB_drained))[c % 2]
                    if not first or c >= 2:
                        pe.wait_ge(drained, fills(b, c // 2, first))
                    if first and c == 1:
                        pe.wait_ge(ternT_ready, 1)
                    for n, t in enumerate(range(*TCH[c])):
                        rows = 128 if t < KT - 1 else KR
                        last = nc.tensor.transpose(bk_[:, 128 * n:128 * n + rows], ctxN[p][0:rows, t, :], ident[0:rows, 0:rows])
                    last.then_inc(filled, 1)
                    if c == 1:
                        pe.wait_ge(xnT_ready, b + 1)
                        nc.tensor.matmul(M_ps[:, S:2 * S], w0_sb[:, :], xnT[p][:, :], start=True, stop=True).then_inc(proj_filled, 1)

            def scores(b, q, p, first):
                u = 2 * b + q
                if q == 0:
                    pe.wait_ge(projT_ready, b + 1)
                    pe.wait_ge(TA_drained, fills(b, 2, first))
                    pe.wait_ge(TB_drained, fills(b, 2, first))
                if not (first and q == 0):
                    pe.wait_ge(exp_done, u)
                for lo in range(0, K, 512):
                    hi = min(lo + 512, K)
                    last = nc.tensor.matmul(S_ps[:, lo:hi], projT[p][:, 128 * q:128 * q + 128], ctxT[p][:, lo:hi],
                                            start=True, stop=True)
                last.then_inc(S_filled, 1)

            def attend(b, q, p, bb, k0, first):
                u = 2 * b + q
                banks = ((TA, TA_filled, TA_drained), (TB, TB_filled, TB_drained))

                def transposes(c):
                    bk_, filled, drained = banks[c % 2]
                    pe.wait_ge(drained, fills(bb, k0 + c // 2, first))
                    for n, t in enumerate(range(*TCH[c])):
                        rows = 128 if t < KT - 1 else KR
                        last = nc.tensor.transpose(bk_[0:rows, 128 * n:128 * n + 128], prob[q][:, 128 * t:128 * t + rows], ident[:, :])
                    last.then_inc(filled, 1)

                def product(c):
                    pe.wait_ge(banks[c % 2][2], fills(bb, k0 + c // 2 + 1, first))
                    for t in range(*TCH[c]):
                        rows = 128 if t < KT - 1 else KR
                        last = nc.tensor.matmul(O_ps[:, 0:D], probT[0:rows, t, :], ctxN[p][0:rows, t, :], start=t == 0, stop=t == KT - 1)
                    return last

                pe.wait_ge(exp_done, u + 1)
                transposes(0)
                transposes(1)
                if not (isinstance(b, int) and b == 0 and q == 0):
                    pe.wait_ge(O_drained, u)
                product(0)
                transposes(2)
                product(1)
                transposes(3)
                product(2).then_inc(prob_used, 1)
                product(3).then_inc(O_filled, 1)

            def quantised_T(b):
                pe.wait_ge(xq_ready, b + 1)
                pe.wait_ge(projT_ready, b + 1)
                for q in range(QT):
                    last = nc.tensor.transpose(Mb[:, 128 * q:128 * q + 128], xq[:, q, :], identb[:, :])
                last.then_inc(xqT_filled, 1)

            def linear(b):
                pe.wait_ge(xqT_ready, b + 1)
                for q in range(QT):
                    last = nc.tensor.matmul(M_ps[:, S + 128 * q:S + 128 * q + 128], xqT[:, 128 * q:128 * q + 128], ternT[:, :],
                                            start=True, stop=True)
                last.then_inc(y_filled, 1)

            def body(b, p, first):
                prep(b, p, first)
                scores(b, 0, p, first)
                if not first:
                    attend(b - 1, 1, 1 - p, b, 2, first)
                scores(b, 1, p, first)
                if not first:
                    quantised_T(b - 1)
                attend(b, 0, p, b, 2 if first else 4, first)
                if not first:
                    linear(b - 1)

            pe.wait_ge(ident_ready, 2)
            pe.wait_ge(w_loaded, 16 * 15)
            body(0, 0, True)
            body(1, 1, False)
            with pe.Fori(1, B // 2) as i:
                for p in range(2):
                    body(2 * i + p, p, False)
            attend(B - 1, 1, 1, B, 0, False)
            quantised_T(B - 1)
            linear(B - 1)

            pe.wait_ge(x2_ready, B)
            pe.wait_ge(consts2_ready, 9)
            pe.wait_ge(maskF_ready, 1)
            for t in range(NT):
                last = nc.tensor.matmul(M_ps[0:B, 0:TAIL], sel15[:, B - 1 - t // QT:2 * B - 1 - t // QT], maskF[:, t, :],
                                        start=t == 0, stop=t == NT - 1)
            last.then_inc(cnt_filled, 1)
            pe.wait_ge(bad_ready, 1)
            nc.tensor.matmul(M_ps[0:1, 0:3], ones_col[:, :], bad[:, :], start=True, stop=True).then_inc(bad_filled, 1)

            pe.wait_ge(flag_ready, 1)
            general = pe.value_load(flag[0:1, 0:1])
            with pe.If(general > 0):
                pe.wait_ge(g_neg, 1)
                with pe.Fori(0, B) as b:
                    pe.wait_ge(g_loaded, 32 * b + 32)
                    for c in range(4):
                        pe.wait_ge(g_T_drained, 4 * b + (c - 1)) if c >= 2 else None
                        for n, t in enumerate(range(*TCH[c])):
                            rows = 128 if t < KT - 1 else KR
                            last = nc.tensor.transpose((TA, TB)[c % 2][:, 128 * n:128 * n + rows], ctxN[0][0:rows, t, :], ident[0:rows, 0:rows])
                        last.then_inc(g_T_filled, 1)
                    pe.wait_ge(g_xn, 2 * b + 2)
                    for q in range(QT):
                        last = nc.tensor.transpose(M_ps[:, 128 * q:128 * q + 128], xnG[:, q, :], ident[:, :])
                    last.then_inc(g_xT_filled, 1)
                    pe.wait_ge(g_xT_ready, b + 1)
                    nc.tensor.matmul(M_ps[:, 0:S], wq_sb[:, :], xnGT, start=True, stop=True).then_inc(g_q_filled, 1)
                    pe.wait_ge(g_T_drained, 4 * b + 4)
                    for lo in range(0, K, 512):
                        hi = min(lo + 512, K)
                        last = nc.tensor.matmul(S_ps[:, lo:hi], wk_sb[:, :], ctxT[0][:, lo:hi], start=True, stop=True)
                    last.then_inc(g_k_filled, 1)
                    pe.wait_ge(g_k_ready, b + 1)
                    for t in range(KT):
                        rows = 128 if t < KT - 1 else KR
                        last = nc.tensor.matmul(PS[0:rows, 128 * t:128 * t + 128], ctxT[0][:, 128 * t:128 * t + rows], wv_sb[:, :],
                                                start=True, stop=True)
                    last.then_inc(g_v_filled, 1)
                    pe.wait_ge(g_v_ready, b + 1)
                    pe.wait_ge(g_q_ready, b + 1)
                with pe.Fori(0, B) as b:
                    for q in range(QT):
                        with pe.Fori(0, H) as h:
                            u = 2 * H * b + h + H * q
                            pe.wait_ge(g_mask_ready, 2 * b + (q + 1))
                            pe.wait_ge(g_head_loaded, 64 * u + 64)
                            for lo in range(0, K, 512):
                                hi = min(lo + 512, K)
                                nc.tensor.matmul(S_ps[:, lo:hi], qhead, khead[:, lo:hi], start=True, stop=False)
                                last = nc.tensor.matmul(S_ps[:, lo:hi], negident, maskQF[:, lo:hi], start=False, stop=True)
                            last.then_inc(g_S_filled, 1)
                            pe.wait_ge(g_exp, u + 1)
                            for c in range(4):
                                if c >= 2:
                                    pe.wait_ge(g_T_drained, 4 * u + (4 * B + c - 1))
                                for n, t in enumerate(range(*TCH[c])):
                                    rows = 128 if t < KT - 1 else KR
                                    last = nc.tensor.transpose((TA, TB)[c % 2][0:rows, 128 * n:128 * n + 128],
                                                               prob[0][:, 128 * t:128 * t + rows], ident[:, :])
                                last.then_inc(g_T_filled, 1)
                            pe.wait_ge(g_T_drained, 4 * u + (4 * B + 4))
                            for t in range(KT):
                                rows = 128 if t < KT - 1 else KR
                                last = nc.tensor.matmul(O_ps[:, 0:DH], probT[0:rows, t, :], vhead[0:rows, t, :], start=t == 0, stop=t == KT - 1)
                            last.then_inc(g_O_filled, 1)
                            pe.wait_ge(g_free, u + 2)
            with pe.Else():
                def tokens_c(m, m_free):
                    pe.wait_ge(*m_free)
                    pe.wait_ge(xnC_ready, 2 * m + 2)
                    for q in range(QT):
                        last = nc.tensor.transpose(M_ps[:, 128 * q:128 * q + 128], xnC[:, q, :], ident[:, :])
                    last.then_inc(xnCT_filled, 1)

                def queries(m):
                    pe.wait_ge(xnCT_ready, m + 1)
                    nc.tensor.matmul(M_ps[:, 0:S], wq_sb[:, :], xnCT, start=True, stop=True).then_inc(q_filled, 1)

                def keys(m, p):
                    pe.wait_ge(q_ready, m + 1)
                    pe.wait_ge(keysS_ready, m + 1)
                    nc.tensor.matmul(M_ps[:, 0:TAIL], wk_sb[:, :], keysS[p], start=True, stop=True).then_inc(k_filled, 1)

                def values(n, p, m_free):
                    pe.wait_ge(*m_free)
                    for t in range(4):
                        last = nc.tensor.matmul(M_ps[0:TP, 128 * t:128 * t + 128], keysS[p][:, TP * t:TP * t + TP], wv_sb[:, :],
                                                start=True, stop=True)
                    last.then_inc(v_filled, 1)

                def scores(n, p, u):
                    if u % H == 0:
                        pe.wait_ge(aug_loaded[u // H][p], half(n, p, 208, 208))
                    if not (isinstance(n, int) and n == 0 and u < 2):
                        pe.wait_ge(S1_max, 32 * n + (u - 1))
                    h, q = u // QT, u % QT
                    nc.tensor.matmul(S1[u % 2], qaug[p][0:RN, h, 128 * q:128 * q + 128], kaug[p][0:RN, h, :],
                                     start=True, stop=True).then_inc(S1_filled, 1)

                def maxT(n):
                    pe.wait_ge(S1_max, 32 * n + 32)
                    pe.wait_ge(v_ready, n + 1)
                    for q in range(QT):
                        last = nc.tensor.transpose(M_ps[0:H, 128 * q:128 * q + 128], nm[:, H * q:H * q + H], ident[:, :])
                    last.then_inc(nmT_filled, 1)

                def scoresT(b, p, h):
                    if h == 0:
                        pe.wait_ge(nm_loaded[p], half(b, p, 48, 48))
                    if not (isinstance(b, int) and b == 0 and h < 2):
                        pe.wait_ge(P_ready, 16 * b + (h - 1))
                    for t in range(4):
                        last = nc.tensor.matmul(ST[h % 2][:, S * t:S * t + S], kaug[p][:, h, TP * t:TP * t + TP], qaug[p][:, h, :],
                                                start=True, stop=True)
                    last.then_inc(ST_filled, 1)

                def weigh(b, p, g, t):
                    if t == 0:
                        pe.wait_ge(P_ready, 16 * b + (4 * g + 4))
                        if not (isinstance(b, int) and b == 0 and g == 0):
                            pe.wait_ge(heads_ready, 4 * b + g)
                    for j in range(4):
                        h = 4 * g + j
                        last = nc.tensor.matmul(PV[32 * j:32 * j + 32, :], vaug[p][:, t, h, :], probs8[0:TP, h % 8, S * t:S * t + S],
                                                start=t == 0, stop=t == 3)
                    if t == 3:
                        last.then_inc(PV_filled, 1)

                def back(b, q, m_free):
                    pe.wait_ge(*m_free)
                    if q == 0:
                        pe.wait_ge(heads_ready, 4 * b + 4)
                    for g in range(4):
                        last = nc.tensor.transpose(M_ps[:, 128 * g:128 * g + 128], headsT[:, g, 128 * q:128 * q + 128], ident[:, :])
                    last.then_inc(back_filled, 1)

                def weigh_step(b, p, h, prev):
                    if h >= 5:
                        weigh(b, p, (h - 5) // 4, (h - 5) % 4)
                    elif prev:
                        weigh(b - 1, 1 - p, (h + 11) // 4, (h + 11) % 4)

                def body(b, p, score, prev, maxi, proj):
                    for h in range(H):
                        if score:
                            scoresT(b, p, h)
                            weigh_step(b, p, h, prev)
                        if maxi:
                            for u in UNITS[h]:
                                scores(b + 1, 1 - p, u)
                        if h == 2 and proj:
                            if isinstance(b, int) and b < 0:
                                tokens_c(b + 2, (k_ready, 1) if b == -1 else (flag_ready, 1))
                            else:
                                tokens_c(b + 2, (nm_ready, b + 1))
                        if h == 3 and proj:
                            queries(b + 2)
                        if h == 4 and proj:
                            keys(b + 2, p)
                        if h == 6 and prev:
                            back(b - 1, 0, (k_ready, b + 3) if proj else (nm_ready, B - 1) if maxi else (nm_ready, B))
                        if h == 7 and prev:
                            back(b - 1, 1, (attn_ready, 2 * b - 1))
                        if h == 9 and maxi:
                            values(b + 1, 1 - p, (attn_ready, 2 * b) if prev else (k_ready, b + 3))
                        if h == 13 and maxi:
                            maxT(b + 1)

                body(-2, 0, False, False, False, True)
                body(-1, 1, False, False, True, True)
                body(0, 0, True, False, True, True)
                body(1, 1, True, True, True, True)
                with pe.Fori(1, B // 2 - 1) as i:
                    for p in range(2):
                        body(2 * i + p, p, True, True, True, True)
                body(B - 2, 0, True, True, True, False)
                body(B - 1, 1, True, True, False, False)
                for h in range(5):
                    weigh_step(B, 0, h, True)
                back(B - 1, 0, (attn_ready, 2 * B - 2))
                back(B - 1, 1, (attn_ready, 2 * B - 1))
            pe.wait_ge(attn_ready, NT)

            def tokens_T(b, p):
                pe.wait_ge(xn3_ready, QT * b + QT)
                for q in range(QT):
                    last = nc.tensor.transpose(bank[4 + p][:, 128 * q:128 * q + 128], xn3[p][:, q, :], ident[:, :])
                last.then_inc(xn3T_filled, 1)

            def router_logits(b, p):
                pe.wait_ge(xn3T_ready, b + 1)
                if not isinstance(b, int) or b >= 2:
                    pe.wait_ge(lg_ready, b - 1)
                for q in range(QT):
                    last = nc.tensor.matmul(bank[6 + p][:, E * q:E * q + E], xn3T[p][:, 128 * q:128 * q + 128], router_sb[:, :],
                                            start=True, stop=True)
                last.then_inc(lg_filled, 1)

            def out_projection(b, p, first):
                pe.wait_ge(ao_ready, b + 1)
                for q in range(QT):
                    last = nc.tensor.transpose(bank[p][:, 128 * q:128 * q + 128], ao[p][:, q, :], ident[:, :])
                last.then_inc(aoT_filled, 1)
                if not first:
                    tokens_T(b - 1, 1 - p)
                pe.wait_ge(aoT_ready, b + 1)
                for q in range(QT):
                    last = nc.tensor.matmul(bank[2 + p][:, 128 * q:128 * q + 128], aoT[p][:, 128 * q:128 * q + 128], wo_sb[:, :],
                                            start=True, stop=True)
                last.then_inc(wo_filled, 1)
                if not first:
                    router_logits(b - 1, 1 - p)

            out_projection(0, 0, True)
            out_projection(1, 1, False)
            with pe.Fori(1, B // 2) as i:
                for p in range(2):
                    out_projection(2 * i + p, p, False)
            tokens_T(B - 1, 1)
            router_logits(B - 1, 1)

            pe.wait_ge(m12_ready, 1)
            pe.wait_ge(gconst_ready, 4)
            tiles = m12.rearrange("p (k t e) -> p k t e", t=QT, e=E)
            sums = bank[0][:, 0:2 * NT * E].rearrange("p (k t e) -> p k t e", t=QT, e=E)
            nc.tensor.matmul(bank[0][:, 0:2 * NT * E], upper, m12, start=True, stop=False)
            nc.tensor.matmul(sums[:, :, 1, :], allones, tiles[:, :, 0, :], start=False, stop=True)
            for t in range(QT):
                last = nc.tensor.matmul(bank[1][:, 0:B * E].rearrange("p (b e) -> p b e", e=E), allones, tiles[:, 0:B, t, :],
                                        start=t == 0, stop=t == QT - 1)
            last.then_inc(cum_filled, 1)

            def dispatch(b, p, again):
                pe.wait_ge(comb_ready, b + 1)
                pe.wait_ge(xs_ready, b + 1)
                if again:
                    pe.wait_ge(xT_drained, b - 1)
                for q in range(QT):
                    last = nc.tensor.matmul(bank[p], xs[p][:, q, :], disp[p][:, q, :], start=q == 0, stop=q == QT - 1)
                last.then_inc(xT_filled, 1)
                for half_bank, filled, drained in ((0, cA_filled, cA_drained), (1, cB_filled, cB_drained)):
                    if again:
                        pe.wait_ge(drained, b - 1)
                    for c in range(2):
                        for q in range(QT):
                            ch = 2 * half_bank + c
                            last = nc.tensor.transpose(bank[2 + 2 * p + half_bank][:, S * c + 128 * q:S * c + 128 * q + 128],
                                                       comb[p][:, q, 128 * ch:128 * ch + 128], ident[:, :])
                    last.then_inc(filled, 1)

            dispatch(0, 0, False)
            dispatch(1, 1, False)
            with pe.Fori(1, B // 2) as i:
                for p in range(2):
                    dispatch(2 * i + p, p, True)

            def down(e, c, p):
                rows = HROWS[c]
                pe.wait_ge(hid_ready, HC * e + (c + 1))
                if c == 0 and (not isinstance(e, int) or e >= 2):
                    pe.wait_ge(eoT_ready, e - 1)
                ins = nc.tensor.matmul(bank[4 + p], woe[p][0:rows, c, :], hid[c % 2][0:rows, :], start=c == 0, stop=c == HC - 1)
                ins.then_inc(eo_filled if c == HC - 1 else hid_used, 1)

            def expert(e, p, first):
                pe.wait_ge(wts_loaded[p], half(e, p, 64, 64))
                rhs = xT[:, ds(e, 1), :].rearrange("p a n -> p (a n)")
                for c in range(HC):
                    rows = HROWS[c]
                    if not (first and c < 2):
                        pe.wait_ge(gelu_done, HC * e + (c - 1))
                    nc.tensor.matmul(bank[c % 2][0:rows, :], w0e[p][:, HLO[c]:HLO[c] + rows], rhs, start=True, stop=True).then_inc(a_filled, 1)
                    if not (first and c < 2):
                        pe.wait_ge(hid_ready, HC * e + (c - 1))
                    nc.tensor.matmul(bank[2 + c % 2][0:rows, :], w1e[p][:, HLO[c]:HLO[c] + rows], rhs, start=True, stop=True).then_inc(b_filled, 1)
                    if c > 0:
                        down(e, c - 1, p)
                    elif not first:
                        down(e - 1, HC - 1, 1 - p)

            pe.wait_ge(xT_drained, B)
            pe.wait_ge(cA_drained, B)
            pe.wait_ge(cB_drained, B)
            expert(0, 0, True)
            expert(1, 1, False)
            with pe.Fori(1, E // 2) as i:
                for p in range(2):
                    expert(2 * i + p, p, False)
            down(E - 1, HC - 1, 1)

            def back_T(g, p):
                pe.wait_ge(outT_ready, g + 1)
                if not isinstance(g, int) or g >= 2:
                    pe.wait_ge(x4_ready, g - 1)
                for q in range(QT):
                    last = nc.tensor.transpose(bank[4 + p][:, 128 * q:128 * q + 128], outT[p][:, 128 * q:128 * q + 128], ident[:, :])
                last.then_inc(y_back_filled, 1)

            def combine(g, p, first):
                pe.wait_ge(eoS_ready, g + 1)
                if not isinstance(g, int) or g >= 2:
                    pe.wait_ge(eo_ready, g - 1)
                for ch in range(E * CAP // 128):
                    last = nc.tensor.transpose(bank[p][:, 128 * ch:128 * ch + 128],
                                               eoS[p][:, 2 * ch:2 * ch + 2, :].rearrange("p e c -> p (e c)"), ident[:, :])
                last.then_inc(eoX_filled, 1)
                if not first:
                    back_T(g - 1, 1 - p)
                pe.wait_ge(eo_ready, g + 1)
                for ch in range(E * CAP // 128):
                    last = nc.tensor.matmul(bank[2 + p][:, 0:S], eo[p][:, ch, :],
                                            combT[:, ds(g, 1), S * ch:S * ch + S].rearrange("p a n -> p (a n)"),
                                            start=ch == 0, stop=ch == E * CAP // 128 - 1)
                last.then_inc(outT_filled, 1)

            pe.wait_ge(eoT_ready, E)
            combine(0, 0, True)
            combine(1, 1, False)
            with pe.Fori(1, B // 2) as i:
                for p in range(2):
                    combine(2 * i + p, p, False)
            back_T(B - 1, 1)



_INS = ["x", "ctx_1024", "mask_Bx1xSxS2_bk1", "g_xattn", "g_ffn", "L0_xattn_W", "L0_xattn_b", "L0_ffn_packed_weight",
        "L0_ffn_weight_scale", "L0_ffn_bias", "L1_xattn_w_q", "L1_xattn_b_q", "L1_xattn_w_k", "L1_xattn_b_k",
        "L1_xattn_w_v", "L1_xattn_b_v", "L1_xattn_w_o", "L1_xattn_b_o", "L1_ffn_router_w", "L1_ffn_w0_kernel",
        "L1_ffn_w1_kernel", "L1_ffn_wo_kernel"]


def kernel(**inputs):
    import numpy as _np
    import concourse.bacc as _bacc
    from concourse import mybir as _mybir
    from concourse.bass_utils import run_bass_kernel_spmd as _run

    nc = _bacc.Bacc("TRN2", target_bir_lowering=False, num_devices=1)
    arrays, args = {}, []
    for name in _INS:
        a = _np.ascontiguousarray(inputs[name])
        arrays[f"in_{name}_dram"] = a
        args.append(nc.dram_tensor(f"in_{name}_dram", a.shape, _mybir.dt.from_np(a.dtype), kind="ExternalInput").ap())
    shape = _np.shape(inputs["x"])
    args.append(nc.dram_tensor("out_0_dram", shape, _mybir.dt.float32, kind="ExternalOutput").ap())
    build(nc, *args)
    r = _run(nc, [arrays], core_ids=[0])
    return r.results[0]["out_0_dram"]
```

```python
from contextlib import ExitStack

import concourse.bass as bass
from concourse import mybir


class Tally:

    def __init__(self, eng, sem):
        self.eng, self.sem, self.n, self.base = eng, sem, 0, 0

    def mark(self, ins):
        ins.then_inc(self.sem, 1)
        self.n += 1
        return self.base + self.n

    def link(self, ins):
        self.eng.wait_ge(self.sem, self.mark(ins))

    def loop(self, start, end, per):
        with self.eng.Fori(start, end) as i:
            n0 = self.n
            self.base = (i - start) * per if start else i * per
            yield i
            assert self.n - n0 == per, (self.n - n0, per)
            self.base = 0
            self.n = n0
        self.n = n0 + per * (end - start)


def build(nc, x, ctx_in, mask, g_xattn, g_ffn, w0, b0, packed, wscale, fbias,
          wq, bq, wk, bk, wv, bv, wo, bo, router, we0, we1, weo, out):
    fp32, bf16 = mybir.dt.float32, mybir.dt.bfloat16
    i32, u8 = mybir.dt.int32, mybir.dt.uint8
    ALU, ACT, AX = mybir.AluOpType, mybir.ActivationFunctionType, mybir.AxisListType
    ds = bass.ds

    B, S, D = x.shape
    K = ctx_in.shape[1]
    QT = S // 128
    NT = B * QT
    KT = -(-K // 128)
    KR = K - 128 * (KT - 1)
    H = 16
    DH = D // H
    TAIL = (K - 1) // 4
    T0 = K - TAIL
    TP = TAIL // 4
    E = router.shape[1]
    CAP = 64
    HID = we0.shape[2]
    HC = -(-HID // 128)
    HR = (HID - 128 * (HC - 2)) // 2
    HROWS = [128] * (HC - 2) + [HR] * 2
    HLO = [sum(HROWS[:c]) for c in range(HC)]
    EPS = 1e-5
    ONES = 1.0 + 0x3F80 / 2 ** 23
    MAGIC = 1.5 * 2.0 ** 23
    NEG = -2.0 ** 100
    NPROD = 6
    RUNS = ((0, 3), (3, 2), (5, 1))
    RS = NPROD * DH
    RM = RS + 1
    RA = 128
    RN = RA - 3

    EARLY = 9
    PER_STEP = (2, 2, 2, 2, 2, 2, 2, 2, 2, 2, 3, 0, 0, 3, 3, 3)
    MAX_STEP = 11
    assert sum(PER_STEP[:MAX_STEP]) == QT * H - EARLY and sum(PER_STEP) == QT * H
    UNITS = [[(0, u) if u < QT * H else (1, u - QT * H) for u in
              range(EARLY + sum(PER_STEP[:h]), EARLY + sum(PER_STEP[:h + 1]))] for h in range(H)]

    stack = ExitStack()
    with stack:
        def sb(name, shape, dt=fp32):
            return stack.enter_context(nc.sbuf_tensor(name, shape, dt))

        def sem(name):
            return stack.enter_context(nc.semaphore(name))

        ident = sb("ident", [128, 128])
        identb = sb("identb", [128, 128], bf16)
        w0_sb, wq_sb, wk_sb, wv_sb, wo_sb = (sb(n, [128, 128]) for n in ("w0_sb", "wq_sb", "wk_sb", "wv_sb", "wo_sb"))
        router_sb = sb("router_sb", [128, E])
        b0_col, bq_col, bk_col = (sb(n, [128, 1]) for n in ("b0_col", "bq_col", "bk_col"))
        fb_row, bv_row, bo_row = (sb(n, [128, 128]) for n in ("fb_row", "bv_row", "bo_row"))
        gates = sb("gates", [128, 4])
        gates_in = sb("gates_in", [128, 4])
        ws_col = sb("ws_col", [128, 1])
        packed_sb = sb("packed_sb", [128, 128], i32)
        tern_i = sb("tern_i", [128, 128], i32)
        tern = sb("tern", [128, 128], bf16)
        ternT = sb("ternT", [128, 128], bf16)
        neghalf = sb("neghalf", [128, NT])
        eps = sb("eps", [128, NT])
        zero = sb("zero", [128, 1])
        zero_col = zero[:, :]
        dve_slot = sb("dve_slot", [128, 1])

        x_sb = sb("x_sb", [128, NT, D])
        keysT = sb("keysT", [128, B, TAIL])
        stats = sb("stats", [128, NT, 6])
        meanvar = sb("meanvar", [128, NT, 2])
        vareps = sb("vareps", [128, NT])
        rstd = sb("rstd", [128, NT])

        class Carver:
            def __init__(self, handle):
                self.handle, self.at = handle, 0

            def take(self, shape, dt=fp32):
                n = 1
                for k in shape[1:]:
                    n *= k
                words = -(-n * (2 if dt == bf16 else 1 if dt == u8 else 4) // 4)
                v = self.handle[0:shape[0], self.at:self.at + words]
                self.at += words
                assert self.at <= self.handle.shape[1], self.at
                if dt != fp32:
                    v = v.bitcast(dt)[:, 0:n]
                if len(shape) == 3:
                    v = v.rearrange("p (a b) -> p a b", a=shape[1])
                if len(shape) == 4:
                    v = v.rearrange("p (a b c) -> p a b c", a=shape[1], b=shape[2])
                return v

        low, high = sb("low", [128, 14400]), sb("high", [128, 29000])

        one = Carver(low)
        ctxN, ctxT, prob = [None] * 2, [None] * 2, [None] * 2
        ctxN[1], ctxT[1], prob[1] = one.take([128, KT, D]), one.take([128, K]), one.take([128, K])
        ctxN[0], ctxT[0], prob[0] = one.take([128, KT, D]), one.take([128, K]), one.take([128, K])
        probT = one.take([128, KT, 128])
        xn = [one.take([128, QT, D]) for p in range(2)]
        xnT = [one.take([128, S]) for p in range(2)]
        projT = [one.take([128, S]) for p in range(2)]
        x1 = [one.take([128, QT, D]) for p in range(2)]
        xnB, yB = one.take([128, QT, D]), one.take([128, QT, D])
        xq, xqT = one.take([128, QT, D], bf16), one.take([128, S], bf16)
        nmax, rsum = sb("nmax", [128, NT]), sb("rsum", [128, NT])
        rgate = sb("rgate", [128, 2])
        statsB, mvB = sb("statsB", [128, QT, 6]), sb("mvB", [128, QT, 2])
        veB, rstdB = sb("veB", [128, QT]), sb("rstdB", [128, QT])
        ve3 = [sb(f"ve3_{p}", [128, QT]) for p in range(2)]
        mv3, rstd3 = [sb(f"mv3_{p}", [128, QT, 2]) for p in range(2)], [sb(f"rstd3_{p}", [128, QT]) for p in range(2)]
        amax, qscale, dscale = (sb(n, [128, QT]) for n in ("amax", "qscale", "dscale"))

        two = Carver(high)
        attn = two.take([128, NT, D])
        at_mask = two.at
        probs8 = two.take([128, 8, 4 * S])
        two.at = max(two.at, at_mask + (NT * (T0 - 1) + 3) // 4 + (NT * (TAIL + 1) + 3) // 4 + NT * TAIL // 2 + 8)
        kaug = [two.take([RA, H, TAIL], bf16) for p in range(2)]
        qaug = [two.take([RA, H, S], bf16) for p in range(2)]
        kaug_words, qaug_words = ([t[p].rearrange("p h k -> p (h k)").bitcast(fp32) for p in range(2)] for t in (kaug, qaug))
        vaug = [two.take([TP, 4, H, 32]) for p in range(2)]
        two = Carver(low)
        two.at = KT * D + 2 * K
        headsT = two.take([128, 4, S])
        keysS = [two.take([128, TAIL]) for p in range(2)]
        xnC, xnCT = two.take([128, QT, D]), two.take([128, S])
        qf, kf = two.take([128, S]), two.take([128, TAIL])
        qres, kres = two.take([128, S]), two.take([128, TAIL])
        qpart = [two.take([128, 3, S], bf16) for p in range(2)]
        kpart = [two.take([128, 3, TAIL], bf16) for p in range(2)]
        nm = [two.take([128, QT * H]) for p in range(2)]
        nmres = two.take([H, S])
        nmpart = [two.take([H, 3, S], bf16) for p in range(2)]
        rden = two.take([128, H])
        chk = Carver(high)
        chk.at = at_mask
        maskA = chk.take([128, NT, T0 - 1], u8)
        maskB = chk.take([128, NT, TAIL + 1], u8)
        maskF = chk.take([128, NT, TAIL], bf16)
        maskpair, maskmin = sb("maskpair", [128, 1]), sb("maskmin", [128, 1])
        bad = sb("bad", [128, 3])
        sel15 = sb("sel15", [128, 2 * B - 1], bf16)
        cnt, cntv = sb("cnt", [B, TAIL]), sb("cntv", [B, TAIL])
        cmin = sb("cmin", [B, 2])
        maskrow = sb("maskrow", [B, TAIL], bf16)
        ones_col = sb("ones_col", [128, 1])
        badsum = sb("badsum", [1, 1])
        flag = sb("flag", [1, 1], i32)
        q_dram = [nc.dram_tensor(f"q_parts{p}", [H * DH, NPROD, S], bf16).ap() for p in range(2)]
        k_dram = [nc.dram_tensor(f"k_parts{p}", [H * DH, NPROD, TAIL], bf16).ap() for p in range(2)]
        maskrow_dram = nc.dram_tensor("mask_rows", [B, TAIL], bf16).ap()

        gen = Carver(high)
        gen.at = at_mask
        maskQ, maskQF = gen.take([128, K], u8), gen.take([128, K], bf16)
        khead, qhead, vhead = gen.take([DH, K]), gen.take([DH, 128]), gen.take([128, KT, DH])
        negident = gen.take([128, 128], bf16)
        xnG, xnGT, qG = gen.take([128, QT, D]), gen.take([128, S]), gen.take([128, S])
        grecip, gmax, gsum = gen.take([128, 1]), gen.take([128, 1]), gen.take([128, 1])
        q_all = nc.dram_tensor("q_all", [B, QT, D, 128], fp32).ap()
        k_all = nc.dram_tensor("k_all", [B, D, K], fp32).ap()
        v_all = nc.dram_tensor("v_all", [B, K, D], fp32).ap()

        wts = Carver(low)
        w0e, w1e, woe = [None] * 2, [None] * 2, [None] * 2
        for p in range(2):
            w0e[p], w1e[p], woe[p] = wts.take([128, HID]), wts.take([128, HID]), wts.take([128, HC, D])
        tri = Carver(low)
        tri.at = KT * D + 2 * K
        ao = [tri.take([128, QT, D]) for p in range(2)]
        aoT = [tri.take([128, S]) for p in range(2)]
        x3t = tri.take([128, QT, D])
        xn3 = [tri.take([128, QT, D]) for p in range(2)]
        xn3T = [tri.take([128, S]) for p in range(2)]
        eoT = tri.take([128, E, B * CAP])
        comb2 = [tri.take([128, QT, E * CAP]) for p in range(2)]
        fin = Carver(high)
        fin.at = at_mask
        combT = fin.take([128, B, E * CAP // 128 * S])
        xT = fin.take([128, E, B * CAP])
        xn_all = fin.take([128, NT, D])
        iota_slot = fin.take([128, E * CAP])
        comb = [fin.take([128, QT, E * CAP]) for p in range(2)]
        disp = [fin.take([128, QT, E * CAP]) for p in range(2)]
        xs = [fin.take([128, QT, D]) for p in range(2)]
        gl = [fin.take([128, B * CAP]) for p in range(2)]
        hid = [fin.take([128, B * CAP]) for p in range(2)]
        eoS = [fin.take([128, E, CAP]) for p in range(2)]
        eo = [fin.take([128, E * CAP // 128, 128]) for p in range(2)]
        outT = [fin.take([128, S]) for p in range(2)]
        iota_e, logits, shifted, expd, raw, equal, cand, m1, m2, rest, pos1, pos2, kept, work = (
            fin.take([128, NT, E]) for _ in range(14))
        m12 = fin.take([128, 2 * NT * E], bf16)
        count1 = fin.take([128, B, E])
        upper, allones = fin.take([128, 128], bf16), fin.take([128, 128], bf16)
        gmx, gate1, gate2, least1, least2, keep1, keep2, place1, place2, slot1, slot2 = (fin.take([128, NT]) for _ in range(11))

        PS = stack.enter_context(nc.psum_tensor("PS", [128, 4096], fp32))
        bank = [PS[:, 512 * i:512 * i + 512] for i in range(8)]
        S_ps, TA, TB, O_ps, M_ps = PS[:, 0:K], bank[4], bank[5], bank[6], bank[7]
        Mb = M_ps.bitcast(bf16)

        x_loaded, xrest_loaded, w_loaded, ternary_loaded = sem("x_loaded"), sem("xrest_loaded"), sem("w_loaded"), sem("ternary_loaded")
        first_loaded = sem("first_loaded")
        ctx_loaded = [sem(f"ctx_loaded{p}") for p in range(2)]
        ident_ready, gates_ready = sem("ident_ready"), sem("gates_ready")
        tern_ready, ternT_filled, ternT_ready = sem("tern_ready"), sem("ternT_filled"), sem("ternT_ready")
        ln_stats, rstd_ready = sem("ln_stats"), sem("rstd_ready")
        xn_ready, xnT_filled, xnT_ready = sem("xn_ready"), sem("xnT_filled"), sem("xnT_ready")
        proj_filled, projT_ready = sem("proj_filled"), sem("projT_ready")
        TA_filled, TA_drained = sem("TA_filled"), sem("TA_drained")
        TB_filled, TB_drained = sem("TB_filled"), sem("TB_drained")
        keys_saved = sem("keys_saved")
        S_filled, max_done, exp_done, prob_used = sem("S_filled"), sem("max_done"), sem("exp_done"), sem("prob_used")
        O_filled, O_drained = sem("O_filled"), sem("O_drained")
        statsB_ready, rstdB_ready = sem("statsB_ready"), sem("rstdB_ready")
        xq_ready, xqT_filled, xqT_ready = sem("xq_ready"), sem("xqT_filled"), sem("xqT_ready")
        y_filled, x2_ready = sem("y_filled"), sem("x2_ready")
        out_stored = sem("out_stored")
        maskA_loaded, maskB_loaded, cnt_read = sem("maskA_loaded"), sem("maskB_loaded"), sem("cnt_read")
        small_ready, consts2_ready = sem("small_ready"), sem("consts2_ready")
        weights_ready = sem("weights_ready")
        cnt_filled, bad_ready, bad_filled, flag_ready = sem("cnt_filled"), sem("bad_ready"), sem("bad_filled"), sem("flag_ready")
        maskrow_ready, maskrow_saved = sem("maskrow_ready"), sem("maskrow_saved")
        keysS_ready = sem("keysS_ready")
        lnC_stats, rstdC_ready, xnC_ready = sem("lnC_stats"), sem("rstdC_ready"), sem("xnC_ready")
        xnCT_filled, xnCT_ready = sem("xnCT_filled"), sem("xnCT_ready")
        q_filled, q_ready, k_filled, k_ready = sem("q_filled"), sem("q_ready"), sem("k_filled"), sem("k_ready")
        v_filled, v_ready = sem("v_filled"), sem("v_ready")
        q_parts_ready, k_parts_ready = sem("q_parts_ready"), sem("k_parts_ready")
        parts_saved = [sem(f"parts_saved{p}") for p in range(2)]
        aug_loaded = [[sem(f"aug{c}_loaded{p}") for p in range(2)] for c in range(2)]
        S1_filled, S1_max = sem("S1_filled"), sem("S1_max")
        nmT_filled, nm_ready = sem("nmT_filled"), sem("nm_ready")
        nm_loaded = [sem(f"nm_loaded{p}") for p in range(2)]
        ST_filled, P_ready = sem("ST_filled"), sem("P_ready")
        PV_filled, heads_ready, back_filled, attn_ready = sem("PV_filled"), sem("heads_ready"), sem("back_filled"), sem("attn_ready")
        g_loaded, g_stats, g_rstd, g_xn = sem("g_loaded"), sem("g_stats"), sem("g_rstd"), sem("g_xn")
        g_T_filled, g_T_drained = sem("g_T_filled"), sem("g_T_drained")
        g_xT_filled, g_xT_ready = sem("g_xT_filled"), sem("g_xT_ready")
        g_q_filled, g_q_ready, g_k_filled, g_k_ready = sem("g_q_filled"), sem("g_q_ready"), sem("g_k_filled"), sem("g_k_ready")
        g_v_filled, g_v_ready, g_saved = sem("g_v_filled"), sem("g_v_ready"), sem("g_saved")
        g_neg, g_mask_loaded, g_mask_ready, g_head_loaded = sem("g_neg"), sem("g_mask_loaded"), sem("g_mask_ready"), sem("g_head_loaded")
        g_S_filled, g_max, g_exp, g_O_filled, g_free = sem("g_S_filled"), sem("g_max"), sem("g_exp"), sem("g_O_filled"), sem("g_free")
        g_S_free = sem("g_S_free")
        wts_loaded = [sem(f"wts_loaded{p}") for p in range(2)]
        ao_ready, aoT_filled, aoT_ready, wo_filled = sem("ao_ready"), sem("aoT_filled"), sem("aoT_ready"), sem("wo_filled")
        x3_read, x3_stats, x3_rstd, xn3_ready = sem("x3_read"), sem("x3_stats"), sem("x3_rstd"), sem("xn3_ready")
        xn3_saved, xn3T_filled, xn3T_ready = sem("xn3_saved"), sem("xn3T_filled"), sem("xn3T_ready")
        lg_filled, lg_ready, gconst_ready = sem("lg_filled"), sem("lg_ready"), sem("gconst_ready")
        shifted_ready, expd_ready, m12_ready, cum_filled = sem("shifted_ready"), sem("expd_ready"), sem("m12_ready"), sem("cum_filled")
        xs_ready, comb_ready = sem("xs_ready"), sem("comb_ready")
        xT_filled, xT_drained = sem("xT_filled"), sem("xT_drained")
        cA_filled, cA_drained, cB_filled, cB_drained = sem("cA_filled"), sem("cA_drained"), sem("cB_filled"), sem("cB_drained")
        a_filled, b_filled, gelu_done, hid_ready = sem("a_filled"), sem("b_filled"), sem("gelu_done"), sem("hid_ready")
        hid_used, eo_filled, eoT_ready = sem("hid_used"), sem("eo_filled"), sem("eoT_ready")
        eoS_ready, eoX_filled, eo_ready = sem("eoS_ready"), sem("eoX_filled"), sem("eo_ready")
        outT_filled, outT_ready, y_back_filled, x4_ready = sem("outT_filled"), sem("outT_ready"), sem("y_back_filled"), sem("x4_ready")
        dve_gen, dve_late, pool_late = sem("dve_gen"), sem("dve_late"), sem("pool_late")
        dve_fast, pool_fast = sem("dve_fast"), sem("pool_fast")
        dve_order, pool_order = sem("dve_order"), sem("pool_order")

        S1 = [bank[0][:, 0:TAIL], bank[1][:, 0:TAIL]]
        ST = [PS[0:TP, 1024 * (1 + j):1024 * (2 + j)] for j in range(2)]
        PV = bank[6][:, 0:S]

        TCH = [(0, 4), (4, 8), (8, 12), (12, KT)]

        def fills(b, k, first):
            return k if first else 6 * b + (k - 2)

        def half(n, p, per, more):
            return per * (n // 2) + more if isinstance(n, int) else (per // 2) * n + (more - per // 2 * p)

        block = stack.enter_context(nc.Block())

        @block.sync
        def _(sp):
            sp.dma_start(x_sb[:, 0:2, :], x.rearrange("b (t p) d -> p (b t) d", p=128)[:, 0:2, :]).then_inc(x_loaded, 16)

            def load_ctx(b, p):
                src = ctx_in[b, :, :] if isinstance(b, int) else ctx_in[ds(b, 1), :, :].rearrange("a k d -> (a k) d")
                sp.dma_start(ctxN[p][:, 0:KT - 1, :],
                             src[0:128 * (KT - 1), :].rearrange("(t p) d -> p t d", p=128)).then_inc(ctx_loaded[p], 16)
                sp.dma_start(ctxN[p][0:KR, KT - 1, :], src[128 * (KT - 1):K, :]).then_inc(ctx_loaded[p], 16)

            load_ctx(0, 0)
            sp.dma_start(x_sb[:, 2:NT, :], x.rearrange("b (t p) d -> p (b t) d", p=128)[:, 2:NT, :]).then_inc(xrest_loaded, 16)
            load_ctx(1, 1)
            with sp.Fori(1, B // 2) as i:
                for p in range(2):
                    sp.wait_ge(O_filled, 4 * i + (2 * p - 2))
                    load_ctx(2 * i + p, p)
            sp.wait_ge(maskrow_ready, 1)
            sp.dma_start(maskrow_dram, maskrow[:, :]).then_inc(maskrow_saved, 16)
            sp.wait_ge(maskrow_saved, 16)

            def save_parts(m, p):
                sp.wait_ge(k_parts_ready, m + 1)
                for n, (g, many) in enumerate(RUNS):
                    sp.dma_start(k_dram[p][:, g:g + many, :],
                                 kpart[p][:, n:n + 1, :].to_broadcast([128, many, TAIL])).then_inc(parts_saved[p], 16)
                sp.wait_ge(q_parts_ready, m + 1)
                for g, many in RUNS:
                    sp.dma_start(q_dram[p][:, g:g + many, :],
                                 qpart[p][:, 0:many, :]).then_inc(parts_saved[p], 16)
                sp.wait_ge(parts_saved[p], half(m, p, 96, 96))

            def load_aug(m, p, c):
                heads, loaded = slice(8 * c, 8 * c + 8), aug_loaded[c][p]
                sp.dma_start(qaug[p][0:RS, heads, :],
                             q_dram[p].rearrange("(h d) g q -> (d g) h q", d=DH)[:, heads, :]).then_inc(loaded, 16)
                sp.dma_start(kaug[p][0:RS, heads, :],
                             k_dram[p].rearrange("(h d) g q -> (d g) h q", d=DH)[:, heads, :]).then_inc(loaded, 16)
                row = maskrow_dram[m:m + 1, :] if isinstance(m, int) else maskrow_dram[ds(m, 1), :]
                sp.dma_start(kaug[p][RS:RM, heads, :],
                             row.unsqueeze(1).to_broadcast([1, H // 2, TAIL])).then_inc(loaded, 16)

            def serve(b, p):
                save_parts(b + 2, p)
                if not isinstance(b, int) or b >= 0:
                    sp.wait_ge(ST_filled, 16 * b + 8)
                load_aug(b + 2, p, 0)
                if not isinstance(b, int) or b >= 0:
                    sp.wait_ge(ST_filled, 16 * b + 16)
                load_aug(b + 2, p, 1)

            sp.wait_ge(flag_ready, 1)
            general = sp.value_load(flag[0:1, 0:1])
            with sp.If(general > 0):
                def load_batch(b):
                    src = ctx_in[b, :, :] if isinstance(b, int) else ctx_in[ds(b, 1), :, :].rearrange("a k d -> (a k) d")
                    sp.dma_start(ctxN[0][:, 0:KT - 1, :],
                                 src[0:128 * (KT - 1), :].rearrange("(t p) d -> p t d", p=128)).then_inc(g_loaded, 16)
                    sp.dma_start(ctxN[0][0:KR, KT - 1, :], src[128 * (KT - 1):K, :]).then_inc(g_loaded, 16)

                def save_batch(b):
                    sp.wait_ge(g_q_ready, b + 1)
                    sp.dma_start(q_all[b:b + 1, :, :, :].rearrange("a q r s -> r (a q) s") if isinstance(b, int) else
                                 q_all[ds(b, 1), :, :, :].rearrange("a q r s -> r (a q) s"),
                                 qG.rearrange("r (q s) -> r q s", q=QT)).then_inc(g_saved, 16)
                    sp.wait_ge(g_k_ready, b + 1)
                    sp.dma_start(k_all[b, :, :] if isinstance(b, int) else k_all[ds(b, 1), :, :].rearrange("a r k -> (a r) k"),
                                 prob[0]).then_inc(g_saved, 16)
                    sp.wait_ge(g_v_ready, b + 1)
                    dst = v_all[b, :, :] if isinstance(b, int) else v_all[ds(b, 1), :, :].rearrange("a k d -> (a k) d")
                    sp.dma_start(dst[0:128 * (KT - 1), :].rearrange("(t p) d -> p t d", p=128),
                                 ctxN[0][:, 0:KT - 1, :]).then_inc(g_saved, 16)
                    sp.dma_start(dst[128 * (KT - 1):K, :], ctxN[0][0:KR, KT - 1, :]).then_inc(g_saved, 16)

                load_batch(0)
                with sp.Fori(1, B) as b:
                    save_batch(b - 1)
                    sp.wait_ge(g_saved, 64 * b)
                    load_batch(b)
                save_batch(B - 1)
                sp.wait_ge(g_saved, 64 * B)
                with sp.Fori(0, B) as b:
                    for q in range(QT):
                        with sp.Fori(0, H) as h:
                            sp.wait_ge(g_free, 2 * H * b + h + (H * q + 1))
                            sp.dma_start(qhead, q_all.rearrange("b q (h d) s -> (b q h) d s", d=DH)[ds(2 * H * b + h + H * q, 1), :, :]
                                         .rearrange("a d s -> (a d) s")).then_inc(g_head_loaded, 16)
                            sp.dma_start(khead, k_all.rearrange("b (h d) k -> (b h) d k", d=DH)[ds(H * b + h, 1), :, :]
                                         .rearrange("a d k -> (a d) k")).then_inc(g_head_loaded, 16)
                            vh = v_all[ds(b, 1), :, ds(DH * h, DH)].rearrange("a k d -> (a k) d")
                            sp.dma_start(vhead[:, 0:KT - 1, :],
                                         vh[0:128 * (KT - 1), :].rearrange("(t p) d -> p t d", p=128)).then_inc(g_head_loaded, 16)
                            sp.dma_start(vhead[0:KR, KT - 1, :], vh[128 * (KT - 1):K, :]).then_inc(g_head_loaded, 16)
            with sp.Else():
                serve(-2, 0)
                serve(-1, 1)
                serve(0, 0)
                serve(1, 1)
                with sp.Fori(1, B // 2 - 1) as i:
                    for p in range(2):
                        serve(2 * i + p, p)

            def load_expert(e, p):
                def of(w):
                    return w[e, :, :] if isinstance(e, int) else w[ds(e, 1), :, :].rearrange("a m h -> (a m) h")
                sp.dma_start(w0e[p], of(we0)).then_inc(wts_loaded[p], 16)
                sp.dma_start(w1e[p], of(we1)).then_inc(wts_loaded[p], 16)
                sp.dma_start(woe[p][:, 0:HC - 2, :],
                             of(weo)[0:128 * (HC - 2), :].rearrange("(t p) d -> p t d", p=128)).then_inc(wts_loaded[p], 16)
                sp.dma_start(woe[p][0:HR, HC - 2:HC, :],
                             of(weo)[128 * (HC - 2):HID, :].rearrange("(t p) d -> p t d", p=HR)).then_inc(wts_loaded[p], 16)

            load_expert(0, 0)
            load_expert(1, 1)
            with sp.Fori(1, E // 2) as i:
                for p in range(2):
                    sp.wait_ge(eo_filled, 2 * i + (p - 1))
                    load_expert(2 * i + p, p)
            out_t = out.rearrange("b (t p) d -> p (b t) d", p=128)
            with sp.Fori(0, B) as b:
                sp.wait_ge(x4_ready, b + 1)
                sp.dma_start(out_t[:, ds(QT * b, QT), :], x_sb[:, ds(QT * b, QT), :]).then_inc(out_stored, 16)
            sp.wait_ge(out_stored, 16 * B)

        @block.gpsimd
        def _(pool):
            order = Tally(pool, pool_order)
            order.link(nc.gpsimd.memset(ident[:, :], 0.0))
            order.link(nc.gpsimd.affine_select(out=ident[:, :], in_=ident[:, :], compare_op=ALU.not_equal, fill=1.0,
                                               base=0, pattern=[[-1, 128]], channel_multiplier=1))
            nc.gpsimd.memset(eps[:, :], EPS)
            nc.gpsimd.memset(zero[:, :], 0.0)
            nc.gpsimd.memset(neghalf[:, :], -0.5).then_inc(ident_ready, 1)
            nc.gpsimd.tensor_copy(identb[:, :], ident[:, :]).then_inc(ident_ready, 1)
            pool.wait_ge(ident_ready, 2)
            def rstd_x(k, lo, hi):
                pool.wait_ge(ln_stats, k + 1)
                order.link(nc.gpsimd.tensor_scalar(vareps[:, lo:hi], meanvar[:, lo:hi, 1], EPS, None, ALU.add))
                nc.gpsimd.tensor_tensor(rstd[:, lo:hi], vareps[:, lo:hi], neghalf[:, lo:hi], ALU.pow).then_inc(rstd_ready, 1)

            rstd_x(0, 0, 2)
            nc.gpsimd.memset(ones_col[:, :], 1.0).then_inc(small_ready, 1)
            nc.gpsimd.memset(bad[:, :], 0.0).then_inc(small_ready, 1)
            order.link(nc.gpsimd.memset(sel15[:, :], 0.0))
            nc.gpsimd.memset(sel15[:, B - 1:B], 1.0).then_inc(small_ready, 1)
            for p in range(2):
                order.link(nc.gpsimd.memset(qaug_words[p], ONES))
                nc.gpsimd.affine_select(out=qaug_words[p], in_=qaug_words[p], compare_op=ALU.is_ge, fill=0.0,
                                        base=RM - 1, pattern=[[0, H * S // 2]], channel_multiplier=-1).then_inc(consts2_ready, 1)
                order.link(nc.gpsimd.memset(vaug[p], 0.0))
                nc.gpsimd.memset(vaug[p][:, :, :, DH:DH + 1], 1.0).then_inc(consts2_ready, 1)
            pool.wait_ge(maskB_loaded, 16)
            nc.gpsimd.tensor_copy(maskF[:, 0:NT // 2, :], maskB[:, 0:NT // 2, 1:TAIL + 1]).then_inc(small_ready, 1)
            rstd_x(1, 2, NT)
            nc.gpsimd.tensor_copy(maskF[:, NT // 2:NT, :], maskB[:, NT // 2:NT, 1:TAIL + 1]).then_inc(small_ready, 1)

            def save_keys(b, p, first):
                pool.wait_ge(TA_drained, fills(b, 2, first))
                pool.wait_ge(TB_drained, fills(b, 2, first))
                nc.gpsimd.tensor_copy(keysT[:, b, :] if isinstance(b, int) else keysT[:, ds(b, 1), :].rearrange("p a k -> p (a k)"),
                                      ctxT[p][:, T0:K]).then_inc(keys_saved, 1)

            def rstd_b(b):
                pool.wait_ge(statsB_ready, b + 1)
                order.link(nc.gpsimd.tensor_tensor(veB[:, :], mvB[:, :, 1], eps[:, 0:QT], ALU.add))
                nc.gpsimd.tensor_tensor(rstdB[:, :], veB[:, :], neghalf[:, 0:QT], ALU.pow).then_inc(rstdB_ready, 1)

            save_keys(0, 0, True)
            save_keys(1, 1, False)
            rstd_b(0)
            for i in order.loop(1, B // 2, 2):
                for p in range(2):
                    save_keys(2 * i + p, p, False)
                    rstd_b(2 * i + (p - 1))
            rstd_b(B - 1)

            pool.wait_ge(flag_ready, 1)
            general = pool.value_load(flag[0:1, 0:1])
            with pool.If(general > 0):
                nc.gpsimd.tensor_scalar(negident, identb[:, :], NEG, None, ALU.mult).then_inc(g_neg, 1)
                nc.gpsimd.memset(grecip, 1.0).then_inc(g_free, 1)
                with pool.Fori(0, B) as b:
                    pool.wait_ge(g_stats, b + 1)
                    nc.gpsimd.tensor_tensor(veB[:, :], mvB[:, :, 1], eps[:, 0:QT], ALU.add).then_inc(g_neg, 1)
                    pool.wait_ge(g_neg, b + 2)
                    nc.gpsimd.tensor_tensor(rstdB[:, :], veB[:, :], neghalf[:, 0:QT], ALU.pow).then_inc(g_rstd, 1)
            with pool.Else():
                fast = Tally(pool, pool_fast)

                def norm_c(m, p, again):
                    if again:
                        pool.wait_ge(v_ready, m - 1)
                    nc.gpsimd.tensor_tensor(keysS[p], keysT[:, ds(m, 1), :].rearrange("p a k -> p (a k)"),
                                            zero_col.to_broadcast([128, TAIL]), ALU.add).then_inc(keysS_ready, 1)
                    pool.wait_ge(lnC_stats, m + 1)
                    fast.link(nc.gpsimd.tensor_tensor(veB[:, :], mvB[:, :, 1], eps[:, 0:QT], ALU.add))
                    nc.gpsimd.tensor_tensor(rstdB[:, :], veB[:, :], neghalf[:, 0:QT], ALU.pow).then_inc(rstdC_ready, 1)

                def split(m, p, again):
                    if again:
                        pool.wait_ge(parts_saved[p], half(m, p, 96, 0))
                        pool.wait_ge(S1_filled, 32 * m - 32)
                    for filled, full, res, part, split_done in ((k_ready, kf, kres, kpart[p], k_parts_ready),
                                                                (q_ready, qf, qres, qpart[p], q_parts_ready)):
                        pool.wait_ge(filled, m + 1)
                        fast.link(nc.gpsimd.tensor_tensor(part[:, 0, :], full, zero_col.to_broadcast(list(full.shape)), ALU.add))
                        fast.link(nc.gpsimd.tensor_tensor(res, full, part[:, 0, :], ALU.subtract))
                        fast.link(nc.gpsimd.tensor_tensor(part[:, 1, :], res, zero_col.to_broadcast(list(full.shape)), ALU.add))
                        nc.gpsimd.tensor_tensor(part[:, 2, :], res, part[:, 1, :], ALU.subtract).then_inc(split_done, 1)

                norm_c(0, 0, False)
                split(0, 0, False)
                norm_c(1, 1, False)
                split(1, 1, False)
                norm_c(2, 0, True)
                split(2, 0, True)
                norm_c(3, 1, True)
                split(3, 1, True)
                for i in fast.loop(1, B // 2 - 1, 14):
                    for p in range(2):
                        norm_c(2 * i + (2 + p), p, True)
                        split(2 * i + (2 + p), p, True)

            late = Tally(pool, pool_late)
            pool.wait_ge(attn_ready, NT)
            nc.gpsimd.iota(iota_slot, pattern=[[1, E * CAP]], base=0, channel_multiplier=0,
                           allow_small_or_imprecise_dtypes=True).then_inc(gconst_ready, 1)
            nc.gpsimd.iota(iota_e, pattern=[[0, NT], [1, E]], base=0, channel_multiplier=0,
                           allow_small_or_imprecise_dtypes=True).then_inc(gconst_ready, 1)
            nc.gpsimd.memset(allones, 1.0).then_inc(gconst_ready, 1)
            pool.wait_ge(gconst_ready, 3)
            nc.gpsimd.affine_select(out=upper, in_=allones, compare_op=ALU.is_gt, fill=0.0,
                                    base=0, pattern=[[1, 128]], channel_multiplier=-1).then_inc(gconst_ready, 1)

            def norm3(b, p):
                pool.wait_ge(x3_stats, b + 1)
                late.link(nc.gpsimd.tensor_tensor(ve3[p][:, :], mv3[p][:, :, 1], eps[:, 0:QT], ALU.add))
                nc.gpsimd.tensor_tensor(rstd3[p][:, :], ve3[p][:, :], neghalf[:, 0:QT], ALU.pow).then_inc(x3_rstd, 1)

            def save_tokens(b, p):
                pool.wait_ge(xn3_ready, QT * b + QT)
                nc.gpsimd.tensor_tensor(xn_all[:, ds(QT * b, QT), :], xn3[p], zero_col.unsqueeze(2).to_broadcast([128, QT, D]),
                                        ALU.add).then_inc(xn3_saved, 1)

            norm3(0, 0)
            norm3(1, 1)
            save_tokens(0, 0)
            for i in late.loop(1, B // 2, 2):
                for p in range(2):
                    norm3(2 * i + p, p)
                    save_tokens(2 * i + (p - 1), 1 - p)
            save_tokens(B - 1, 1)

            def take_tokens(b, p, again):
                if again:
                    pool.wait_ge(xT_filled, b - 1)
                nc.gpsimd.tensor_tensor(xs[p], xn_all[:, ds(QT * b, QT), :], zero_col.unsqueeze(2).to_broadcast([128, QT, D]),
                                        ALU.add).then_inc(xs_ready, 1)

            pool.wait_ge(xn3_saved, B)
            take_tokens(0, 0, False)
            take_tokens(1, 1, False)
            with pool.Fori(1, B // 2) as i:
                for p in range(2):
                    take_tokens(2 * i + p, p, True)

            def take_slots(g, p, again):
                if again:
                    pool.wait_ge(eoX_filled, g - 1)
                nc.gpsimd.tensor_tensor(eoS[p], eoT[:, :, ds(CAP * g, CAP)], zero_col.unsqueeze(2).to_broadcast([128, E, CAP]),
                                        ALU.add).then_inc(eoS_ready, 1)

            pool.wait_ge(eoT_ready, E)
            take_slots(0, 0, False)
            take_slots(1, 1, False)
            with pool.Fori(1, B // 2) as i:
                for p in range(2):
                    take_slots(2 * i + p, p, True)

        @block.scalar
        def _(act):
            act.dma_start(w0_sb[:, :], w0).then_inc(first_loaded, 16)
            act.dma_start(b0_col[:, :], b0.rearrange("(p a) -> p a", a=1)).then_inc(first_loaded, 16)
            for dst, src in ((gates_in[:, 0:2], g_xattn), (gates_in[:, 2:4], g_ffn)):
                act.dma_start(dst, src.rearrange("(a n) -> a n", a=1).to_broadcast([128, 2])).then_inc(first_loaded, 16)
            for j in range(4):
                act.dma_start(packed_sb[32 * j:32 * j + 32, :], packed.rearrange("(r i) -> r i", r=32)).then_inc(ternary_loaded, 16)
            for dst, src in ((fb_row, fbias), (ws_col, wscale), (bv_row, bv), (bo_row, bo)):
                act.dma_start(dst[:, :], src.rearrange("(a n) -> a n", a=1).to_broadcast([128, src.shape[0]])).then_inc(w_loaded, 16)
            for dst, src in ((wq_sb, wq), (wk_sb, wk), (wv_sb, wv), (wo_sb, wo), (router_sb, router)):
                act.dma_start(dst[:, :], src).then_inc(w_loaded, 16)
            for dst, src in ((bq_col, bq), (bk_col, bk)):
                act.dma_start(dst[:, :], src.rearrange("(p a) -> p a", a=1)).then_inc(w_loaded, 16)
            masks = mask.rearrange("b a (t p) k -> p (b a t) k", p=128)
            act.dma_start(maskB, masks[:, :, T0 - 1:K]).then_inc(maskB_loaded, 16)
            act.dma_start(maskA, masks[:, :, 0:T0 - 1]).then_inc(maskA_loaded, 16)
            act.wait_ge(first_loaded, 16 * 4)
            nc.scalar.activation(gates[:, :], gates_in[:, :], ACT.Tanh).then_inc(gates_ready, 1)

            def drain_ctx(b, p, first):
                for k, c in enumerate((0, 2)):
                    lo, hi = 128 * TCH[c][0], 128 * TCH[c][1]
                    act.wait_ge(TA_filled, fills(b, k + 1, first))
                    if k == 0 and (not isinstance(b, int) or b >= 2):
                        act.wait_ge(keys_saved, b - 1)
                    nc.scalar.activation(ctxT[p][:, lo:hi], TA[:, 0:hi - lo], ACT.Copy).then_inc(TA_drained, 1)

            def drain_probs(b, k0, first):
                for k, c in enumerate((0, 2)):
                    act.wait_ge(TA_filled, fills(b, k0 + k + 1, first))
                    n = TCH[c][1] - TCH[c][0]
                    nc.scalar.activation(probT[:, TCH[c][0]:TCH[c][1], :],
                                         TA.rearrange("p (t q) -> p t q", q=128)[:, 0:n, :], ACT.Copy).then_inc(TA_drained, 1)

            def softmax(b, q):
                act.wait_ge(max_done, 2 * b + (q + 1))
                if not isinstance(b, int) or b >= 1:
                    act.wait_ge(prob_used, 2 * b + (q - 1))
                u = 2 * b + q
                nc.scalar.activation(prob[q][:, :], S_ps, ACT.Exp, bias=nmax[:, ds(u, 1)],
                                     accum_out=rsum[:, ds(u, 1)]).then_inc(exp_done, 1)

            def body(b, p, first):
                drain_ctx(b, p, first)
                if not first:
                    drain_probs(b, 2, first)
                softmax(b, 0)
                drain_probs(b, 2 if first else 4, first)
                softmax(b, 1)

            body(0, 0, True)
            body(1, 1, False)
            with act.Fori(1, B // 2) as i:
                for p in range(2):
                    body(2 * i + p, p, False)
            drain_probs(B, 0, False)

            act.wait_ge(flag_ready, 1)
            general = act.value_load(flag[0:1, 0:1])
            with act.If(general > 0):
                with act.Fori(0, B) as b:
                    for c in range(4):
                        lo, hi = 128 * TCH[c][0], min(128 * TCH[c][1], K)
                        act.wait_ge(g_T_filled, 4 * b + (c + 1))
                        nc.scalar.activation(ctxT[0][:, lo:hi], (TA, TB)[c % 2][:, 0:hi - lo], ACT.Copy).then_inc(g_T_drained, 1)
                with act.Fori(0, B) as b:
                    for q in range(QT):
                        act.wait_ge(g_free, 2 * H * b + (H * q + 1))
                        act.dma_start(maskQ, mask[ds(b, 1), :, 128 * q:128 * q + 128, :].rearrange("a c q k -> (a c q) k")
                                      ).then_inc(g_mask_loaded, 16)
                        with act.Fori(0, H) as h:
                            u = 2 * H * b + h + H * q
                            act.wait_ge(g_max, u + 1)
                            nc.scalar.activation(prob[0], S_ps, ACT.Exp, bias=gmax, accum_out=gsum).then_inc(g_exp, 1)
                            for c in range(4):
                                n, rows = TCH[c][1] - TCH[c][0], 128 if c < 3 else KR
                                act.wait_ge(g_T_filled, 4 * u + (4 * B + c + 1))
                                nc.scalar.activation(probT[0:rows, TCH[c][0]:TCH[c][1], :],
                                                     (TA, TB)[c % 2].rearrange("p (t q) -> p t q", q=128)[0:rows, 0:n, :],
                                                     ACT.Copy).then_inc(g_T_drained, 1)
            with act.Else():
                def drain(b, g):
                    act.wait_ge(PV_filled, 4 * b + (g + 1))
                    if g == 0 and not (isinstance(b, int) and b == 0):
                        act.wait_ge(back_filled, 2 * b)
                    nc.scalar.activation(headsT[:, g, :], PV, ACT.Copy).then_inc(heads_ready, 1)

                def keys(m):
                    if not (isinstance(m, int) and m == 0):
                        act.wait_ge(k_parts_ready, m)
                    act.wait_ge(k_filled, m + 1)
                    nc.scalar.activation(kf, M_ps[:, 0:TAIL], ACT.Identity, bias=bk_col[:, :]).then_inc(k_ready, 1)

                def load_max(n, p):
                    act.wait_ge(nm_ready, n + 1)
                    for c in range(3):
                        act.dma_start(qaug[p][RN + c:RN + c + 1, :, :], nmpart[p][:, c, :]).then_inc(nm_loaded[p], 16)

                def heads(b, p, prev, maxi, proj):
                    for h in range(H):
                        if h % 4 == 0 and h < 8 and prev:
                            drain(b - 1, 2 + h // 4)
                        if h % 4 == 0 and h >= 8:
                            drain(b, h // 4 - 2)
                        act.wait_ge(ST_filled, 16 * b + (h + 1))
                        nc.scalar.activation(probs8[0:TP, h % 8, :], ST[h % 2], ACT.Exp).then_inc(P_ready, 1)
                        if h == 0 and proj:
                            keys(b + 2)
                        if h == MAX_STEP + 1 and maxi:
                            load_max(b + 1, 1 - p)

                keys(0)
                keys(1)
                load_max(0, 0)
                heads(0, 0, False, True, True)
                heads(1, 1, True, True, True)
                with act.Fori(1, B // 2 - 1) as i:
                    for p in range(2):
                        heads(2 * i + p, p, True, True, True)
                heads(B - 2, 0, True, True, False)
                heads(B - 1, 1, True, False, False)
                drain(B - 1, 2)
                drain(B - 1, 3)

            act.wait_ge(attn_ready, NT)

            def drain_tokens(b, p):
                act.wait_ge(xn3T_filled, b + 1)
                nc.scalar.activation(xn3T[p], bank[4 + p][:, 0:S], ACT.Copy).then_inc(xn3T_ready, 1)

            def attention(b, p):
                nc.scalar.activation(ao[p], attn[:, ds(QT * b, QT), :], ACT.Copy).then_inc(ao_ready, 1)

            def drain_aoT(b, p):
                act.wait_ge(aoT_filled, b + 1)
                nc.scalar.activation(aoT[p], bank[p][:, 0:S], ACT.Copy).then_inc(aoT_ready, 1)

            attention(0, 0)
            attention(1, 1)
            drain_aoT(0, 0)
            attention(2, 0)
            drain_aoT(1, 1)
            attention(3, 1)
            drain_aoT(2, 0)
            drain_tokens(0, 0)
            with act.Fori(2, B // 2) as i:
                for p in range(2):
                    attention(2 * i + p, p)
                    drain_aoT(2 * i + (p - 1), 1 - p)
                    drain_tokens(2 * i + (p - 3), 1 - p)
            drain_aoT(B - 1, 1)
            for b in range(B - 3, B):
                drain_tokens(b, b % 2)

            act.wait_ge(shifted_ready, 1)
            nc.scalar.activation(expd, shifted, ACT.Exp).then_inc(expd_ready, 1)

            with act.Fori(0, B // 2) as i:
                for p in range(2):
                    b = 2 * i + p
                    act.wait_ge(xT_filled, b + 1)
                    nc.scalar.activation(xT[:, :, ds(CAP * b, CAP)], bank[p].rearrange("p (e c) -> p e c", e=E), ACT.Copy).then_inc(xT_drained, 1)
                    act.wait_ge(cA_filled, b + 1)
                    nc.scalar.activation(combT[:, ds(b, 1), 0:512].rearrange("p a n -> p (a n)"), bank[2 + 2 * p], ACT.Copy).then_inc(cA_drained, 1)
                    act.wait_ge(cB_filled, b + 1)
                    nc.scalar.activation(combT[:, ds(b, 1), 512:1024].rearrange("p a n -> p (a n)"), bank[3 + 2 * p], ACT.Copy).then_inc(cB_drained, 1)

            def gelus(e, p, first):
                for c in range(HC):
                    rows = HROWS[c]
                    act.wait_ge(a_filled, HC * e + (c + 1))
                    if not (first and c < 2):
                        act.wait_ge(hid_ready, HC * e + (c - 1))
                    nc.scalar.activation(gl[c % 2][0:rows, :], bank[c % 2][0:rows, :], ACT.Gelu_apprx_tanh).then_inc(gelu_done, 1)
                    if c == 1 and not first:
                        drain_expert(e - 1, 1 - p)

            def drain_expert(e, p):
                act.wait_ge(eo_filled, e + 1)
                nc.scalar.activation(eoT[:, ds(e, 1), :].rearrange("p a n -> p (a n)"), bank[4 + p], ACT.Copy).then_inc(eoT_ready, 1)

            gelus(0, 0, True)
            gelus(1, 1, False)
            with act.Fori(1, E // 2) as i:
                for p in range(2):
                    gelus(2 * i + p, p, False)
            drain_expert(E - 1, 1)

            with act.Fori(0, B // 2) as i:
                for p in range(2):
                    g = 2 * i + p
                    act.wait_ge(outT_filled, g + 1)
                    nc.scalar.activation(outT[p], bank[2 + p][:, 0:S], ACT.Copy).then_inc(outT_ready, 1)

        @block.vector
        def _(dve):
            order = Tally(dve, dve_order)

            def ln(lo, hi):
                for t in range(lo, hi):
                    m = order.mark(nc.vector.bn_stats(stats[:, t, :], x_sb[:, t, :]))
                dve.wait_ge(dve_order, m)
                for t in range(lo, hi):
                    last = nc.vector.bn_aggr(meanvar[:, t, :], stats[:, t, :])
                last.then_inc(ln_stats, 1)

            dve.wait_ge(x_loaded, 16)
            ln(0, 2)
            for p in range(2):
                nc.vector.memset(kaug_words[p], ONES).then_inc(consts2_ready, 1)

            def normalise(b, p):
                for q in range(QT):
                    u = 2 * b + q
                    src = x_sb[:, u, :] if isinstance(b, int) else x_sb[:, ds(u, 1), :].rearrange("p a d -> p (a d)")
                    nc.vector.tensor_scalar(xn[p][:, q, :], src, meanvar[:, ds(u, 1), 0], rstd[:, ds(u, 1)],
                                            ALU.subtract, ALU.mult).then_inc(xn_ready, 1)

            def prep(b, p, first):
                dve.wait_ge(xnT_filled, b + 1)
                nc.vector.tensor_copy(xnT[p][:, :], M_ps[:, 0:S]).then_inc(xnT_ready, 1)
                if first:
                    dve.wait_ge(ternT_filled, 1)
                    nc.vector.tensor_copy(ternT[:, :], TB.bitcast(bf16)[:, 0:128]).then_inc(ternT_ready, 1)
                for k, c in enumerate((1, 3)):
                    lo, hi = 128 * TCH[c][0], min(128 * TCH[c][1], K)
                    dve.wait_ge(TB_filled, fills(b, k + 1, first))
                    if k == 0 and (not isinstance(b, int) or b >= 2):
                        dve.wait_ge(keys_saved, b - 1)
                    nc.vector.tensor_copy(ctxT[p][:, lo:hi], TB[:, 0:hi - lo]).then_inc(TB_drained, 1)
                    if k == 0:
                        dve.wait_ge(proj_filled, b + 1)
                        nc.vector.tensor_scalar(projT[p][:, :], M_ps[:, S:2 * S], b0_col[:, :], None, ALU.add).then_inc(projT_ready, 1)

            def ternary():
                dve.wait_ge(ternary_loaded, 64)
                for j in range(4):
                    m = order.mark(nc.vector.tensor_scalar(tern_i[32 * j:32 * j + 32, :], packed_sb[32 * j:32 * j + 32, :],
                                                           2 * j, 3, ALU.logical_shift_right, ALU.bitwise_and))
                dve.wait_ge(dve_order, m)
                nc.vector.tensor_scalar(tern[:, :], tern_i[:, :], -1.0, None, ALU.add).then_inc(tern_ready, 1)

            def maximum(b, q):
                u = 2 * b + q
                dve.wait_ge(S_filled, u + 1)
                nc.vector.tensor_reduce(nmax[:, ds(u, 1)], S_ps, AX.X, ALU.max, negate=True).then_inc(max_done, 1)

            def drain_probs(b, k0, first):
                for k, c in enumerate((1, 3)):
                    n = TCH[c][1] - TCH[c][0]
                    rows = 128 if c == 1 else KR
                    dve.wait_ge(TB_filled, fills(b, k0 + k + 1, first))
                    nc.vector.tensor_copy(probT[0:rows, TCH[c][0]:TCH[c][1], :],
                                          TB.rearrange("p (t q) -> p t q", q=128)[0:rows, 0:n, :]).then_inc(TB_drained, 1)

            def attend(b, q, p):
                u = 2 * b + q
                dve.wait_ge(exp_done, u + 1)
                order.link(nc.vector.reciprocal(rgate[:, 0:1], rsum[:, ds(u, 1)]))
                order.link(nc.vector.tensor_scalar(rgate[:, 1:2], rgate[:, 0:1], gates[:, 0:1], None, ALU.mult))
                dve.wait_ge(O_filled, u + 1)
                xt = x_sb[:, ds(u, 1), :].rearrange("p a d -> p (a d)")
                nc.vector.scalar_tensor_tensor(x1[p][:, q, :], O_ps[:, 0:D], rgate[:, 1:2], xt, ALU.mult, ALU.add).then_inc(O_drained, 1)

            def quantise(b, p):
                xt = [x1[p][:, q, :] for q in range(QT)]
                dve.wait_ge(O_drained, 2 * b + 2)
                for q in range(QT):
                    m = order.mark(nc.vector.bn_stats(statsB[:, q, :], xt[q]))
                dve.wait_ge(dve_order, m)
                nc.vector.memset(dve_slot[:, :], 0.0)
                for q in range(QT):
                    last = nc.vector.bn_aggr(mvB[:, q, :], statsB[:, q, :])
                last.then_inc(statsB_ready, 1)
                dve.wait_ge(statsB_ready, b + 1)
                dve.wait_ge(rstdB_ready, b + 1)
                for q in range(QT):
                    m = order.mark(nc.vector.tensor_scalar(xnB[:, q, :], xt[q], mvB[:, q, 0:1], rstdB[:, q:q + 1],
                                                           ALU.subtract, ALU.mult))
                dve.wait_ge(dve_order, m)
                order.link(nc.vector.tensor_reduce(amax[:, :], xnB[:, :, :], AX.X, ALU.max, apply_absolute_value=True))
                order.link(nc.vector.tensor_scalar(amax[:, :], amax[:, :], 1e-5, None, ALU.max))
                order.link(nc.vector.reciprocal(qscale[:, :], amax[:, :]))
                order.link(nc.vector.tensor_scalar(qscale[:, :], qscale[:, :], 127.0, None, ALU.mult))
                order.mark(nc.vector.tensor_scalar(dscale[:, :], amax[:, :], ws_col[:, :], 1.0 / 127.0, ALU.mult, ALU.mult))
                for q in range(QT):
                    m = order.mark(nc.vector.tensor_scalar(xnB[:, q, :], xnB[:, q, :], qscale[:, q:q + 1], MAGIC, ALU.mult, ALU.add))
                dve.wait_ge(dve_order, m)
                order.link(nc.vector.tensor_scalar(xnB[:, :, :], xnB[:, :, :], MAGIC - 128.0, MAGIC + 127.0, ALU.max, ALU.min))
                nc.vector.tensor_scalar(xq[:, :, :], xnB[:, :, :], -MAGIC, None, ALU.add).then_inc(xq_ready, 1)

            def drain_xq(b):
                dve.wait_ge(xqT_filled, b + 1)
                nc.vector.tensor_copy(xqT[:, :], Mb[:, 0:S]).then_inc(xqT_ready, 1)

            def linear(b, p):
                dve.wait_ge(y_filled, b + 1)
                for q in range(QT):
                    m = order.mark(nc.vector.scalar_tensor_tensor(yB[:, q, :], M_ps[:, S + 128 * q:S + 128 * q + 128],
                                                                  dscale[:, q:q + 1], fb_row[:, :], ALU.mult, ALU.add))
                dve.wait_ge(dve_order, m)
                xt = x_sb[:, ds(2 * b, 2), :]
                nc.vector.scalar_tensor_tensor(xt, yB[:, :, :], gates[:, 2:3], x1[p][:, :, :], ALU.mult, ALU.add).then_inc(x2_ready, 1)

            words = maskA.rearrange("p t k -> p (t k)").bitcast(i32)

            def fold(n, least):
                while n > least:
                    n //= 2
                    order.link(nc.vector.tensor_tensor(words[:, 0:n], words[:, 0:n], words[:, n:2 * n], ALU.bitwise_and))
                return n

            def check(step):
                n = NT * (T0 - 1) // 4
                if step == 0:
                    dve.wait_ge(maskA_loaded, 16)
                    fold(n, n // 2)
                if step == 1:
                    fold(n // 2, n // 4)
                if step == 2:
                    n = fold(n // 4, 300)
                    order.link(nc.vector.tensor_reduce(maskpair[:, :], words[:, 0:n].bitcast(mybir.dt.uint16), AX.X, ALU.min))
                    dve.wait_ge(small_ready, 3)
                    order.link(nc.vector.tensor_scalar(bad[:, 0:1], maskpair[:, :], 257.0, None, ALU.is_lt))

            def body(b, p, first, checking=False):
                normalise(b, p)
                if first:
                    ternary()
                prep(b, p, first)
                if first:
                    dve.wait_ge(xrest_loaded, 16)
                    ln(2, NT)
                if checking:
                    check(0)
                maximum(b, 0)
                if checking:
                    check(1)
                if not first:
                    drain_probs(b, 2, first)
                    attend(b - 1, 1, 1 - p)
                    quantise(b - 1, 1 - p)
                if checking:
                    check(2)
                maximum(b, 1)
                if not first:
                    drain_xq(b - 1)
                drain_probs(b, 2 if first else 4, first)
                attend(b, 0, p)
                if not first:
                    linear(b - 1, 1 - p)

            dve.wait_ge(gates_ready, 1)
            dve.wait_ge(rstd_ready, 1)
            body(0, 0, True)
            dve.wait_ge(rstd_ready, 2)
            dve.wait_ge(w_loaded, 16 * 11)
            body(1, 1, False, True)
            dve.wait_ge(maskB_loaded, 16)
            order.link(nc.vector.tensor_reduce(maskmin[:, :], maskB[:, :, 0:1].rearrange("p t k -> p (t k)"), AX.X, ALU.min))
            order.link(nc.vector.tensor_scalar(bad[:, 1:2], maskmin[:, :], 1.0, None, ALU.is_lt))
            dve.wait_ge(cnt_filled, 1)
            nc.vector.tensor_copy(cnt[:, :], M_ps[0:B, 0:TAIL]).then_inc(cnt_read, 1)
            dve.wait_ge(cnt_read, 1)
            nc.vector.tensor_scalar(maskrow[:, :], cnt[:, :], NEG / S, None, ALU.mult).then_inc(maskrow_ready, 1)
            order.link(nc.vector.scalar_tensor_tensor(cntv[:, :], cnt[:, :], float(S), cnt[:, :], ALU.subtract, ALU.mult))
            order.link(nc.vector.tensor_reduce(cmin[:, 0:1], cntv[:, :], AX.X, ALU.min))
            order.link(nc.vector.tensor_reduce(cmin[:, 1:2], cnt[:, :], AX.X, ALU.min))
            nc.vector.tensor_tensor(bad[0:B, 2:3], cmin[:, 1:2], cmin[:, 0:1], ALU.subtract).then_inc(bad_ready, 1)
            for i in order.loop(1, B // 2, 36):
                for p in range(2):
                    body(2 * i + p, p, False)
            drain_probs(B, 0, False)
            attend(B - 1, 1, 1)
            quantise(B - 1, 1)
            dve.wait_ge(bad_filled, 1)
            order.link(nc.vector.tensor_reduce(badsum[:, :], O_ps[0:1, 0:3], AX.X, ALU.add))
            nc.vector.tensor_scalar(flag[:, :], badsum[:, :], 0.0, None, ALU.is_gt).then_inc(flag_ready, 1)
            drain_xq(B - 1)
            linear(B - 1, 1)

            dve.wait_ge(flag_ready, 1)
            general = dve.value_load(flag[0:1, 0:1])
            with dve.If(general > 0):
                slow = Tally(dve, dve_gen)
                for b in slow.loop(0, B, 2):
                    xt = [x_sb[:, ds(2 * b + q, 1), :].rearrange("p a d -> p (a d)") for q in range(QT)]
                    for q in range(QT):
                        m = slow.mark(nc.vector.bn_stats(statsB[:, q, :], xt[q]))
                    dve.wait_ge(dve_gen, m)
                    nc.vector.memset(dve_slot[:, :], 0.0)
                    for q in range(QT):
                        last = nc.vector.bn_aggr(mvB[:, q, :], statsB[:, q, :])
                    last.then_inc(g_stats, 1)
                    dve.wait_ge(g_stats, b + 1)
                    dve.wait_ge(g_rstd, b + 1)
                    for q in range(QT):
                        nc.vector.tensor_scalar(xnG[:, q, :], xt[q], mvB[:, q, 0:1], rstdB[:, q:q + 1],
                                                ALU.subtract, ALU.mult).then_inc(g_xn, 1)
                    dve.wait_ge(g_xT_filled, b + 1)
                    nc.vector.tensor_copy(xnGT, M_ps[:, 0:S]).then_inc(g_xT_ready, 1)
                    dve.wait_ge(g_q_filled, b + 1)
                    nc.vector.tensor_scalar(qG, M_ps[:, 0:S], bq_col[:, :], DH ** -0.5, ALU.add, ALU.mult).then_inc(g_q_ready, 1)
                    dve.wait_ge(g_k_filled, b + 1)
                    nc.vector.tensor_scalar(prob[0], S_ps, bk_col[:, :], None, ALU.add).then_inc(g_k_ready, 1)
                    dve.wait_ge(g_v_filled, b + 1)
                    for t in range(KT):
                        rows = 128 if t < KT - 1 else KR
                        last = nc.vector.tensor_tensor(ctxN[0][0:rows, t, :], PS[0:rows, 128 * t:128 * t + 128], bv_row[0:rows, :], ALU.add)
                    last.then_inc(g_v_ready, 1)
                with dve.Fori(0, B) as b:
                    for q in range(QT):
                        dve.wait_ge(g_mask_loaded, 32 * b + (16 * q + 16))
                        nc.vector.tensor_copy(maskQF, maskQ).then_inc(g_mask_ready, 1)
                        with dve.Fori(0, H) as h:
                            u = 2 * H * b + h + H * q
                            dve.wait_ge(g_S_filled, u + 1)
                            nc.vector.tensor_reduce(gmax, S_ps, AX.X, ALU.max, negate=True).then_inc(g_max, 1)
                            dve.wait_ge(g_exp, u + 1)
                            nc.vector.reciprocal(grecip, gsum).then_inc(g_S_free, 1)
                            dve.wait_ge(g_S_free, u + 1)
                            dve.wait_ge(g_O_filled, u + 1)
                            nc.vector.tensor_scalar(attn[:, ds(2 * b + q, 1), ds(DH * h, DH)].rearrange("p a d -> p (a d)"), O_ps[:, 0:DH], grecip,
                                                    None, ALU.mult).then_inc(g_free, 1)
                dve.wait_ge(g_free, NT * H + 1)
                nc.vector.memset(dve_slot[:, :], 0.0).then_inc(attn_ready, NT)
            with dve.Else():
                fast = Tally(dve, dve_fast)

                def moments(m):
                    nc.vector.memset(dve_slot[:, :], 0.0)
                    for q in range(QT):
                        n = fast.mark(nc.vector.bn_stats(statsB[:, q, :], x_sb[:, ds(2 * m + q, 1), :].rearrange("p a d -> p (a d)")))
                    dve.wait_ge(dve_fast, n)
                    nc.vector.memset(dve_slot[:, :], 0.0)
                    for q in range(QT):
                        last = nc.vector.bn_aggr(mvB[:, q, :], statsB[:, q, :])
                    last.then_inc(lnC_stats, 1)

                def normalise(m):
                    dve.wait_ge(lnC_stats, m + 1)
                    dve.wait_ge(rstdC_ready, m + 1)
                    for q in range(QT):
                        nc.vector.tensor_scalar(xnC[:, q, :], x_sb[:, ds(2 * m + q, 1), :].rearrange("p a d -> p (a d)"),
                                                mvB[:, q, 0:1], rstdB[:, q:q + 1], ALU.subtract, ALU.mult).then_inc(xnC_ready, 1)

                def drain_xnT(m):
                    dve.wait_ge(xnCT_filled, m + 1)
                    nc.vector.tensor_copy(xnCT, M_ps[:, 0:S]).then_inc(xnCT_ready, 1)

                def queries(m):
                    dve.wait_ge(q_filled, m + 1)
                    if not (isinstance(m, int) and m == 0):
                        dve.wait_ge(q_parts_ready, m)
                    nc.vector.tensor_scalar(qf, M_ps[:, 0:S], bq_col[:, :], DH ** -0.5, ALU.add, ALU.mult).then_inc(q_ready, 1)

                def values(n, p):
                    dve.wait_ge(v_filled, n + 1)
                    for t in range(4):
                        last = nc.vector.tensor_tensor(vaug[p][:, t, :, 0:DH], M_ps[0:TP, 128 * t:128 * t + 128].rearrange("p (h d) -> p h d", d=DH),
                                                       bv_row[0:TP, :].rearrange("p (h d) -> p h d", d=DH), ALU.add)
                    last.then_inc(v_ready, 1)

                def head_maximum(n, p, u):
                    dve.wait_ge(S1_filled, 32 * n + (u + 1))
                    at = H * (u % QT) + u // QT
                    nc.vector.tensor_reduce(nm[p][:, at:at + 1], S1[u % 2], AX.X, ALU.max, negate=True).then_inc(S1_max, 1)

                def split_max(n, p):
                    dve.wait_ge(nmT_filled, n + 1)
                    src = M_ps[0:H, 0:S]
                    fast.link(nc.vector.tensor_copy(nmpart[p][:, 0, :], src))
                    fast.link(nc.vector.tensor_tensor(nmres, src, nmpart[p][:, 0, :], ALU.subtract))
                    fast.link(nc.vector.tensor_copy(nmpart[p][:, 1, :], nmres))
                    nc.vector.tensor_tensor(nmpart[p][:, 2, :], nmres, nmpart[p][:, 1, :], ALU.subtract).then_inc(nm_ready, 1)

                def divide(b, q):
                    dve.wait_ge(back_filled, 2 * b + (q + 1))
                    o = M_ps.rearrange("p (h e) -> p h e", e=32)
                    fast.link(nc.vector.reciprocal(rden, o[:, :, DH]))
                    dst = attn[:, ds(2 * b + q, 1), :].rearrange("p a (h d) -> p (a h) d", d=DH)
                    nc.vector.tensor_tensor(dst, o[:, :, 0:DH], rden.unsqueeze(2).to_broadcast([128, H, DH]),
                                            ALU.mult).then_inc(attn_ready, 1)

                def body(b, p, prev, maxi, proj):
                    for h in range(H):
                        for k, u in UNITS[h]:
                            if (maxi, proj)[k]:
                                head_maximum(b + 1 + k, (1 - p, p)[k], u)
                        if h == 0 and proj:
                            moments(b + 2)
                        if h == 1 and proj:
                            normalise(b + 2)
                        if h == 1 and proj:
                            drain_xnT(b + 2)
                        if h == 2 and proj:
                            queries(b + 2)
                        if h in (6, 7) and prev:
                            divide(b - 1, h - 6)
                        if h == 9 and maxi:
                            values(b + 1, 1 - p)
                        if h == MAX_STEP and maxi:
                            split_max(b + 1, 1 - p)

                for m in range(2):
                    moments(m)
                    normalise(m)
                    drain_xnT(m)
                    queries(m)
                for u in range(QT * H):
                    head_maximum(0, 0, u)
                values(0, 0)
                split_max(0, 0)
                for u in range(EARLY):
                    head_maximum(1, 1, u)
                body(0, 0, False, True, True)
                body(1, 1, True, True, True)
                for i in fast.loop(1, B // 2 - 1, 14):
                    for p in range(2):
                        body(2 * i + p, p, True, True, True)
                body(B - 2, 0, True, True, False)
                body(B - 1, 1, True, False, False)
                divide(B - 1, 0)
                divide(B - 1, 1)

            late = Tally(dve, dve_late)
            dve.wait_ge(attn_ready, NT)

            def drain_logits(b, p):
                dve.wait_ge(lg_filled, b + 1)
                nc.vector.tensor_copy(logits[:, ds(QT * b, QT), :], bank[6 + p][:, 0:QT * E].rearrange("p (t e) -> p t e", e=E)).then_inc(lg_ready, 1)

            def out_projection(b, p):
                xt = [x_sb[:, ds(2 * b + q, 1), :].rearrange("p a d -> p (a d)") for q in range(QT)]
                dve.wait_ge(wo_filled, b + 1)
                for q in range(QT):
                    m = late.mark(nc.vector.tensor_tensor(x3t[:, q, :], bank[2 + p][:, 128 * q:128 * q + 128], bo_row[:, :], ALU.add))
                dve.wait_ge(dve_late, m)
                x2t = x_sb[:, ds(2 * b, 2), :]
                nc.vector.scalar_tensor_tensor(x2t, x3t, gates[:, 1:2], x2t, ALU.mult, ALU.add).then_inc(x3_read, 1)
                dve.wait_ge(x3_read, b + 1)
                nc.vector.memset(dve_slot[:, :], 0.0)
                for q in range(QT):
                    m = late.mark(nc.vector.bn_stats(statsB[:, q, :], xt[q]))
                dve.wait_ge(dve_late, m)
                nc.vector.memset(dve_slot[:, :], 0.0)
                for q in range(QT):
                    last = nc.vector.bn_aggr(mv3[p][:, q, :], statsB[:, q, :])
                last.then_inc(x3_stats, 1)

            def normalise3(b, p):
                dve.wait_ge(x3_stats, b + 1)
                dve.wait_ge(x3_rstd, b + 1)
                if not isinstance(b, int) or b >= 2:
                    dve.wait_ge(xn3_saved, b - 1)
                for q in range(QT):
                    nc.vector.tensor_scalar(xn3[p][:, q, :], x_sb[:, ds(2 * b + q, 1), :].rearrange("p a d -> p (a d)"),
                                            mv3[p][:, q, 0:1], rstd3[p][:, q:q + 1], ALU.subtract, ALU.mult).then_inc(xn3_ready, 1)

            out_projection(0, 0)
            normalise3(0, 0)
            out_projection(1, 1)
            for i in late.loop(1, B // 2, 8):
                for p in range(2):
                    normalise3(2 * i + (p - 1), 1 - p)
                    out_projection(2 * i + p, p)
                    drain_logits(2 * i + (p - 2), p)
            normalise3(B - 1, 1)
            drain_logits(B - 2, 0)
            drain_logits(B - 1, 1)
            dve.wait_ge(lg_ready, B)
            dve.wait_ge(gconst_ready, 4)

            def wide(v):
                return v.unsqueeze(2).to_broadcast([128, NT, E])

            def link(ins):
                late.link(ins)

            def first_of(values, best, least, onehot):
                link(nc.vector.tensor_tensor(equal, values, wide(best), ALU.is_equal))
                link(nc.vector.scalar_tensor_tensor(cand, equal, -float(E), iota_e, ALU.mult, ALU.add))
                link(nc.vector.tensor_reduce(least, cand, AX.X, ALU.min))
                link(nc.vector.tensor_tensor(onehot, cand, wide(least), ALU.is_equal))

            link(nc.vector.tensor_reduce(gmx, logits, AX.X, ALU.max))
            nc.vector.tensor_tensor(shifted, logits, wide(gmx), ALU.subtract).then_inc(shifted_ready, 1)
            dve.wait_ge(expd_ready, 1)
            link(nc.vector.tensor_reduce(gmx, expd, AX.X, ALU.add))
            link(nc.vector.reciprocal(gmx, gmx))
            link(nc.vector.tensor_tensor(raw, expd, wide(gmx), ALU.mult))
            link(nc.vector.tensor_reduce(gate1, raw, AX.X, ALU.max))
            first_of(raw, gate1, least1, m1)
            link(nc.vector.tensor_tensor(work, raw, m1, ALU.mult))
            link(nc.vector.tensor_tensor(rest, raw, work, ALU.subtract))
            link(nc.vector.tensor_reduce(gate2, rest, AX.X, ALU.max))
            first_of(rest, gate2, least2, m2)
            half_ = NT * E
            link(nc.vector.tensor_copy(m12[:, 0:half_], m1.rearrange("p t e -> p (t e)")))
            nc.vector.tensor_copy(m12[:, half_:2 * half_], m2.rearrange("p t e -> p (t e)")).then_inc(m12_ready, 1)
            dve.wait_ge(cum_filled, 1)
            link(nc.vector.tensor_copy(pos1, bank[0][:, 0:half_].rearrange("p (t e) -> p t e", e=E)))
            link(nc.vector.tensor_scalar(count1, bank[1][:, 0:B * E].rearrange("p (b e) -> p b e", e=E), float(CAP), None, ALU.min))
            behind = bank[0][:, half_:2 * half_].rearrange("p (b t e) -> p b t e", t=QT, e=E)
            pos2v = pos2.rearrange("p (b t) e -> p b t e", t=QT)
            for t in range(QT):
                link(nc.vector.tensor_tensor(pos2v[:, :, t, :], behind[:, :, t, :], count1, ALU.add))
            for onehot, pos, least, keep, place, slot in ((m1, pos1, least1, keep1, place1, slot1),
                                                          (m2, pos2, least2, keep2, place2, slot2)):
                link(nc.vector.scalar_tensor_tensor(kept, pos, float(CAP), onehot, ALU.is_lt, ALU.mult))
                link(nc.vector.tensor_reduce(keep, kept, AX.X, ALU.add))
                link(nc.vector.tensor_tensor(work, pos, onehot, ALU.mult))
                link(nc.vector.tensor_reduce(place, work, AX.X, ALU.add))
                link(nc.vector.scalar_tensor_tensor(place, least, float(CAP), place, ALU.mult, ALU.add))
                link(nc.vector.scalar_tensor_tensor(slot, place, float(E * CAP + 1), keep, ALU.add, ALU.mult))
                link(nc.vector.tensor_scalar(slot, slot, -1.0, None, ALU.add))

            def weights(b, p, again):
                if again:
                    dve.wait_ge(cB_filled, b - 1)
                for q in range(QT):
                    u = 2 * b + q
                    for dst, slot, gate in ((comb[p], slot1, gate1), (comb2[p], slot2, gate2)):
                        nc.vector.tensor_scalar(dst[:, q, :], iota_slot, slot[:, ds(u, 1)], gate[:, ds(u, 1)],
                                                ALU.is_equal, ALU.mult).then_inc(weights_ready, 1)

            def dispatch(b, p):
                dve.wait_ge(weights_ready, 4 * b + 4)
                link(nc.vector.tensor_tensor(comb[p], comb[p], comb2[p], ALU.add))
                nc.vector.tensor_scalar(disp[p], comb[p], 0.0, None, ALU.not_equal).then_inc(comb_ready, 1)

            weights(0, 0, False)
            dispatch(0, 0)
            weights(1, 1, False)
            dispatch(1, 1)
            for i in late.loop(1, B // 2, 2):
                for p in range(2):
                    weights(2 * i + p, p, True)
                    dispatch(2 * i + p, p)

            def hidden(e, first):
                for c in range(HC):
                    rows = HROWS[c]
                    dve.wait_ge(b_filled, HC * e + (c + 1))
                    dve.wait_ge(gelu_done, HC * e + (c + 1))
                    if c == 1 and not first:
                        dve.wait_ge(eo_filled, e)
                    if c >= 2 or (c == 0 and not first):
                        dve.wait_ge(hid_used, (HC - 1) * e + max(c - 1, 0))
                    nc.vector.tensor_tensor(hid[c % 2][0:rows, :], bank[2 + c % 2][0:rows, :], gl[c % 2][0:rows, :], ALU.mult).then_inc(hid_ready, 1)

            hidden(0, True)
            with dve.Fori(1, E) as e:
                hidden(e, False)

            def residual(g, p):
                dve.wait_ge(y_back_filled, g + 1)
                xt = x_sb[:, ds(2 * g, 2), :]
                nc.vector.scalar_tensor_tensor(xt, bank[4 + p][:, 0:S].rearrange("p (t d) -> p t d", d=D), gates[:, 3:4], xt,
                                               ALU.mult, ALU.add).then_inc(x4_ready, 1)

            def slots(g, p):
                dve.wait_ge(eoX_filled, g + 1)
                nc.vector.tensor_copy(eo[p], bank[p].rearrange("p (t d) -> p t d", d=D)).then_inc(eo_ready, 1)

            slots(0, 0)
            slots(1, 1)
            with dve.Fori(1, B // 2) as i:
                for p in range(2):
                    slots(2 * i + p, p)
                    residual(2 * i + (p - 2), p)
            residual(B - 2, 0)
            residual(B - 1, 1)

        @block.tensor
        def _(pe):
            def prep(b, p, first):
                pe.wait_ge(xn_ready, 2 * b + 2)
                if not isinstance(b, int) or b >= 2:
                    pe.wait_ge(x2_ready, b - 1)
                for q in range(QT):
                    last = nc.tensor.transpose(M_ps[:, 128 * q:128 * q + 128], xn[p][:, q, :], ident[:, :])
                last.then_inc(xnT_filled, 1)
                if first:
                    pe.wait_ge(tern_ready, 1)
                    nc.tensor.transpose(TB.bitcast(bf16)[:, 0:128], tern[:, :], identb[:, :]).then_inc(ternT_filled, 1)
                pe.wait_ge(ctx_loaded[p], 32 * (b // 2 + 1) if isinstance(b, int) else 16 * b + (32 - 16 * p))
                for c in range(4):
                    bk_, filled, drained = ((TA, TA_filled, TA_drained), (TB, TB_filled, TB_drained))[c % 2]
                    if not first or c >= 2:
                        pe.wait_ge(drained, fills(b, c // 2, first))
                    if first and c == 1:
                        pe.wait_ge(ternT_ready, 1)
                    for n, t in enumerate(range(*TCH[c])):
                        rows = 128 if t < KT - 1 else KR
                        last = nc.tensor.transpose(bk_[:, 128 * n:128 * n + rows], ctxN[p][0:rows, t, :], ident[0:rows, 0:rows])
                    last.then_inc(filled, 1)
                    if c == 1:
                        pe.wait_ge(xnT_ready, b + 1)
                        nc.tensor.matmul(M_ps[:, S:2 * S], w0_sb[:, :], xnT[p][:, :], start=True, stop=True).then_inc(proj_filled, 1)

            def scores(b, q, p, first):
                u = 2 * b + q
                if q == 0:
                    pe.wait_ge(projT_ready, b + 1)
                    pe.wait_ge(TA_drained, fills(b, 2, first))
                    pe.wait_ge(TB_drained, fills(b, 2, first))
                if not (first and q == 0):
                    pe.wait_ge(exp_done, u)
                for lo in range(0, K, 512):
                    hi = min(lo + 512, K)
                    last = nc.tensor.matmul(S_ps[:, lo:hi], projT[p][:, 128 * q:128 * q + 128], ctxT[p][:, lo:hi],
                                            start=True, stop=True)
                last.then_inc(S_filled, 1)

            def attend(b, q, p, bb, k0, first):
                u = 2 * b + q
                banks = ((TA, TA_filled, TA_drained), (TB, TB_filled, TB_drained))

                def transposes(c):
                    bk_, filled, drained = banks[c % 2]
                    pe.wait_ge(drained, fills(bb, k0 + c // 2, first))
                    for n, t in enumerate(range(*TCH[c])):
                        rows = 128 if t < KT - 1 else KR
                        last = nc.tensor.transpose(bk_[0:rows, 128 * n:128 * n + 128], prob[q][:, 128 * t:128 * t + rows], ident[:, :])
                    last.then_inc(filled, 1)

                def product(c):
                    pe.wait_ge(banks[c % 2][2], fills(bb, k0 + c // 2 + 1, first))
                    for t in range(*TCH[c]):
                        rows = 128 if t < KT - 1 else KR
                        last = nc.tensor.matmul(O_ps[:, 0:D], probT[0:rows, t, :], ctxN[p][0:rows, t, :], start=t == 0, stop=t == KT - 1)
                    return last

                pe.wait_ge(exp_done, u + 1)
                transposes(0)
                transposes(1)
                if not (isinstance(b, int) and b == 0 and q == 0):
                    pe.wait_ge(O_drained, u)
                product(0)
                transposes(2)
                product(1)
                transposes(3)
                product(2).then_inc(prob_used, 1)
                product(3).then_inc(O_filled, 1)

            def quantised_T(b):
                pe.wait_ge(xq_ready, b + 1)
                pe.wait_ge(projT_ready, b + 1)
                for q in range(QT):
                    last = nc.tensor.transpose(Mb[:, 128 * q:128 * q + 128], xq[:, q, :], identb[:, :])
                last.then_inc(xqT_filled, 1)

            def linear(b):
                pe.wait_ge(xqT_ready, b + 1)
                for q in range(QT):
                    last = nc.tensor.matmul(M_ps[:, S + 128 * q:S + 128 * q + 128], xqT[:, 128 * q:128 * q + 128], ternT[:, :],
                                            start=True, stop=True)
                last.then_inc(y_filled, 1)

            def body(b, p, first):
                prep(b, p, first)
                scores(b, 0, p, first)
                if not first:
                    attend(b - 1, 1, 1 - p, b, 2, first)
                scores(b, 1, p, first)
                if not first:
                    quantised_T(b - 1)
                attend(b, 0, p, b, 2 if first else 4, first)
                if not first:
                    linear(b - 1)

            pe.wait_ge(ident_ready, 2)
            pe.wait_ge(first_loaded, 16 * 4)
            body(0, 0, True)
            pe.wait_ge(w_loaded, 16 * 11)
            body(1, 1, False)
            pe.wait_ge(x2_ready, 1)
            pe.wait_ge(small_ready, 5)
            for t in range(NT):
                last = nc.tensor.matmul(M_ps[0:B, 0:TAIL], sel15[:, B - 1 - t // QT:2 * B - 1 - t // QT], maskF[:, t, :],
                                        start=t == 0, stop=t == NT - 1)
            last.then_inc(cnt_filled, 1)
            pe.wait_ge(cnt_read, 1)
            with pe.Fori(1, B // 2) as i:
                for p in range(2):
                    body(2 * i + p, p, False)
            attend(B - 1, 1, 1, B, 0, False)
            pe.wait_ge(bad_ready, 1)
            pe.wait_ge(consts2_ready, 6)
            pe.wait_ge(O_drained, QT * B)
            nc.tensor.matmul(O_ps[0:1, 0:3], ones_col[:, :], bad[:, :], start=True, stop=True).then_inc(bad_filled, 1)
            quantised_T(B - 1)
            linear(B - 1)

            pe.wait_ge(x2_ready, B)
            pe.wait_ge(flag_ready, 1)
            general = pe.value_load(flag[0:1, 0:1])
            with pe.If(general > 0):
                pe.wait_ge(g_neg, 1)
                with pe.Fori(0, B) as b:
                    pe.wait_ge(g_loaded, 32 * b + 32)
                    for c in range(4):
                        if c >= 2:
                            pe.wait_ge(g_T_drained, 4 * b + (c - 1))
                        for n, t in enumerate(range(*TCH[c])):
                            rows = 128 if t < KT - 1 else KR
                            last = nc.tensor.transpose((TA, TB)[c % 2][:, 128 * n:128 * n + rows], ctxN[0][0:rows, t, :], ident[0:rows, 0:rows])
                        last.then_inc(g_T_filled, 1)
                    pe.wait_ge(g_xn, 2 * b + 2)
                    for q in range(QT):
                        last = nc.tensor.transpose(M_ps[:, 128 * q:128 * q + 128], xnG[:, q, :], ident[:, :])
                    last.then_inc(g_xT_filled, 1)
                    pe.wait_ge(g_xT_ready, b + 1)
                    nc.tensor.matmul(M_ps[:, 0:S], wq_sb[:, :], xnGT, start=True, stop=True).then_inc(g_q_filled, 1)
                    pe.wait_ge(g_T_drained, 4 * b + 4)
                    for lo in range(0, K, 512):
                        hi = min(lo + 512, K)
                        last = nc.tensor.matmul(S_ps[:, lo:hi], wk_sb[:, :], ctxT[0][:, lo:hi], start=True, stop=True)
                    last.then_inc(g_k_filled, 1)
                    pe.wait_ge(g_k_ready, b + 1)
                    for t in range(KT):
                        rows = 128 if t < KT - 1 else KR
                        last = nc.tensor.matmul(PS[0:rows, 128 * t:128 * t + 128], ctxT[0][:, 128 * t:128 * t + rows], wv_sb[:, :],
                                                start=True, stop=True)
                    last.then_inc(g_v_filled, 1)
                    pe.wait_ge(g_v_ready, b + 1)
                    pe.wait_ge(g_q_ready, b + 1)
                with pe.Fori(0, B) as b:
                    for q in range(QT):
                        with pe.Fori(0, H) as h:
                            u = 2 * H * b + h + H * q
                            pe.wait_ge(g_mask_ready, 2 * b + (q + 1))
                            pe.wait_ge(g_head_loaded, 64 * u + 64)
                            for lo in range(0, K, 512):
                                hi = min(lo + 512, K)
                                nc.tensor.matmul(S_ps[:, lo:hi], qhead, khead[:, lo:hi], start=True, stop=False)
                                last = nc.tensor.matmul(S_ps[:, lo:hi], negident, maskQF[:, lo:hi], start=False, stop=True)
                            last.then_inc(g_S_filled, 1)
                            pe.wait_ge(g_exp, u + 1)
                            for c in range(4):
                                if c >= 2:
                                    pe.wait_ge(g_T_drained, 4 * u + (4 * B + c - 1))
                                for n, t in enumerate(range(*TCH[c])):
                                    rows = 128 if t < KT - 1 else KR
                                    last = nc.tensor.transpose((TA, TB)[c % 2][0:rows, 128 * n:128 * n + 128],
                                                               prob[0][:, 128 * t:128 * t + rows], ident[:, :])
                                last.then_inc(g_T_filled, 1)
                            pe.wait_ge(g_T_drained, 4 * u + (4 * B + 4))
                            for t in range(KT):
                                rows = 128 if t < KT - 1 else KR
                                last = nc.tensor.matmul(O_ps[:, 0:DH], probT[0:rows, t, :], vhead[0:rows, t, :], start=t == 0, stop=t == KT - 1)
                            last.then_inc(g_O_filled, 1)
                            pe.wait_ge(g_free, u + 2)
            with pe.Else():
                def tokens_c(m):
                    pe.wait_ge(k_ready, m + 1)
                    pe.wait_ge(xnC_ready, 2 * m + 2)
                    for q in range(QT):
                        last = nc.tensor.transpose(M_ps[:, 128 * q:128 * q + 128], xnC[:, q, :], ident[:, :])
                    last.then_inc(xnCT_filled, 1)

                def queries(m):
                    pe.wait_ge(xnCT_ready, m + 1)
                    nc.tensor.matmul(M_ps[:, 0:S], wq_sb[:, :], xnCT, start=True, stop=True).then_inc(q_filled, 1)

                def keys(m, p, m_free):
                    pe.wait_ge(*m_free)
                    pe.wait_ge(keysS_ready, m + 1)
                    nc.tensor.matmul(M_ps[:, 0:TAIL], wk_sb[:, :], keysS[p], start=True, stop=True).then_inc(k_filled, 1)

                def values(n, p, m_free):
                    pe.wait_ge(*m_free)
                    for t in range(4):
                        last = nc.tensor.matmul(M_ps[0:TP, 128 * t:128 * t + 128], keysS[p][:, TP * t:TP * t + TP], wv_sb[:, :],
                                                start=True, stop=True)
                    last.then_inc(v_filled, 1)

                def scores(n, p, u):
                    if u % H == 0:
                        pe.wait_ge(aug_loaded[u // H][p], half(n, p, 48, 48))
                    if not (isinstance(n, int) and n == 0 and u < 2):
                        pe.wait_ge(S1_max, 32 * n + (u - 1))
                    h, q = u // QT, u % QT
                    nc.tensor.matmul(S1[u % 2], qaug[p][0:RN, h, 128 * q:128 * q + 128], kaug[p][0:RN, h, :],
                                     start=True, stop=True).then_inc(S1_filled, 1)

                def maxT(n, p):
                    pe.wait_ge(S1_max, 32 * n + 32)
                    pe.wait_ge(v_ready, n + 1)
                    for q in range(QT):
                        last = nc.tensor.transpose(M_ps[0:H, 128 * q:128 * q + 128], nm[p][:, H * q:H * q + H], ident[:, :])
                    last.then_inc(nmT_filled, 1)

                def scoresT(b, p, h):
                    if h == 0:
                        pe.wait_ge(nm_loaded[p], half(b, p, 48, 48))
                    if not (isinstance(b, int) and b == 0 and h < 2):
                        pe.wait_ge(P_ready, 16 * b + (h - 1))
                    for t in range(4):
                        last = nc.tensor.matmul(ST[h % 2][:, S * t:S * t + S], kaug[p][:, h, TP * t:TP * t + TP], qaug[p][:, h, :],
                                                start=True, stop=True)
                    last.then_inc(ST_filled, 1)

                def weigh(b, p, g, t):
                    if t == 0:
                        pe.wait_ge(P_ready, 16 * b + (4 * g + 4))
                        if not (isinstance(b, int) and b == 0 and g == 0):
                            pe.wait_ge(heads_ready, 4 * b + g)
                    for j in range(4):
                        h = 4 * g + j
                        last = nc.tensor.matmul(PV[32 * j:32 * j + 32, :], vaug[p][:, t, h, :], probs8[0:TP, h % 8, S * t:S * t + S],
                                                start=t == 0, stop=t == 3)
                    if t == 3:
                        last.then_inc(PV_filled, 1)

                def back(b, q, m_free):
                    pe.wait_ge(*m_free)
                    if q == 0:
                        pe.wait_ge(heads_ready, 4 * b + 4)
                    for g in range(4):
                        last = nc.tensor.transpose(M_ps[:, 128 * g:128 * g + 128], headsT[:, g, 128 * q:128 * q + 128], ident[:, :])
                    last.then_inc(back_filled, 1)

                def weigh_step(b, p, h, prev):
                    if h >= 5:
                        weigh(b, p, (h - 5) // 4, (h - 5) % 4)
                    elif prev:
                        weigh(b - 1, 1 - p, (h + 11) // 4, (h + 11) % 4)

                def body(b, p, score, prev, maxi, proj):
                    for h in range(H):
                        units = [(b + 1 + k, (1 - p, p)[k], u) for k, u in UNITS[h] if (maxi, proj)[k]]
                        if units:
                            scores(*units[0])
                        if score:
                            scoresT(b, p, h)
                        if units:
                            scores(*units[1])
                        if score:
                            weigh_step(b, p, h, prev)
                        if len(units) > 2:
                            scores(*units[2])
                        if h == 0 and proj:
                            keys(b + 2, p, (nm_ready, b + 1))
                        if h == 1 and proj:
                            tokens_c(b + 2)
                        if h == 2 and proj:
                            queries(b + 2)
                        if h == 6 and prev:
                            back(b - 1, 0, (q_ready, b + 3) if proj else (nm_ready, B - 1) if maxi else (nm_ready, B))
                        if h == 7 and prev:
                            back(b - 1, 1, (attn_ready, 2 * b - 1))
                        if h == 9 and maxi:
                            values(b + 1, 1 - p, (attn_ready, 2 * b) if prev else (q_ready, b + 3))
                        if h == MAX_STEP and maxi:
                            maxT(b + 1, 1 - p)

                keys(0, 0, (flag_ready, 1))
                tokens_c(0)
                queries(0)
                keys(1, 1, (q_ready, 1))
                tokens_c(1)
                queries(1)
                for u in range(QT * H):
                    scores(0, 0, u)
                values(0, 0, (q_ready, 2))
                maxT(0, 0)
                for u in range(EARLY):
                    scores(1, 1, u)
                body(0, 0, True, False, True, True)
                body(1, 1, True, True, True, True)
                with pe.Fori(1, B // 2 - 1) as i:
                    for p in range(2):
                        body(2 * i + p, p, True, True, True, True)
                body(B - 2, 0, True, True, True, False)
                body(B - 1, 1, True, True, False, False)
                for h in range(5):
                    weigh_step(B, 0, h, True)
                back(B - 1, 0, (attn_ready, 2 * B - 2))
                back(B - 1, 1, (attn_ready, 2 * B - 1))
            pe.wait_ge(attn_ready, NT)

            def tokens_T(b, p):
                pe.wait_ge(xn3_ready, QT * b + QT)
                for q in range(QT):
                    last = nc.tensor.transpose(bank[4 + p][:, 128 * q:128 * q + 128], xn3[p][:, q, :], ident[:, :])
                last.then_inc(xn3T_filled, 1)

            def router_logits(b, p):
                pe.wait_ge(xn3T_ready, b + 1)
                if not isinstance(b, int) or b >= 2:
                    pe.wait_ge(lg_ready, b - 1)
                for q in range(QT):
                    last = nc.tensor.matmul(bank[6 + p][:, E * q:E * q + E], xn3T[p][:, 128 * q:128 * q + 128], router_sb[:, :],
                                            start=True, stop=True)
                last.then_inc(lg_filled, 1)

            def attention_T(b, p):
                pe.wait_ge(ao_ready, b + 1)
                for q in range(QT):
                    last = nc.tensor.transpose(bank[p][:, 128 * q:128 * q + 128], ao[p][:, q, :], ident[:, :])
                last.then_inc(aoT_filled, 1)

            def out_projection(b, p):
                pe.wait_ge(aoT_ready, b + 1)
                for q in range(QT):
                    last = nc.tensor.matmul(bank[2 + p][:, 128 * q:128 * q + 128], aoT[p][:, 128 * q:128 * q + 128], wo_sb[:, :],
                                            start=True, stop=True)
                last.then_inc(wo_filled, 1)

            def body(b, p):
                attention_T(b, p)
                if not isinstance(b, int) or b >= 3:
                    tokens_T(b - 3, 1 - p)
                if not isinstance(b, int) or b >= 1:
                    out_projection(b - 1, 1 - p)
                if not isinstance(b, int) or b >= 3:
                    router_logits(b - 3, 1 - p)

            for b in range(4):
                body(b, b % 2)
            with pe.Fori(2, B // 2) as i:
                for p in range(2):
                    body(2 * i + p, p)
            tokens_T(B - 3, 1)
            out_projection(B - 1, 1)
            router_logits(B - 3, 1)
            for b in range(B - 2, B):
                tokens_T(b, b % 2)
                router_logits(b, b % 2)

            pe.wait_ge(m12_ready, 1)
            pe.wait_ge(gconst_ready, 4)
            tiles = m12.rearrange("p (k t e) -> p k t e", t=QT, e=E)
            sums = bank[0][:, 0:2 * NT * E].rearrange("p (k t e) -> p k t e", t=QT, e=E)
            nc.tensor.matmul(bank[0][:, 0:2 * NT * E], upper, m12, start=True, stop=False)
            nc.tensor.matmul(sums[:, :, 1, :], allones, tiles[:, :, 0, :], start=False, stop=True)
            for t in range(QT):
                last = nc.tensor.matmul(bank[1][:, 0:B * E].rearrange("p (b e) -> p b e", e=E), allones, tiles[:, 0:B, t, :],
                                        start=t == 0, stop=t == QT - 1)
            last.then_inc(cum_filled, 1)

            def dispatch(b, p, again):
                pe.wait_ge(comb_ready, b + 1)
                pe.wait_ge(xs_ready, b + 1)
                if again:
                    pe.wait_ge(xT_drained, b - 1)
                for q in range(QT):
                    last = nc.tensor.matmul(bank[p], xs[p][:, q, :], disp[p][:, q, :], start=q == 0, stop=q == QT - 1)
                last.then_inc(xT_filled, 1)
                for half_bank, filled, drained in ((0, cA_filled, cA_drained), (1, cB_filled, cB_drained)):
                    if again:
                        pe.wait_ge(drained, b - 1)
                    for c in range(2):
                        for q in range(QT):
                            ch = 2 * half_bank + c
                            last = nc.tensor.transpose(bank[2 + 2 * p + half_bank][:, S * c + 128 * q:S * c + 128 * q + 128],
                                                       comb[p][:, q, 128 * ch:128 * ch + 128], ident[:, :])
                    last.then_inc(filled, 1)

            dispatch(0, 0, False)
            dispatch(1, 1, False)
            with pe.Fori(1, B // 2) as i:
                for p in range(2):
                    dispatch(2 * i + p, p, True)

            def down(e, c, p):
                rows = HROWS[c]
                pe.wait_ge(hid_ready, HC * e + (c + 1))
                if c == 0 and (not isinstance(e, int) or e >= 2):
                    pe.wait_ge(eoT_ready, e - 1)
                ins = nc.tensor.matmul(bank[4 + p], woe[p][0:rows, c, :], hid[c % 2][0:rows, :], start=c == 0, stop=c == HC - 1)
                ins.then_inc(eo_filled if c == HC - 1 else hid_used, 1)

            def expert(e, p, first):
                pe.wait_ge(wts_loaded[p], half(e, p, 64, 64))
                rhs = xT[:, ds(e, 1), :].rearrange("p a n -> p (a n)")
                for c in range(HC):
                    rows = HROWS[c]
                    if not (first and c < 2):
                        pe.wait_ge(gelu_done, HC * e + (c - 1))
                    nc.tensor.matmul(bank[c % 2][0:rows, :], w0e[p][:, HLO[c]:HLO[c] + rows], rhs, start=True, stop=True).then_inc(a_filled, 1)
                    if not (first and c < 2):
                        pe.wait_ge(hid_ready, HC * e + (c - 1))
                    nc.tensor.matmul(bank[2 + c % 2][0:rows, :], w1e[p][:, HLO[c]:HLO[c] + rows], rhs, start=True, stop=True).then_inc(b_filled, 1)
                    if c > 0:
                        down(e, c - 1, p)
                    elif not first:
                        down(e - 1, HC - 1, 1 - p)

            pe.wait_ge(xT_drained, B)
            pe.wait_ge(cA_drained, B)
            pe.wait_ge(cB_drained, B)
            expert(0, 0, True)
            expert(1, 1, False)
            with pe.Fori(1, E // 2) as i:
                for p in range(2):
                    expert(2 * i + p, p, False)
            down(E - 1, HC - 1, 1)

            def back_T(g, p):
                pe.wait_ge(outT_ready, g + 1)
                if not isinstance(g, int) or g >= 2:
                    pe.wait_ge(x4_ready, g - 1)
                for q in range(QT):
                    last = nc.tensor.transpose(bank[4 + p][:, 128 * q:128 * q + 128], outT[p][:, 128 * q:128 * q + 128], ident[:, :])
                last.then_inc(y_back_filled, 1)

            def outputs_T(g, p):
                pe.wait_ge(eoS_ready, g + 1)
                if not isinstance(g, int) or g >= 2:
                    pe.wait_ge(eo_ready, g - 1)
                for ch in range(E * CAP // 128):
                    last = nc.tensor.transpose(bank[p][:, 128 * ch:128 * ch + 128],
                                               eoS[p][:, 2 * ch:2 * ch + 2, :].rearrange("p e c -> p (e c)"), ident[:, :])
                last.then_inc(eoX_filled, 1)

            def combine(g, p):
                pe.wait_ge(eo_ready, g + 1)
                for ch in range(E * CAP // 128):
                    last = nc.tensor.matmul(bank[2 + p][:, 0:S], eo[p][:, ch, :],
                                            combT[:, ds(g, 1), S * ch:S * ch + S].rearrange("p a n -> p (a n)"),
                                            start=ch == 0, stop=ch == E * CAP // 128 - 1)
                last.then_inc(outT_filled, 1)

            def body(g, p):
                outputs_T(g, p)
                if not isinstance(g, int) or g >= 1:
                    combine(g - 1, 1 - p)
                if not isinstance(g, int) or g >= 2:
                    back_T(g - 2, p)

            pe.wait_ge(eoT_ready, E)
            for g in range(4):
                body(g, g % 2)
            with pe.Fori(2, B // 2) as i:
                for p in range(2):
                    body(2 * i + p, p)
            combine(B - 1, 1)
            back_T(B - 2, 0)
            back_T(B - 1, 1)


_INS = ["x", "ctx_1024", "mask_Bx1xSxS2_bk1", "g_xattn", "g_ffn", "L0_xattn_W", "L0_xattn_b", "L0_ffn_packed_weight",
        "L0_ffn_weight_scale", "L0_ffn_bias", "L1_xattn_w_q", "L1_xattn_b_q", "L1_xattn_w_k", "L1_xattn_b_k",
        "L1_xattn_w_v", "L1_xattn_b_v", "L1_xattn_w_o", "L1_xattn_b_o", "L1_ffn_router_w", "L1_ffn_w0_kernel",
        "L1_ffn_w1_kernel", "L1_ffn_wo_kernel"]


def kernel(**inputs):
    import numpy as _np
    import concourse.bacc as _bacc
    from concourse import mybir as _mybir
    from concourse.bass_utils import run_bass_kernel_spmd as _run

    nc = _bacc.Bacc("TRN2", target_bir_lowering=False, num_devices=1)
    arrays, args = {}, []
    for name in _INS:
        a = _np.ascontiguousarray(inputs[name])
        arrays[f"in_{name}_dram"] = a
        args.append(nc.dram_tensor(f"in_{name}_dram", a.shape, _mybir.dt.from_np(a.dtype), kind="ExternalInput").ap())
    shape = _np.shape(inputs["x"])
    args.append(nc.dram_tensor("out_0_dram", shape, _mybir.dt.float32, kind="ExternalOutput").ap())
    build(nc, *args)
    r = _run(nc, [arrays], core_ids=[0])
    return r.results[0]["out_0_dram"]
```
